# Optimizing a Trainium2 kernel written in Bass

```python
import numpy as np
import jax
import jax.numpy as jnp

def _softmax(x, axis=-1):
    return jax.nn.softmax(x, axis=axis)

def _gelu(x):
    return jax.nn.gelu(x, approximate=True)

def _silu(x):
    return jax.nn.silu(x)

def _sigmoid(x):
    return jax.nn.sigmoid(x)

def _layernorm(x, axis=-1, eps=1e-05):
    m = jnp.mean(x, axis=axis, keepdims=True)
    v = jnp.var(x, axis=axis, keepdims=True)
    return (x - m) / jnp.sqrt(v + eps)

def _scatter_add(tgt, idx, src, axis=0):
    return tgt.at[idx].add(src)

def _segment_sum(src, seg, n):
    return jax.ops.segment_sum(src, seg, n)
kernel_name = 'mk_xattn_ffn_d4_seqx_r8_6cdb69'

def setup_inputs(seed: int=0):
    np.random.seed(seed)
    _w = jnp.asarray

    def _rec_inputs():
        import jax
        import jax.numpy as jnp
        _rk = jax.random.key(seed)
        x = 2.818e-05 + 1 * jax.random.normal(jax.random.fold_in(_rk, 1), (64, 64, 128), jnp.float32)
        _lenS = 64 - jax.random.randint(jax.random.fold_in(_rk, 7), (64,), 0, max(1, 64 // 4) + 1, jnp.int32)
        _lenS2 = 64 - jax.random.randint(jax.random.fold_in(_rk, 8), (64,), 0, max(1, 64 // 4) + 1, jnp.int32)
        _ctx_2048P = jax.random.normal(jax.random.fold_in(_rk, 11), (64, 16, 256), jnp.float32)
        _ctx_2048c = jax.random.dirichlet(jax.random.fold_in(_rk, 511), 0.3 * jnp.ones((16,), jnp.float32), (64, 64))
        _ctx_2048t = jnp.einsum('bsk,bkd->bsd', _ctx_2048c, _ctx_2048P)
        _ctx_2048t = _ctx_2048t * jax.lax.rsqrt(jnp.mean(jnp.square(_ctx_2048t)) + 1e-12) * 0.953939
        ctx_2048 = -0.000125008 + 0.999885 * (_ctx_2048t + 0.3 * jax.random.normal(jax.random.fold_in(_rk, 611), (64, 64, 256), jnp.float32))
        _validS = jnp.arange(64)[None, :] < _lenS[:, None]
        _validS2 = jnp.arange(64)[None, :] < _lenS2[:, None]
        _causal = jnp.tril(jnp.ones((64, 64), dtype=bool))
        mask_BxS2_fk1 = jnp.where(jnp.broadcast_to(_validS2[:, :], (64, 64)), 1.0, 0.0).astype(jnp.float32)
        mask_BxS2_if0 = jnp.where(jnp.ones((64, 64), dtype=bool), 4, 0).astype(jnp.int32)
        return (x, ctx_2048, mask_BxS2_fk1, mask_BxS2_if0)
    x, ctx_2048, mask_BxS2_fk1, mask_BxS2_if0 = _rec_inputs()

    def _L0_xattn_setup():
        import jax, jax.numpy as jnp
        import numpy as np
        B, S, T = (32, 64, 64)
        SRC_SIZE, TGT_SIZE, OUT_SIZE, NUM_HEAD = (256, 128, 128, 8)
        HEAD_DIM = OUT_SIZE // NUM_HEAD
        key = jax.random.key(seed)
        ks = jax.random.split(key, 12)
        src = jax.random.normal(ks[0], (B, S, SRC_SIZE), dtype=jnp.float32)
        tgt = jax.random.normal(ks[1], (B, T, TGT_SIZE), dtype=jnp.float32)
        src_mask = (jax.random.uniform(ks[2], (B, S)) > 0.3).astype(jnp.float32)
        src_mask = src_mask.at[:, 0].set(1.0)
        tgt_mask = (jax.random.uniform(ks[3], (B, T)) > 0.3).astype(jnp.float32)
        tgt_mask = tgt_mask.at[:, 0].set(1.0)

        def lin(k, out_f, in_f):
            return jax.random.normal(k, (out_f, in_f), dtype=jnp.float32) / np.sqrt(in_f)
        W_src = lin(ks[4], 2 * OUT_SIZE, SRC_SIZE)
        b_src = jnp.zeros((2 * OUT_SIZE,), jnp.float32)
        W_tgt = lin(ks[5], OUT_SIZE, TGT_SIZE)
        b_tgt = jnp.zeros((OUT_SIZE,), jnp.float32)
        W_out = lin(ks[6], OUT_SIZE, OUT_SIZE + TGT_SIZE)
        b_out = jnp.zeros((OUT_SIZE,), jnp.float32)
        return {'src': src, 'tgt': tgt, 'src_mask': src_mask, 'tgt_mask': tgt_mask, 'W_src': W_src, 'b_src': b_src, 'W_tgt': W_tgt, 'b_tgt': b_tgt, 'W_out': W_out, 'b_out': b_out}
    _L0_xattn_all = _L0_xattn_setup()
    _L0_xattn_in = {k: v for k, v in _L0_xattn_all.items() if k in ('W_src', 'b_src', 'W_tgt', 'b_tgt', 'W_out', 'b_out')}
    del _L0_xattn_all

    def _L0_ffn_setup():
        import jax, jax.numpy as jnp
        import numpy as np
        B, T, C = (4, 256, 128)
        H, E = (512, 8)
        key = jax.random.key(seed)
        ks = jax.random.split(key, 6)
        scale = 0.02
        x = jax.random.normal(ks[0], (B, T, C), dtype=jnp.float32)
        w_router = jax.random.normal(ks[1], (C, E), dtype=jnp.float32) * scale
        b_router = jnp.zeros((E,), dtype=jnp.float32)
        w1 = jax.random.normal(ks[2], (E, C, H), dtype=jnp.float32) * scale
        b1 = jnp.zeros((E, H), dtype=jnp.float32)
        w2 = jax.random.normal(ks[3], (E, H, C), dtype=jnp.float32) * scale
        b2 = jnp.zeros((E, C), dtype=jnp.float32)
        return {'x': x, 'w_router': w_router, 'b_router': b_router, 'w1': w1, 'b1': b1, 'w2': w2, 'b2': b2}
    _L0_ffn_all = _L0_ffn_setup()
    _L0_ffn_in = {k: v for k, v in _L0_ffn_all.items() if k in ('w_router', 'b_router', 'w1', 'b1', 'w2', 'b2')}
    del _L0_ffn_all

    def _L1_xattn_setup():
        import jax, jax.numpy as jnp
        import numpy as np
        B, N, DIM = (8, 512, 128)
        M, CTX = (32, 256)
        HEADS, DH = (16, 64)
        INNER = HEADS * DH
        EPS = 1e-06

        def _split_heads(t):
            b, n, _ = t.shape
            return t.reshape(b, n, HEADS, DH).transpose(0, 2, 1, 3)
        key = jax.random.key(seed)
        ks = jax.random.split(key, 6)
        x = jax.random.normal(ks[0], (B, N, DIM), dtype=jnp.float32)
        context = jax.random.normal(ks[1], (B, M, CTX), dtype=jnp.float32)
        Wq = jax.random.normal(ks[2], (DIM, INNER), dtype=jnp.float32) / np.sqrt(DIM)
        Wkv = jax.random.normal(ks[3], (CTX, 2 * INNER), dtype=jnp.float32) / np.sqrt(CTX)
        null_kv = jax.random.normal(ks[4], (2, DH), dtype=jnp.float32) / np.sqrt(2.0)
        Wout = jax.random.normal(ks[5], (INNER, DIM), dtype=jnp.float32) / np.sqrt(INNER)
        ln_scale = jnp.ones((DIM,), dtype=jnp.float32)
        ln_bias = jnp.zeros((DIM,), dtype=jnp.float32)
        return {'x': x, 'context': context, 'Wq': Wq, 'Wkv': Wkv, 'null_kv': null_kv, 'Wout': Wout, 'ln_scale': ln_scale, 'ln_bias': ln_bias}
    _L1_xattn_all = _L1_xattn_setup()
    _L1_xattn_in = {k: v for k, v in _L1_xattn_all.items() if k in ('Wq', 'Wkv', 'null_kv', 'Wout', 'ln_scale', 'ln_bias')}
    del _L1_xattn_all

    def _L1_ffn_setup():
        import jax, jax.numpy as jnp
        import numpy as np
        B, T, C = (4, 256, 128)
        E = 8
        K = 2
        H = 176
        HS = 176 * 2
        key = jax.random.key(seed)
        k = jax.random.split(key, 8)
        s = 0.02
        return {'x': jax.random.normal(k[0], (B, T, C), jnp.float32), 'Wg': jax.random.normal(k[1], (C, E), jnp.float32) * s, 'W1': jax.random.normal(k[2], (E, C, H), jnp.float32) * s, 'W2': jax.random.normal(k[3], (E, C, H), jnp.float32) * s, 'W3': jax.random.normal(k[4], (E, H, C), jnp.float32) * s, 'Ws1': jax.random.normal(k[5], (C, HS), jnp.float32) * s, 'Ws2': jax.random.normal(k[6], (C, HS), jnp.float32) * s, 'Ws3': jax.random.normal(k[7], (HS, C), jnp.float32) * s}
    _L1_ffn_all = _L1_ffn_setup()
    _L1_ffn_in = {k: v for k, v in _L1_ffn_all.items() if k in ('Wg', 'W1', 'W2', 'W3', 'Ws1', 'Ws2', 'Ws3')}
    del _L1_ffn_all

    def _L2_xattn_setup():
        import jax, jax.numpy as jnp
        import numpy as np
        B, L, P = (4, 512, 128)
        D_MODEL = 128
        D_GLOBAL = 256
        HEADDIM = 32
        EPSILON = 0.001
        RMS_EPS = 1e-05

        def rmsnorm(x, g, eps=RMS_EPS):
            var = jnp.mean(jnp.square(x), axis=-1, keepdims=True)
            return x * jax.lax.rsqrt(var + eps) * g

        def _hnet_depool(h, h_patch_full, patch_lens):
            h_patch = h_patch_full[..., :D_MODEL]
            bsz, plen = (h_patch.shape[0], h_patch.shape[1])
            seqlen = h.shape[1]
            logp = jnp.full((bsz, plen), -EPSILON, dtype=jnp.float32)
            bidx = jnp.cumsum(patch_lens, axis=1) - 1
            boundary_mask = jnp.zeros((bsz, seqlen), dtype=jnp.int32)
            boundary_mask = boundary_mask.at[jnp.arange(bsz)[:, None], bidx].set(1)
            dt = (-jnp.log(-jnp.expm1(logp))).astype(h_patch.dtype)
            x = h_patch / dt[..., None]
            n_heads = D_MODEL // HEADDIM
            A = -jnp.ones((n_heads,), dtype=jnp.float32)
            bcoef = jnp.exp(logp).astype(h_patch.dtype)
            x4 = x.reshape(bsz, plen, n_heads, HEADDIM)
            a = jnp.exp(dt[:, :, None] * A[None, None, :])
            u = (dt * bcoef)[:, :, None, None] * x4
            a_b = jnp.broadcast_to(a[..., None], u.shape)

            def comb(lft, rgt):
                aL, uL = lft
                aR, uR = rgt
                return (aL * aR, uL * aR + uR)
            _, s = jax.lax.associative_scan(comb, (a_b, u), axis=1)
            depool = s.reshape(bsz, plen, D_MODEL)
            plug = jnp.clip(jnp.cumsum(boundary_mask, axis=1) - 1, 0, plen - 1)
            depool_out = depool[jnp.arange(bsz)[:, None], plug]
            return depool_out + h
        key = jax.random.key(seed)
        k1, k2, k3, k4 = jax.random.split(key, 4)
        embeds = jax.random.normal(k1, (B, L, D_MODEL), dtype=jnp.float32)
        patch_embeds = jax.random.normal(k2, (B, P, D_GLOBAL), dtype=jnp.float32)
        patch_lens = jnp.full((B, P), L // P, dtype=jnp.int64)
        W_in = jax.random.normal(k3, (D_MODEL, D_MODEL), dtype=jnp.float32) * 0.02
        b_in = jnp.zeros((D_MODEL,), dtype=jnp.float32)
        g_res = jnp.ones((D_MODEL,), dtype=jnp.float32)
        g_init = jnp.ones((D_GLOBAL,), dtype=jnp.float32)
        return {'embeds': embeds, 'patch_embeds': patch_embeds, 'patch_lens': patch_lens, 'W_in': W_in, 'b_in': b_in, 'g_res': g_res, 'g_init': g_init}
    _L2_xattn_all = _L2_xattn_setup()
    _L2_xattn_in = {k: v for k, v in _L2_xattn_all.items() if k in ('W_in', 'b_in', 'g_res', 'g_init')}
    del _L2_xattn_all

    def _L2_ffn_setup():
        import jax, jax.numpy as jnp
        import numpy as np
        D_MODEL = 128
        D_INNER = 256
        N_EXPERTS = 8
        TOP_K = 2
        INIT_STD = 0.02
        key = jax.random.key(seed)
        ks = jax.random.split(key, 6)
        B, S = (2, 256)
        x = jax.random.normal(ks[0], (B, S, D_MODEL), dtype=jnp.float32)
        router_w = jax.random.normal(ks[1], (N_EXPERTS, D_MODEL), dtype=jnp.float32) * (INIT_STD * 0.1)
        router_b = jnp.zeros((N_EXPERTS,), dtype=jnp.float32)
        gate_w = jax.random.normal(ks[2], (N_EXPERTS, D_MODEL, D_INNER), dtype=jnp.float32) * INIT_STD
        up_w = jax.random.normal(ks[3], (N_EXPERTS, D_MODEL, D_INNER), dtype=jnp.float32) * INIT_STD
        down_w = jax.random.normal(ks[4], (N_EXPERTS, D_INNER, D_MODEL), dtype=jnp.float32) * INIT_STD
        return {'x': x, 'router_w': router_w, 'router_b': router_b, 'gate_w': gate_w, 'up_w': up_w, 'down_w': down_w}
    _L2_ffn_all = _L2_ffn_setup()
    _L2_ffn_in = {k: v for k, v in _L2_ffn_all.items() if k in ('router_w', 'router_b', 'gate_w', 'up_w', 'down_w')}
    del _L2_ffn_all

    def _L3_xattn_setup():
        import jax, jax.numpy as jnp
        import numpy as np
        NUM_HEADS = 16
        key = jax.random.key(seed)
        ks = jax.random.split(key, 5)
        dim = 128
        B, N, N_c = (4, 128, 32)
        x = jax.random.normal(ks[0], (B, N, dim), dtype=jnp.float32)
        context = jax.random.normal(ks[1], (B, N_c, 2 * dim), dtype=jnp.float32)
        w_qkv = jax.random.normal(ks[2], (3 * dim, dim), dtype=jnp.float32) * 0.02
        w_proj = jax.random.normal(ks[3], (dim, dim), dtype=jnp.float32) * 0.02
        b_proj = jax.random.normal(ks[4], (dim,), dtype=jnp.float32) * 0.02
        return {'x': x, 'context': context, 'w_qkv': w_qkv, 'w_proj': w_proj, 'b_proj': b_proj}
    _L3_xattn_all = _L3_xattn_setup()
    _L3_xattn_in = {k: v for k, v in _L3_xattn_all.items() if k in ('w_qkv', 'w_proj', 'b_proj')}
    del _L3_xattn_all

    def _L3_ffn_setup():
        import jax, jax.numpy as jnp
        import numpy as np
        B, S, D, H, E = (4, 256, 128, 256, 8)
        key = jax.random.key(seed)
        ks = jax.random.split(key, 8)
        scale = 0.02
        return {'x': jax.random.normal(ks[0], (B, S, D), dtype=jnp.float32), 'Wr': jax.random.normal(ks[1], (D, E), dtype=jnp.float32) * scale, 'br': jnp.zeros((E,), dtype=jnp.float32), 'W1': jax.random.normal(ks[2], (E, D, H), dtype=jnp.float32) * scale, 'b1': jnp.zeros((E, H), dtype=jnp.float32), 'W2': jax.random.normal(ks[3], (E, H, D), dtype=jnp.float32) * scale, 'b2': jnp.zeros((E, D), dtype=jnp.float32)}
    _L3_ffn_all = _L3_ffn_setup()
    _L3_ffn_in = {k: v for k, v in _L3_ffn_all.items() if k in ('Wr', 'br', 'W1', 'b1', 'W2', 'b2')}
    del _L3_ffn_all
    return {'x': x, 'ctx_2048': ctx_2048, 'mask_BxS2_fk1': mask_BxS2_fk1, 'mask_BxS2_if0': mask_BxS2_if0, 'L0_xattn_W_src': _L0_xattn_in['W_src'], 'L0_xattn_b_src': _L0_xattn_in['b_src'], 'L0_xattn_W_tgt': _L0_xattn_in['W_tgt'], 'L0_xattn_b_tgt': _L0_xattn_in['b_tgt'], 'L0_xattn_W_out': _L0_xattn_in['W_out'], 'L0_xattn_b_out': _L0_xattn_in['b_out'], 'L0_ffn_w_router': _L0_ffn_in['w_router'], 'L0_ffn_b_router': _L0_ffn_in['b_router'], 'L0_ffn_w1': _L0_ffn_in['w1'], 'L0_ffn_b1': _L0_ffn_in['b1'], 'L0_ffn_w2': _L0_ffn_in['w2'], 'L0_ffn_b2': _L0_ffn_in['b2'], 'L1_xattn_Wq': _L1_xattn_in['Wq'], 'L1_xattn_Wkv': _L1_xattn_in['Wkv'], 'L1_xattn_null_kv': _L1_xattn_in['null_kv'], 'L1_xattn_Wout': _L1_xattn_in['Wout'], 'L1_xattn_ln_scale': _L1_xattn_in['ln_scale'], 'L1_xattn_ln_bias': _L1_xattn_in['ln_bias'], 'L1_ffn_Wg': _L1_ffn_in['Wg'], 'L1_ffn_W1': _L1_ffn_in['W1'], 'L1_ffn_W2': _L1_ffn_in['W2'], 'L1_ffn_W3': _L1_ffn_in['W3'], 'L1_ffn_Ws1': _L1_ffn_in['Ws1'], 'L1_ffn_Ws2': _L1_ffn_in['Ws2'], 'L1_ffn_Ws3': _L1_ffn_in['Ws3'], 'L2_xattn_W_in': _L2_xattn_in['W_in'], 'L2_xattn_b_in': _L2_xattn_in['b_in'], 'L2_xattn_g_res': _L2_xattn_in['g_res'], 'L2_xattn_g_init': _L2_xattn_in['g_init'], 'L2_ffn_router_w': _L2_ffn_in['router_w'], 'L2_ffn_router_b': _L2_ffn_in['router_b'], 'L2_ffn_gate_w': _L2_ffn_in['gate_w'], 'L2_ffn_up_w': _L2_ffn_in['up_w'], 'L2_ffn_down_w': _L2_ffn_in['down_w'], 'L3_xattn_w_qkv': _L3_xattn_in['w_qkv'], 'L3_xattn_w_proj': _L3_xattn_in['w_proj'], 'L3_xattn_b_proj': _L3_xattn_in['b_proj'], 'L3_ffn_Wr': _L3_ffn_in['Wr'], 'L3_ffn_br': _L3_ffn_in['br'], 'L3_ffn_W1': _L3_ffn_in['W1'], 'L3_ffn_b1': _L3_ffn_in['b1'], 'L3_ffn_W2': _L3_ffn_in['W2'], 'L3_ffn_b2': _L3_ffn_in['b2']}

def reference(x, ctx_2048, mask_BxS2_fk1, mask_BxS2_if0, L0_xattn_W_src, L0_xattn_b_src, L0_xattn_W_tgt, L0_xattn_b_tgt, L0_xattn_W_out, L0_xattn_b_out, L0_ffn_w_router, L0_ffn_b_router, L0_ffn_w1, L0_ffn_b1, L0_ffn_w2, L0_ffn_b2, L1_xattn_Wq, L1_xattn_Wkv, L1_xattn_null_kv, L1_xattn_Wout, L1_xattn_ln_scale, L1_xattn_ln_bias, L1_ffn_Wg, L1_ffn_W1, L1_ffn_W2, L1_ffn_W3, L1_ffn_Ws1, L1_ffn_Ws2, L1_ffn_Ws3, L2_xattn_W_in, L2_xattn_b_in, L2_xattn_g_res, L2_xattn_g_init, L2_ffn_router_w, L2_ffn_router_b, L2_ffn_gate_w, L2_ffn_up_w, L2_ffn_down_w, L3_xattn_w_qkv, L3_xattn_w_proj, L3_xattn_b_proj, L3_ffn_Wr, L3_ffn_br, L3_ffn_W1, L3_ffn_b1, L3_ffn_W2, L3_ffn_b2):
    import jax
    import jax.numpy as jnp

    def _L0_xattn_ref(src, tgt, src_mask, tgt_mask, W_src, b_src, W_tgt, b_tgt, W_out, b_out):
        import jax, jax.numpy as jnp
        import numpy as np
        B, S, T = (32, 64, 64)
        SRC_SIZE, TGT_SIZE, OUT_SIZE, NUM_HEAD = (256, 128, 128, 8)
        HEAD_DIM = OUT_SIZE // NUM_HEAD
        b, s, _ = src.shape
        t = tgt.shape[1]
        src_trans = jnp.einsum('bsf,of->bso', src, W_src) + b_src
        tgt_trans = jnp.einsum('btf,of->bto', tgt, W_tgt) + b_tgt
        src_trans = src_trans * src_mask[:, :, None]
        tgt_trans = tgt_trans * tgt_mask[:, :, None]
        src_key, src_val = jnp.split(src_trans, 2, axis=2)
        k = src_key.reshape(b, s, NUM_HEAD, HEAD_DIM)
        v = src_val.reshape(b, s, NUM_HEAD, HEAD_DIM)
        q = tgt_trans.reshape(b, t, NUM_HEAD, HEAD_DIM)
        scores = jnp.einsum('bthd,bshd->bhts', q, k) / np.sqrt(HEAD_DIM)
        scores = jnp.where(src_mask[:, None, None, :] == 0, -jnp.inf, scores)
        attn = jax.nn.softmax(scores, axis=-1)
        tgt_update = jnp.einsum('bhts,bshd->bthd', attn, v).reshape(b, t, OUT_SIZE)
        cat_tgt = jnp.concatenate([tgt, tgt_update], axis=2)
        return jnp.einsum('btf,of->bto', cat_tgt, W_out) + b_out

    def _L0_ffn_ref(x, w_router, b_router, w1, b1, w2, b2):
        import jax, jax.numpy as jnp
        import numpy as np
        B, T, C = (4, 256, 128)
        H, E = (512, 8)
        logits = jnp.einsum('btc,ce->bte', x, w_router) + b_router
        probs = jax.nn.softmax(logits, axis=-1)
        top1 = jnp.argmax(probs, axis=-1)
        out = jnp.zeros_like(x)
        for e in range(E):
            h = jax.nn.gelu(jnp.einsum('btc,ch->bth', x, w1[e]) + b1[e], approximate=False)
            y = jnp.einsum('bth,hc->btc', h, w2[e]) + b2[e]
            out = out + jnp.where((top1 == e)[..., None], y, 0.0)
        return out

    def _L1_xattn_ref(x, context, Wq, Wkv, null_kv, Wout, ln_scale, ln_bias):
        import jax, jax.numpy as jnp
        import numpy as np
        B, N, DIM = (8, 512, 128)
        M, CTX = (32, 256)
        HEADS, DH = (16, 64)
        INNER = HEADS * DH
        EPS = 1e-06

        def _split_heads(t):
            b, n, _ = t.shape
            return t.reshape(b, n, HEADS, DH).transpose(0, 2, 1, 3)
        scale = DH ** (-0.5)
        b = x.shape[0]
        q = _split_heads(jnp.einsum('bnd,df->bnf', x, Wq))
        kv = jnp.einsum('bmc,cf->bmf', context, Wkv)
        k, v = jnp.split(kv, 2, axis=-1)
        k, v = (_split_heads(k), _split_heads(v))
        nk = jnp.broadcast_to(null_kv[0], (b, HEADS, 1, DH))
        nv = jnp.broadcast_to(null_kv[1], (b, HEADS, 1, DH))
        k = jnp.concatenate((nk, k), axis=-2)
        v = jnp.concatenate((nv, v), axis=-2)
        q = q * scale
        sim = jnp.einsum('bhid,bhjd->bhij', q, k)
        attn = jax.nn.softmax(sim, axis=-1)
        out = jnp.einsum('bhij,bhjd->bhid', attn, v)
        out = out.transpose(0, 2, 1, 3).reshape(b, -1, INNER)
        out = jnp.einsum('bnf,fd->bnd', out, Wout)
        mu = jnp.mean(out, axis=-1, keepdims=True)
        var = jnp.var(out, axis=-1, keepdims=True)
        out = (out - mu) * jax.lax.rsqrt(var + EPS) * ln_scale + ln_bias
        return out

    def _L1_ffn_ref(x, Wg, W1, W2, W3, Ws1, Ws2, Ws3):
        import jax, jax.numpy as jnp
        import numpy as np
        B, T, C = (4, 256, 128)
        E = 8
        K = 2
        H = 176
        HS = 176 * 2
        b, t, c = x.shape
        xf = x.reshape(-1, c)
        n = xf.shape[0]
        router = xf @ Wg
        top_logits, idx = jax.lax.top_k(router, K)
        probs = jax.nn.softmax(top_logits.astype(jnp.float32), axis=-1).astype(x.dtype)
        w = jnp.zeros((n, E), x.dtype).at[jnp.arange(n)[:, None], idx].add(probs)
        h = jax.nn.silu(jnp.einsum('tc,ech->eth', xf, W1)) * jnp.einsum('tc,ech->eth', xf, W2)
        y = jnp.einsum('eth,ehc,te->tc', h, W3, w)
        y = y.reshape(b, t, c)
        hs = jax.nn.silu(xf @ Ws1) * (xf @ Ws2)
        y = y + (hs @ Ws3).reshape(b, t, c)
        return y

    def _L2_xattn_ref(embeds, patch_embeds, patch_lens, W_in, b_in, g_res, g_init):
        import jax, jax.numpy as jnp
        import numpy as np
        B, L, P = (4, 512, 128)
        D_MODEL = 128
        D_GLOBAL = 256
        HEADDIM = 32
        EPSILON = 0.001
        RMS_EPS = 1e-05

        def rmsnorm(x, g, eps=RMS_EPS):
            var = jnp.mean(jnp.square(x), axis=-1, keepdims=True)
            return x * jax.lax.rsqrt(var + eps) * g

        def _hnet_depool(h, h_patch_full, patch_lens):
            h_patch = h_patch_full[..., :D_MODEL]
            bsz, plen = (h_patch.shape[0], h_patch.shape[1])
            seqlen = h.shape[1]
            logp = jnp.full((bsz, plen), -EPSILON, dtype=jnp.float32)
            bidx = jnp.cumsum(patch_lens, axis=1) - 1
            boundary_mask = jnp.zeros((bsz, seqlen), dtype=jnp.int32)
            boundary_mask = boundary_mask.at[jnp.arange(bsz)[:, None], bidx].set(1)
            dt = (-jnp.log(-jnp.expm1(logp))).astype(h_patch.dtype)
            x = h_patch / dt[..., None]
            n_heads = D_MODEL // HEADDIM
            A = -jnp.ones((n_heads,), dtype=jnp.float32)
            bcoef = jnp.exp(logp).astype(h_patch.dtype)
            x4 = x.reshape(bsz, plen, n_heads, HEADDIM)
            a = jnp.exp(dt[:, :, None] * A[None, None, :])
            u = (dt * bcoef)[:, :, None, None] * x4
            a_b = jnp.broadcast_to(a[..., None], u.shape)

            def comb(lft, rgt):
                aL, uL = lft
                aR, uR = rgt
                return (aL * aR, uL * aR + uR)
            _, s = jax.lax.associative_scan(comb, (a_b, u), axis=1)
            depool = s.reshape(bsz, plen, D_MODEL)
            plug = jnp.clip(jnp.cumsum(boundary_mask, axis=1) - 1, 0, plen - 1)
            depool_out = depool[jnp.arange(bsz)[:, None], plug]
            return depool_out + h
        h = rmsnorm(embeds, g_res)
        h = jnp.einsum('bld,ed->ble', h, W_in) + b_in
        h_patch = rmsnorm(patch_embeds, g_init)
        return _hnet_depool(h, h_patch, patch_lens)

    def _L2_ffn_ref(x, router_w, router_b, gate_w, up_w, down_w):
        import jax, jax.numpy as jnp
        import numpy as np
        D_MODEL = 128
        D_INNER = 256
        N_EXPERTS = 8
        TOP_K = 2
        INIT_STD = 0.02
        logits = jnp.einsum('bsd,ed->bse', x, router_w) + router_b
        probs = jax.nn.softmax(logits, axis=-1)
        top_p, top_i = jax.lax.top_k(probs, TOP_K)
        top_p = top_p / jnp.sum(top_p, axis=-1, keepdims=True)
        onehot = jax.nn.one_hot(top_i, N_EXPERTS, dtype=x.dtype)
        combine = jnp.einsum('bsk,bske->bse', top_p, onehot)
        g = jnp.einsum('bsd,edf->ebsf', x, gate_w)
        u = jnp.einsum('bsd,edf->ebsf', x, up_w)
        h = jax.nn.silu(g) * u
        y = jnp.einsum('ebsf,efd->ebsd', h, down_w)
        out = jnp.einsum('ebsd,bse->bsd', y, combine)
        return out

    def _L3_xattn_ref(x, context, w_qkv, w_proj, b_proj):
        import jax, jax.numpy as jnp
        import numpy as np
        NUM_HEADS = 16
        B, N, C = x.shape
        H = NUM_HEADS
        D = C // H
        scale = D ** (-0.5)
        qkv = (x @ w_qkv.T).reshape(B, N, 3, H, D).transpose(2, 0, 3, 1, 4)
        q, k, v = (qkv[0], qkv[1], qkv[2])
        N_c = context.shape[1]
        kv = context.reshape(B, N_c, 2, H, D).transpose(2, 0, 3, 1, 4)
        extra_k, extra_v = (kv[0], kv[1])
        k = jnp.concatenate([extra_k, k], axis=2)
        v = jnp.concatenate([extra_v, v], axis=2)
        dtype = q.dtype
        attn = jnp.einsum('bhnd,bhmd->bhnm', q * scale, k).astype(jnp.float32)
        attn = jax.nn.softmax(attn, axis=-1).astype(dtype)
        out = jnp.einsum('bhnm,bhmd->bhnd', attn, v)
        out = out.transpose(0, 2, 1, 3).reshape(B, N, C)
        return out @ w_proj.T + b_proj

    def _L3_ffn_ref(x, Wr, br, W1, b1, W2, b2):
        import jax, jax.numpy as jnp
        import numpy as np
        B, S, D, H, E = (4, 256, 128, 256, 8)
        d = x.shape[-1]
        tokens = x.reshape(-1, d)
        logits = tokens @ Wr + br
        probs = jax.nn.softmax(logits, axis=-1)
        expert = jnp.argmax(probs, axis=-1)
        max_prob = jnp.take_along_axis(probs, expert[:, None], axis=-1)
        h = jax.nn.relu(jnp.einsum('td,edh->teh', tokens, W1) + b1[None])
        y = jnp.einsum('teh,ehd->ted', h, W2) + b2[None]
        out = jnp.take_along_axis(y, expert[:, None, None], axis=1)[:, 0, :]
        return (out * max_prob).reshape(x.shape)
    x = x + _L0_xattn_ref(ctx_2048, _layernorm(x, axis=-1), mask_BxS2_fk1, mask_BxS2_fk1, L0_xattn_W_src, L0_xattn_b_src, L0_xattn_W_tgt, L0_xattn_b_tgt, L0_xattn_W_out, L0_xattn_b_out)
    x = x + _L0_ffn_ref(_layernorm(x, axis=-1), L0_ffn_w_router, L0_ffn_b_router, L0_ffn_w1, L0_ffn_b1, L0_ffn_w2, L0_ffn_b2)
    x = x + _L1_xattn_ref(_layernorm(x, axis=-1), ctx_2048, L1_xattn_Wq, L1_xattn_Wkv, L1_xattn_null_kv, L1_xattn_Wout, L1_xattn_ln_scale, L1_xattn_ln_bias)
    x = x + _L1_ffn_ref(_layernorm(x, axis=-1), L1_ffn_Wg, L1_ffn_W1, L1_ffn_W2, L1_ffn_W3, L1_ffn_Ws1, L1_ffn_Ws2, L1_ffn_Ws3)
    x = x + _L2_xattn_ref(_layernorm(x, axis=-1), ctx_2048, mask_BxS2_if0, L2_xattn_W_in, L2_xattn_b_in, L2_xattn_g_res, L2_xattn_g_init)
    x = x + _L2_ffn_ref(_layernorm(x, axis=-1), L2_ffn_router_w, L2_ffn_router_b, L2_ffn_gate_w, L2_ffn_up_w, L2_ffn_down_w)
    x = x + _L3_xattn_ref(_layernorm(x, axis=-1), ctx_2048, L3_xattn_w_qkv, L3_xattn_w_proj, L3_xattn_b_proj)
    x = x + _L3_ffn_ref(_layernorm(x, axis=-1), L3_ffn_Wr, L3_ffn_br, L3_ffn_W1, L3_ffn_b1, L3_ffn_W2, L3_ffn_b2)
    return x

_drawn_inputs = setup_inputs


def setup_inputs(seed=0):
    import zlib

    import numpy as np

    out = dict(_drawn_inputs(seed))
    spreads = {'L0_xattn_b_src': (0.0, 0.1),
     'L0_xattn_b_tgt': (0.0, 0.7),
     'L0_xattn_b_out': (0.0, 0.1),
     'L0_ffn_b_router': (0.0, 0.1),
     'L0_ffn_b1': (0.0, 0.621),
     'L0_ffn_b2': (0.0, 0.1),
     'L1_xattn_ln_scale': (1.0, 0.2),
     'L1_xattn_ln_bias': (0.0, 0.1),
     'L2_xattn_b_in': (0.0, 0.1),
     'L2_xattn_g_res': (1.0, 0.6),
     'L2_xattn_g_init': (1.0, 0.2),
     'L2_ffn_router_b': (0.0, 0.8),
     'L3_ffn_br': (0.0, 0.8),
     'L3_ffn_b1': (0.0, 0.8),
     'L3_ffn_b2': (0.0, 0.8)}
    factors = {'L1_xattn_null_kv': 3.559,
     'L1_ffn_Wg': 8.0,
     'L1_ffn_W1': 8.0,
     'L1_ffn_W2': 8.0,
     'L1_ffn_W3': 8.0,
     'L1_ffn_Ws1': 8.0,
     'L1_ffn_Ws2': 8.0,
     'L1_ffn_Ws3': 8.0,
     'L2_ffn_router_w': 8.0,
     'L2_ffn_gate_w': 8.0,
     'L2_ffn_up_w': 8.0,
     'L2_ffn_down_w': 8.0,
     'L3_xattn_w_qkv': 6.735,
     'L3_xattn_b_proj': 17.137,
     'L3_ffn_Wr': 5.92,
     'L3_ffn_W1': 8.0,
     'L3_ffn_W2': 8.0}
    for name, (base, spread) in spreads.items():
        noise = np.random.default_rng([zlib.crc32(name.encode()), seed]).standard_normal(out[name].shape)
        drawn = base * np.exp(spread * noise) if base else spread * noise
        out[name] = jnp.asarray(drawn.astype(out[name].dtype))
    for name, factor in factors.items():
        out[name] = (out[name] * factor).astype(out[name].dtype)
    return out
```

```python
from contextlib import ExitStack

import concourse.bass as bass
import numpy as np
from concourse import mybir

F32 = mybir.dt.float32
BF16 = mybir.dt.bfloat16
I32 = mybir.dt.int32
ALU = mybir.AluOpType
ACT = mybir.ActivationFunctionType
AX = mybir.AxisListType.X

P = 128
B, S, D, CTX = 64, 64, 128, 256
TILES = B * S // P
GT = 4
GROUPS = TILES // GT
GN = GT * P
NE = 8
LN_EPS = 1e-5
HEADROOM = 8


class Signals:

    def __init__(self, nc, ctx, kind, by_engine):
        named = {name: ctx.enter_context(nc.semaphore(f"{kind}_{name}"))
                 for engine in by_engine for name in by_engine[engine]}
        self.done = named
        self.semaphores = {engine: [named[name] for name in by_engine[engine]] for engine in by_engine}
        self.values = {name: HEADROOM for name in named}

    def at(self):
        return dict(self.values)

    def phase_ends(self, counts, default):
        for name in self.values:
            self.values[name] += counts.get(name, default)


class Link:

    def __init__(self, eng, semaphore, value):
        self.eng, self.semaphore, self.value = eng, semaphore, value

    def __call__(self, instruction):
        self.value = self.value + 1
        instruction.then_inc(self.semaphore, 1)
        self.eng.wait_ge(self.semaphore, self.value)


class Core:

    def __init__(self, nc, ctx):
        self.nc, self.ctx = nc, ctx
        self.x = self.sb("x_tok", [P, TILES, D])
        self.mean_var = self.sb("mean_var", [P, TILES, 2])
        self.rstd = self.sb("rstd", [P, TILES])
        self.ident = self.sb("ident", [P, P])
        self.ctx_loads = 0

    def sb(self, name, shape, dt=F32):
        return self.ctx.enter_context(self.nc.sbuf_tensor(name, shape, dt))


class Experts:

    def __init__(self, tag, chunks, per, act, top, gated=False, b1=False, b2=False, br=False,
                 times_prob=False):
        self.shared = False
        self.tag, self.chunks, self.per, self.act, self.top = tag, chunks, per, act, top
        self.gated, self.b1, self.b2, self.br, self.times_prob = gated, b1, b2, br, times_prob
        self.spreads = chunks // per
        self.whole = top == 1 and not times_prob
        self.route_steps = (19 if top == 2 else 8 if times_prob else 6) + (1 if self.whole else 6)


PE_TURN_X, ACT_XT = 0, 2
PE_LOGITS, DVE_ROUTE_A = 3, 4
ACT_ROUTE, DVE_ROUTE_B = 6, 6
PE_TURN_W, DVE_WEIGHTS = 8, 9
PE_TURN_Y, DVE_UPDATE = 10, 12
UPDATE_STEPS = 3


def in_pairs(eng, body):
    body(0, 0)
    body(1, 1)
    with eng.Fori(1, GROUPS // 2 - 1) as pair:
        body(pair * 2, 0)
        body(pair * 2 + 1, 1)
    body(GROUPS - 2, 0)
    body(GROUPS - 1, 1)


def is_group(g, *which):
    return isinstance(g, int) and g in which


def experts_phase(core, cfg, io, loaded, out=None):
    nc = core.nc
    n, per = cfg.chunks, cfg.per
    done, at = core.expert_signals.done, core.expert_signals.at()

    with ExitStack() as local:
        def sb(name, shape, dt=F32):
            return local.enter_context(nc.sbuf_tensor(f"{cfg.tag}_{name}", shape, dt))

        def pb(name, shape):
            return local.enter_context(nc.psum_tensor(f"{cfg.tag}_{name}", shape, F32))

        xn = sb("xn", [P, 2, GT, D])
        xt = sb("xt", [P, 2, GN])
        act = sb("act", [P, 2, GN])
        prod = sb("prod", [P, GN])
        hid = sb("hid", [P, 2, GN])
        y_sb = sb("y_sb", [P, GN])
        logit = sb("logit", [P, GT, NE])
        others = sb("others", [P, GT, NE])
        hits = sb("hits", [P, GT, NE])
        first = sb("first", [P, GT, NE])
        second = sb("second", [P, GT, NE])
        best = sb("best", [P, GT])
        col = sb("col", [P, 4, GT])
        gap = sb("gap", [P, GT])
        fn = sb("fn", [P, GT, NE])
        w_tok = sb("w_tok", [P, GT, NE])
        w_t = sb("w_t", [NE, 2, GN])
        rest = sb("rest", [NE, 2, GN])
        w_parts = sb("w_parts", [P, 2, GN], BF16)
        std = sb("std", [P, TILES])
        stats = sb("stats", [P, GT, 6])
        mv = sb("mv", [P, GT, 2])

        g_ps = pb("g_ps", [P, 2, GN])
        u_ps = pb("u_ps", [P, 2, GN]) if cfg.gated else None
        w_ps = pb("w_ps", [P, 2, GN])
        y_ps = pb("y_ps", [P, GN])
        side = pb("side", [P, GN])

        block = local.enter_context(nc.Block())

        @block.tensor
        def _(pe):
            def turn_x(g, buf):
                pe.wait_ge(done["normed"], at["normed"] + g + 1)
                pe.wait_ge(done["x_updated"], at["x_updated"] + g - 2)
                for t in range(GT):
                    mm = nc.tensor.transpose(side[:, t * P:(t + 1) * P], xn[:, buf, t, :], core.ident[:, :])
                mm.then_inc(done["x_turned"], 1)

            def logits(g, buf):
                pe.wait_ge(done["xt_ready"], at["xt_ready"] + g + 1)
                for t in range(GT):
                    mm = nc.tensor.matmul(side[:, t * NE:(t + 1) * NE], xt[:, buf, t * P:(t + 1) * P],
                                          io["w_router"], start=True, stop=True)
                mm.then_inc(done["logits"], 1)

            def turn_w(g):
                pe.wait_ge(done["routed"], at["routed"] + g + 1)
                for t in range(GT):
                    mm = nc.tensor.transpose(side[0:NE, t * P:(t + 1) * P], w_tok[:, t, :], core.ident[:, :])
                mm.then_inc(done["w_turned"], 1)

            def turn_y(g):
                pe.wait_ge(done["y_out"], at["y_out"] + g + 1)
                pe.wait_ge(done["x_updated"], at["x_updated"] + g)
                ahead = min(g + 3, GROUPS) if isinstance(g, int) else g + 3
                pe.wait_ge(done["parts_ready"], at["parts_ready"] + ahead)
                for t in range(GT):
                    mm = nc.tensor.transpose(side[:, t * P:(t + 1) * P], y_sb[:, t * P:(t + 1) * P],
                                             core.ident[:, :])
                mm.then_inc(done["y_turned"], 1)

            def project(g, buf, c):
                k = g * n + c
                pe.wait_ge(done["activated"], at["activated"] + k - 1)
                nc.tensor.matmul(g_ps[:, c % 2, :], io["w_in"][:, c * P:(c + 1) * P], xt[:, buf, :],
                                 start=True, stop=True).then_inc(done["projected"], 1)
                if cfg.gated:
                    pe.wait_ge(done["gated"], at["gated"] + k - 1)
                    nc.tensor.matmul(u_ps[:, c % 2, :], io["w_up"][:, c * P:(c + 1) * P], xt[:, buf, :],
                                     start=True, stop=True).then_inc(done["up_projected"], 1)
                if c % per == 0:
                    s = c // per
                    if c == 0:
                        pe.wait_ge(done["parts_ready"], at["parts_ready"] + g + 1)
                    pe.wait_ge(done["weighted"], at["weighted"] + k - per)
                    nc.tensor.matmul(w_ps[:, s % 2, :], io["pick"][:, s, :], w_parts[:, buf, :],
                                     start=True, stop=True).then_inc(done["spread"], 1)

            def add(g, buf, c):
                if c == 0:
                    pe.wait_ge(done["y_out"], at["y_out"] + g)
                    if cfg.b2:
                        nc.tensor.matmul(y_ps[:, :], io["b_out"], w_t[:, buf, :], start=True, stop=False)
                pe.wait_ge(done["weighted"], at["weighted"] + g * n + c + 1)
                nc.tensor.matmul(y_ps[:, :], io["w_out"][:, c, :], hid[:, c % 2, :],
                                 start=(c == 0 and not cfg.b2), stop=(c == n - 1))\
                    .then_inc(done["summed"], 1)

            def body(g, buf):
                last = is_group(g, GROUPS - 1)
                for c in range(n):
                    if c + 2 < n:
                        project(g, buf, c + 2)
                    elif not last:
                        project(g + 1, 1 - buf, c + 2 - n)
                    add(g, buf, c)
                    if c == PE_TURN_X and not last:
                        turn_x(g + 1, 1 - buf)
                    if c == PE_LOGITS and not last:
                        logits(g + 1, 1 - buf)
                    if c == PE_TURN_W and not last:
                        turn_w(g + 1)
                    if c == PE_TURN_Y and not is_group(g, 0):
                        turn_y(g - 1)

            for s, v in loaded:
                pe.wait_ge(s, v)
            turn_x(0, 0)
            logits(0, 0)
            turn_w(0)
            project(0, 0, 0)
            project(0, 0, 1)
            in_pairs(pe, body)
            turn_y(GROUPS - 1)

        @block.scalar
        def _(act_eng):
            def xt_out(g, buf):
                act_eng.wait_ge(done["x_turned"], at["x_turned"] + g + 1)
                nc.scalar.activation(xt[:, buf, :], side[:, :], ACT.Copy).then_inc(done["xt_ready"], 1)

            def route_fn(g):
                if cfg.top == 2:
                    act_eng.wait_ge(done["gap_ready"], at["gap_ready"] + g + 1)
                    nc.scalar.activation(fn[:, :, 0], gap[:, :], ACT.Tanh, scale=0.5)\
                        .then_inc(done["fn_ready"], 1)
                elif cfg.times_prob:
                    act_eng.wait_ge(done["gap_ready"], at["gap_ready"] + g + 1)
                    nc.scalar.activation(fn[:, :, :], others[:, :, :], ACT.Exp).then_inc(done["fn_ready"], 1)

            def y_out(g):
                act_eng.wait_ge(done["summed"], at["summed"] + (g + 1) * n)
                act_eng.wait_ge(done["y_turned"], at["y_turned"] + g)
                nc.scalar.activation(y_sb[:, :], y_ps[:, :], ACT.Copy).then_inc(done["y_out"], 1)

            def activate(g, c):
                k = g * n + c
                act_eng.wait_ge(done["projected"], at["projected"] + k + 1)
                if cfg.gated:
                    act_eng.wait_ge(done["gated"], at["gated"] + k - 1)
                else:
                    act_eng.wait_ge(done["weighted"], at["weighted"] + k - 1)
                bias = io["b_in"][:, c:c + 1] if cfg.b1 else 0.0
                nc.scalar.activation(act[:, c % 2, :], g_ps[:, c % 2, :], cfg.act, bias=bias)\
                    .then_inc(done["activated"], 1)

            def body(g, buf):
                last = is_group(g, GROUPS - 1)
                for c in range(n):
                    activate(g, c)
                    if c == 1 and not is_group(g, 0):
                        y_out(g - 1)
                    if c == ACT_XT and not last:
                        xt_out(g + 1, 1 - buf)
                    if c == ACT_ROUTE and not last:
                        route_fn(g + 1)

            act_eng.wait_ge(done["std_in"], at["std_in"] + 1)
            nc.scalar.activation(std[:, :], std[:, :], ACT.Sqrt).then_inc(done["std"], 1)
            for s, v in loaded:
                act_eng.wait_ge(s, v)
            xt_out(0, 0)
            route_fn(0)
            in_pairs(act_eng, body)
            y_out(GROUPS - 1)

        @block.vector
        def _(dve):
            V = nc.vector

            def per_token(ap):
                return ap.unsqueeze(2).broadcast_to([P, GT, NE])

            def norm(g, buf):
                dve.wait_ge(done["x_turned"], at["x_turned"] + g - 1)
                for t in range(GT):
                    i = g * GT + t
                    ins = V.tensor_scalar(xn[:, buf, t, :], core.x[:, bass.ds(i, 1), :],
                                          core.mean_var[:, bass.ds(i, 1), 0], core.rstd[:, bass.ds(i, 1)],
                                          ALU.subtract, ALU.mult)
                ins.then_inc(done["normed"], 1)

            def one_hot(link, values, out):
                link(V.tensor_reduce(col[:, 0, :], values, AX, ALU.max))
                link(V.tensor_tensor(hits[:, :, :], values, per_token(col[:, 0, :]), ALU.is_equal))
                link(V.tensor_tensor(hits[:, :, :], hits[:, :, :], io["falling"], ALU.mult))
                link(V.tensor_reduce(col[:, 1, :], hits[:, :, :], AX, ALU.max))
                link(V.tensor_tensor(out, hits[:, :, :], per_token(col[:, 1, :]), ALU.is_equal))

            def route_a(g):
                dve.wait_ge(done["logits"], at["logits"] + g + 1)
                dve.wait_ge(done["w_turned"], at["w_turned"] + g)
                link = Link(dve, done["route_step"], at["route_step"] + g * cfg.route_steps)
                got = side[:, 0:GT * NE].rearrange("p (t e) -> p t e", e=NE)
                if cfg.br:
                    link(V.tensor_tensor(logit[:, :, :], got, io["b_router"], ALU.add))
                else:
                    link(V.tensor_copy(logit[:, :, :], got))
                one_hot(link, logit[:, :, :], first[:, :, :])
                if cfg.top == 2:
                    link(V.tensor_copy(best[:, :], col[:, 0, :]))
                    link(V.tensor_scalar(others[:, :, :], first[:, :, :], -1.0, 1.0, ALU.mult, ALU.add))
                    link(V.tensor_tensor(others[:, :, :], others[:, :, :], logit[:, :, :], ALU.mult))
                    link(V.scalar_tensor_tensor(others[:, :, :], first[:, :, :], -3e38, others[:, :, :],
                                                ALU.mult, ALU.add))
                    one_hot(link, others[:, :, :], second[:, :, :])
                    V.tensor_tensor(gap[:, :], best[:, :], col[:, 0, :], ALU.subtract)\
                        .then_inc(done["gap_ready"], 1)
                elif cfg.times_prob:
                    V.tensor_tensor(others[:, :, :], logit[:, :, :], per_token(col[:, 0, :]), ALU.subtract)\
                        .then_inc(done["gap_ready"], 1)
                else:
                    V.tensor_copy(w_tok[:, :, :], first[:, :, :]).then_inc(done["routed"], 1)
                return link

            def route_b(g, link):
                if cfg.top == 2:
                    dve.wait_ge(done["fn_ready"], at["fn_ready"] + g + 1)
                    link(V.tensor_scalar(col[:, 2, :], fn[:, :, 0], 0.5, 0.5, ALU.mult, ALU.add))
                    link(V.tensor_scalar(col[:, 3, :], fn[:, :, 0], -0.5, 0.5, ALU.mult, ALU.add))
                    link(V.tensor_tensor(first[:, :, :], first[:, :, :], per_token(col[:, 2, :]), ALU.mult))
                    link(V.tensor_tensor(second[:, :, :], second[:, :, :], per_token(col[:, 3, :]), ALU.mult))
                    V.tensor_tensor(w_tok[:, :, :], first[:, :, :], second[:, :, :], ALU.add)\
                        .then_inc(done["routed"], 1)
                elif cfg.times_prob:
                    dve.wait_ge(done["fn_ready"], at["fn_ready"] + g + 1)
                    link(V.tensor_reduce(col[:, 2, :], fn[:, :, :], AX, ALU.add))
                    link(V.reciprocal(col[:, 3, :], col[:, 2, :]))
                    V.tensor_tensor(w_tok[:, :, :], first[:, :, :], per_token(col[:, 3, :]), ALU.mult)\
                        .then_inc(done["routed"], 1)

            def weights_out(g, buf, link):
                dve.wait_ge(done["w_turned"], at["w_turned"] + g + 1)
                parts = w_parts[:, buf, :]
                link(V.tensor_copy(w_t[:, buf, :], side[0:NE, :]))
                if not cfg.whole:
                    link(V.tensor_copy(parts[0:NE, :], w_t[:, buf, :]))
                    link(V.tensor_tensor(rest[:, 0, :], w_t[:, buf, :], parts[0:NE, :], ALU.subtract))
                    link(V.tensor_copy(parts[32:32 + NE, :], rest[:, 0, :]))
                    link(V.tensor_copy(rest[:, 1, :], parts[32:32 + NE, :]))
                    link(V.tensor_tensor(rest[:, 1, :], rest[:, 0, :], rest[:, 1, :], ALU.subtract))
                    V.tensor_copy(parts[64:64 + NE, :], rest[:, 1, :]).then_inc(done["parts_ready"], 1)
                else:
                    V.tensor_copy(parts[0:NE, :], w_t[:, buf, :]).then_inc(done["parts_ready"], 1)

            def update_x(g):
                dve.wait_ge(done["y_turned"], at["y_turned"] + g + 1)
                link = Link(dve, done["update_step"], at["update_step"] + g * UPDATE_STEPS)
                x4 = core.x[:, bass.ds(g * GT, GT), :]
                link(V.tensor_tensor(x4, x4, side[:, :].rearrange("p (t d) -> p t d", d=D), ALU.add))
                dve.sem_inc(core.passed, 1)
                for t in range(GT):
                    ins = V.bn_stats(stats[:, t, :], core.x[:, bass.ds(g * GT + t, 1), :])
                link(ins)
                dve.sem_inc(core.passed, 1)
                for t in range(GT):
                    ins = V.bn_aggr(mv[:, t, :], stats[:, t, :])
                link(ins)
                V.tensor_copy(core.mean_var[:, bass.ds(g * GT, GT), :], mv[:, :, :])\
                    .then_inc(done["x_updated"], 1)

            def weight(g, c):
                k = g * n + c
                dve.wait_ge(done["activated"], at["activated"] + k + 1)
                got = act[:, c % 2, :]
                if cfg.gated:
                    dve.wait_ge(done["up_projected"], at["up_projected"] + k + 1)
                    dve.wait_ge(done["weighted"], at["weighted"] + k)
                    V.tensor_tensor(prod[:, :], got, u_ps[:, c % 2, :], ALU.mult).then_inc(done["gated"], 1)
                    dve.wait_ge(done["gated"], at["gated"] + k + 1)
                    got = prod[:, :]
                dve.wait_ge(done["spread"], at["spread"] + g * cfg.spreads + c // per + 1)
                dve.wait_ge(done["summed"], at["summed"] + k - 1)
                V.tensor_tensor(hid[:, c % 2, :], got, w_ps[:, (c // per) % 2, :], ALU.mult)\
                    .then_inc(done["weighted"], 1)

            def body(g, buf):
                last = is_group(g, GROUPS - 1)
                for c in range(n):
                    weight(g, c)
                    if c == DVE_ROUTE_A and not last:
                        link = route_a(g + 1)
                    if c == DVE_ROUTE_B and not last:
                        route_b(g + 1, link)
                    if c == DVE_WEIGHTS and not last:
                        weights_out(g + 1, 1 - buf, link)
                    if c == DVE_UPDATE:
                        if not is_group(g, 0):
                            update_x(g - 1)
                        if not is_group(g, GROUPS - 2, GROUPS - 1):
                            norm(g + 2, buf)

            V.tensor_scalar(std[:, :], core.mean_var[:, :, 1], LN_EPS, None, ALU.add).then_inc(done["std_in"], 1)
            V.memset(w_parts[:, :, :], 0.0).then_inc(done["cleared"], 1)
            dve.wait_ge(done["cleared"], at["cleared"] + 1)
            if cfg.shared:
                V.memset(w_parts[96:97, :, :], 1.0)
            dve.wait_ge(done["std"], at["std"] + 1)
            V.reciprocal(core.rstd[:, :], std[:, :]).then_inc(done["rstd"], 1)
            dve.wait_ge(done["rstd"], at["rstd"] + 1)
            for s, v in loaded:
                dve.wait_ge(s, v)
            norm(0, 0)
            norm(1, 1)
            link = route_a(0)
            route_b(0, link)
            weights_out(0, 0, link)
            in_pairs(dve, body)
            update_x(GROUPS - 1)

        @block.sync
        def _(sp):
            if out is None:
                return
            for g in range(GROUPS):
                sp.wait_ge(done["x_updated"], at["x_updated"] + g + 1)
                sp.dma_start(out[g * GN:(g + 1) * GN, :].rearrange("(t p) d -> p t d", p=P),
                             core.x[:, g * GT:(g + 1) * GT, :]).then_inc(core.out_done, 16)
            sp.wait_ge(core.out_done, 16 * GROUPS)

    counts = {"projected": GROUPS * n, "activated": GROUPS * n, "weighted": GROUPS * n, "summed": GROUPS * n,
              "spread": GROUPS * cfg.spreads, "route_step": GROUPS * cfg.route_steps,
              "update_step": GROUPS * UPDATE_STEPS, "std_in": 1, "std": 1, "rstd": 1, "cleared": 1,
              "up_projected": GROUPS * n * cfg.gated, "gated": GROUPS * n * cfg.gated,
              "gap_ready": GROUPS * (not cfg.whole), "fn_ready": GROUPS * (not cfg.whole)}
    core.expert_signals.phase_ends(counts, GROUPS)


EXPERT_SIGNALS = {
    "PE": ("x_turned", "logits", "w_turned", "y_turned", "projected", "up_projected", "spread", "summed"),
    "ACT": ("xt_ready", "fn_ready", "y_out", "activated", "std"),
    "DVE": ("normed", "routed", "parts_ready", "x_updated", "gated", "weighted", "std_in", "rstd",
            "cleared", "route_step", "update_step", "gap_ready"),
}


H0 = 8
HD0 = D // H0
PAIRS0 = H0 // 2
MASKED = -1e30


def over_tiles(eng, body):
    body(0, 0, 0)
    body(1, 1, 0)
    with eng.Fori(1, TILES // 2 - 1) as pair:
        body(pair * 2, 0, pair)
        body(pair * 2 + 1, 1, pair)
    body(TILES - 2, 0, TILES // 2 - 1)
    body(TILES - 1, 1, TILES // 2 - 1)


def start_later_loads(core, sp, phase):
    for dst, dram, sem in core.later[phase]:
        sp.dma_start(dst, dram).then_inc(sem, 16)


def is_tile(j, *which):
    return isinstance(j, int) and j in which


def load_contexts(core, sp, bufs, copies=1):
    done, at = core.attention_signals.done, core.attention_signals.at()
    ctx_dram = core.dram["ctx_t"]
    k0 = core.ctx_loads

    def body(j, buf, pair):
        sp.wait_ge(done["v_projected"], at["v_projected"] + j - 1)
        src = ctx_dram[:, bass.ds(j, 1), :, :].rearrange("p j h t -> p (j h) t")
        if copies == 1:
            sp.dma_start(bufs[:, buf, :, :], src).then_inc(core.ctx_in[buf], 16)
            return
        src = src.rearrange("p h (b s) -> p (h b) s", b=2)
        for i in range(copies):
            sp.dma_start(bufs[:, buf, :, i, :], src).then_inc(core.ctx_in[buf], 16)

    over_tiles(sp, body)
    core.ctx_loads = k0 + copies * TILES // 2


def new_rstd(core, std, act_eng=None, dve=None):
    nc, done, at = core.nc, core.attention_signals.done, core.attention_signals.at()
    if act_eng is not None:
        act_eng.wait_ge(done["std_in"], at["std_in"] + 1)
        nc.scalar.activation(std[:, :], std[:, :], ACT.Sqrt).then_inc(done["std"], 1)
    if dve is not None:
        nc.vector.tensor_scalar(std[:, :], core.mean_var[:, :, 1], LN_EPS, None, ALU.add)\
            .then_inc(done["std_in"], 1)
        dve.wait_ge(done["std"], at["std"] + 1)
        nc.vector.reciprocal(core.rstd[:, :], std[:, :]).then_inc(done["rstd"], 1)
        dve.wait_ge(done["rstd"], at["rstd"] + 1)


def add_to_x(core, dve, link, j, result, stats, mv):
    V = core.nc.vector
    xj = core.x[:, bass.ds(j, 1), :]
    link(V.tensor_tensor(xj, xj, result, ALU.add))
    dve.sem_inc(core.passed, 1)
    link(V.bn_stats(stats[:, :], xj))
    dve.sem_inc(core.passed, 1)
    link(V.bn_aggr(mv[:, :], stats[:, :]))
    V.tensor_copy(core.mean_var[:, bass.ds(j, 1), :], mv[:, :].unsqueeze(1))\
        .then_inc(core.attention_signals.done["updated"], 1)


ADD_STEPS = 3
ATTENTION_SIGNALS = {
    "PE": ("x_turned", "projected", "v_projected", "scored", "p_turned", "pv_done", "o_turned", "final",
           "act_piece", "v_half", "setup"),
    "ACT": ("xt_ready", "v_ready", "exped", "pt_ready", "ot_ready", "std", "act_read",
            "null_ready"),
    "DVE": ("normed", "proj_read", "s_read", "shifted", "o_ready", "updated", "std_in", "rstd", "cleared",
            "soft_step", "o_step", "add_step", "k_ready", "y_stats", "y_step"),
    "Pool": ("pool_setup", "pool_var", "y_rstd", "q_ready"),
}


def l0_attention(core, io, loaded, out=None):
    nc = core.nc
    done, at = core.attention_signals.done, core.attention_signals.at()
    scale = float(HD0) ** -0.5

    with ExitStack() as local:
        def sb(name, shape, dt=F32):
            return local.enter_context(nc.sbuf_tensor("l0a_" + name, shape, dt))

        def pb(name, shape):
            return local.enter_context(nc.psum_tensor("l0a_" + name, shape, F32))

        ctx_sb = sb("ctx", [P, 2, 4, 2, S])
        mask_q = sb("mask_q", [P, B * S])
        mask_k = sb("mask_k", [P, TILES, S])
        xn = sb("xn", [P, 2, D])
        xt = sb("xt", [P, 2, P])
        qt = sb("qt", [P, P])
        k_diag = sb("k_diag", [P, 2, H0, S])
        v_diag = sb("v_diag", [P, 2, 2, PAIRS0, 2, HD0 + 1])
        s_sb = sb("s_sb", [P, H0, S])
        probs = sb("probs", [P, H0, S])
        top = sb("top", [P, H0])
        pt = sb("pt", [P, PAIRS0, P])
        o_sb = sb("o_sb", [P, H0, HD0])
        inv = sb("inv", [P, H0])
        ot = sb("ot", [P, P])
        ones = sb("ones", [1, P])
        std = sb("std", [P, TILES])
        stats = sb("stats", [P, 6])
        mv = sb("mv", [P, 2])

        x_ps = pb("x_ps", [P, 512])
        qk_ps = pb("qk_ps", [P, 512])
        v_ps = pb("v_ps", [P, 512])
        s_ps = pb("s_ps", [P, H0, S])
        pt_ps = pb("pt_ps", [P, PAIRS0, P])
        o_ps = pb("o_ps", [P, 512])
        ot_ps = pb("ot_ps", [P, 512])
        y_ps = pb("y_ps", [P, 512])
        o_view = o_ps[:, 0:H0 * (HD0 + 1)].rearrange("p (h d) -> p h d", d=HD0 + 1)
        ctx_base = core.ctx_loads
        masks_in = core.masks_in

        block = local.enter_context(nc.Block())

        @block.sync
        def _(sp):
            sp.dma_start(mask_q[:, :], core.dram["mask"].rearrange("b s -> (b s)").unsqueeze(0)
                         .broadcast_to([P, B * S])).then_inc(masks_in, 16)
            for b in range(2):
                keys = core.dram["mask"].rearrange("(j b) s -> b j s", b=2)[b:b + 1, :, :]
                sp.dma_start(mask_k[b * S:(b + 1) * S, :, :], keys.broadcast_to([S, TILES, S]))\
                    .then_inc(masks_in, 16)
            load_contexts(core, sp, ctx_sb, copies=2)

        @block.tensor
        def _(pe):
            mmul = nc.tensor.matmul

            def turn_x(j, buf):
                pe.wait_ge(done["normed"], at["normed"] + j + 1)
                pe.wait_ge(done["xt_ready"], at["xt_ready"] + j)
                nc.tensor.transpose(x_ps[:, 0:P], xn[:, buf, :], core.ident[:, :]).then_inc(done["x_turned"], 1)

            def project(j, buf, pair):
                pe.wait_ge(done["xt_ready"], at["xt_ready"] + j + 1)
                pe.wait_ge(done["proj_read"], at["proj_read"] + j)
                pe.wait_ge(core.ctx_in[buf], (pair * 2 + ctx_base + 2) * 16)
                mmul(qk_ps[:, 0:P], io["w_q"], xt[:, buf, :], start=True, stop=True)
                for half in range(2):
                    mm = mmul(qk_ps[:, P:2 * P], io["w_k"][:, half, :], ctx_sb[:, buf, 2 * half:2 * half + 2, 0, :],
                              start=(half == 0), stop=(half == 1))
                mm.then_inc(done["projected"], 1)
                pe.wait_ge(done["v_ready"], at["v_ready"] + j)
                for b in range(2):
                    for half in range(2):
                        tok = ctx_sb[:, buf, 2 * half + b, :, :]
                        mm = mmul(v_ps[:, b * P:(b + 1) * P], tok, io["w_v"][:, half, :],
                                  start=(half == 0), stop=(half == 1))
                mm.then_inc(done["v_projected"], 1)

            def scores(j):
                pe.wait_ge(done["proj_read"], at["proj_read"] + j + 1)
                pe.wait_ge(done["s_read"], at["s_read"] + j)
                for b in range(2):
                    mm = mmul(s_ps[b * S:(b + 1) * S, :, :], qt[:, b * S:(b + 1) * S], k_diag[:, b, :, :],
                              start=True, stop=True)
                mm.then_inc(done["scored"], 1)

            def turn_p(j):
                pe.wait_ge(done["exped"], at["exped"] + j + 1)
                pe.wait_ge(done["pt_ready"], at["pt_ready"] + j)
                for c in range(PAIRS0):
                    mm = nc.tensor.transpose(pt_ps[:, c, :], probs[:, 2 * c:2 * c + 2, :], core.ident[:, :])
                mm.then_inc(done["p_turned"], 1)

            def weigh_v(j, buf):
                pe.wait_ge(done["pt_ready"], at["pt_ready"] + j + 1)
                pe.wait_ge(done["v_ready"], at["v_ready"] + j + 1)
                pe.wait_ge(done["o_ready"], at["o_ready"] + j)
                for c in range(PAIRS0):
                    for b in range(2):
                        mm = mmul(o_ps[b * S:(b + 1) * S, c * 2 * (HD0 + 1):(c + 1) * 2 * (HD0 + 1)],
                                  pt[:, c, b * S:(b + 1) * S], v_diag[:, buf, b, c, :, :], start=True, stop=True)
                mm.then_inc(done["pv_done"], 1)

            def turn_o(j):
                pe.wait_ge(done["o_ready"], at["o_ready"] + j + 1)
                pe.wait_ge(done["ot_ready"], at["ot_ready"] + j)
                nc.tensor.transpose(ot_ps[:, 0:P], o_sb[:, :, :], core.ident[:, :]).then_inc(done["o_turned"], 1)

            def final(j, buf):
                pe.wait_ge(done["ot_ready"], at["ot_ready"] + j + 1)
                pe.wait_ge(done["updated"], at["updated"] + j)
                mmul(y_ps[:, 0:D], xt[:, buf, :], io["w_o"][:, 0, :], start=True, stop=False)
                mmul(y_ps[:, 0:D], ot[:, :], io["w_o"][:, 1, :], start=False, stop=False)
                mmul(y_ps[:, 0:D], ones[:, :], io["b_o"], start=False, stop=True).then_inc(done["final"], 1)

            def body(j, buf, pair):
                last = is_tile(j, TILES - 1)
                if not last:
                    turn_x(j + 1, 1 - buf)
                if not is_tile(j, 0):
                    final(j - 1, 1 - buf)
                if not last:
                    project(j + 1, 1 - buf, pair + buf)
                turn_p(j)
                weigh_v(j, buf)
                if not last:
                    scores(j + 1)
                turn_o(j)

            for s, v in loaded:
                pe.wait_ge(s, v)
            turn_x(0, 0)
            project(0, 0, 0)
            scores(0)
            over_tiles(pe, body)
            final(TILES - 1, 1)

        @block.scalar
        def _(act_eng):
            A = nc.scalar

            def xt_out(j, buf):
                act_eng.wait_ge(done["x_turned"], at["x_turned"] + j + 1)
                act_eng.wait_ge(done["final"], at["final"] + j - 1)
                A.activation(xt[:, buf, :], x_ps[:, 0:P], ACT.Copy).then_inc(done["xt_ready"], 1)

            def v_out(j, buf):
                act_eng.wait_ge(done["v_projected"], at["v_projected"] + j + 1)
                act_eng.wait_ge(done["pv_done"], at["pv_done"] + j - 1)
                for b in range(2):
                    for h in range(2):
                        rows = slice(h * S, (h + 1) * S)
                        src = v_ps[rows, b * P:(b + 1) * P].rearrange("p (c h d) -> p c h d", h=2, d=HD0)
                        ins = A.activation(v_diag[rows, buf, b, :, h, 0:HD0], src[:, :, h, :], ACT.Copy)
                ins.then_inc(done["v_ready"], 1)

            def pt_out(j):
                act_eng.wait_ge(done["p_turned"], at["p_turned"] + j + 1)
                act_eng.wait_ge(done["pv_done"], at["pv_done"] + j)
                A.activation(pt[:, :, :], pt_ps[:, :, :], ACT.Copy).then_inc(done["pt_ready"], 1)

            def ot_out(j):
                act_eng.wait_ge(done["o_turned"], at["o_turned"] + j + 1)
                act_eng.wait_ge(done["final"], at["final"] + j)
                A.activation(ot[:, :], ot_ps[:, 0:P], ACT.Identity, bias=io["b_v"]).then_inc(done["ot_ready"], 1)

            def exps(j):
                act_eng.wait_ge(done["shifted"], at["shifted"] + j + 1)
                act_eng.wait_ge(done["p_turned"], at["p_turned"] + j)
                A.activation(probs[:, :, :], s_sb[:, :, :], ACT.Exp, scale=scale).then_inc(done["exped"], 1)

            def body(j, buf, pair):
                last = is_tile(j, TILES - 1)
                if not last:
                    xt_out(j + 1, 1 - buf)
                    v_out(j + 1, 1 - buf)
                pt_out(j)
                ot_out(j)
                if not last:
                    exps(j + 1)

            new_rstd(core, std, act_eng=act_eng)
            for s, v in loaded:
                act_eng.wait_ge(s, v)
            act_eng.wait_ge(done["cleared"], at["cleared"] + 3)
            xt_out(0, 0)
            v_out(0, 0)
            exps(0)
            over_tiles(act_eng, body)

        @block.vector
        def _(dve):
            V = nc.vector

            def norm(j, buf):
                dve.wait_ge(done["x_turned"], at["x_turned"] + j - 1)
                V.tensor_scalar(xn[:, buf, :], core.x[:, bass.ds(j, 1), :], core.mean_var[:, bass.ds(j, 1), 0],
                                core.rstd[:, bass.ds(j, 1)], ALU.subtract, ALU.mult).then_inc(done["normed"], 1)

            def qk_out(j):
                dve.wait_ge(done["projected"], at["projected"] + j + 1)
                dve.wait_ge(done["scored"], at["scored"] + j)
                V.scalar_tensor_tensor(qt[:, :], qk_ps[:, 0:P], io["b_q"], mask_q[:, bass.ds(j * P, P)],
                                       ALU.add, ALU.mult)
                head = io["heads"].unsqueeze(2).broadcast_to([P, H0, S])
                for b in range(2):
                    keys = qk_ps[:, P + b * S:P + (b + 1) * S].unsqueeze(1).broadcast_to([P, H0, S])
                    ins = V.scalar_tensor_tensor(k_diag[:, b, :, :], keys, io["b_k"], head, ALU.add, ALU.mult)
                ins.then_inc(done["proj_read"], 1)

            def soften(j):
                dve.wait_ge(done["scored"], at["scored"] + j + 1)
                dve.wait_ge(done["exped"], at["exped"] + j)
                link = Link(dve, done["soft_step"], at["soft_step"] + j)
                neg = mask_k[:, bass.ds(j, 1), :].broadcast_to([P, H0, S])
                V.tensor_tensor(s_sb[:, :, :], s_ps[:, :, :], neg, ALU.add).then_inc(done["s_read"], 1)
                dve.wait_ge(done["s_read"], at["s_read"] + j + 1)
                link(V.tensor_reduce(top[:, :], s_sb[:, :, :], AX, ALU.max))
                V.tensor_tensor(s_sb[:, :, :], s_sb[:, :, :], top[:, :].unsqueeze(2).broadcast_to([P, H0, S]),
                                ALU.subtract).then_inc(done["shifted"], 1)

            def scale_o(j):
                dve.wait_ge(done["pv_done"], at["pv_done"] + j + 1)
                dve.wait_ge(done["o_turned"], at["o_turned"] + j)
                link = Link(dve, done["o_step"], at["o_step"] + j)
                link(V.reciprocal(inv[:, :], o_view[:, :, HD0]))
                V.tensor_tensor(o_sb[:, :, :], o_view[:, :, 0:HD0],
                                inv[:, :].unsqueeze(2).broadcast_to([P, H0, HD0]), ALU.mult)\
                    .then_inc(done["o_ready"], 1)

            def update(j):
                dve.wait_ge(done["final"], at["final"] + j + 1)
                add_to_x(core, dve, Link(dve, done["add_step"], at["add_step"] + j * ADD_STEPS), j, y_ps[:, 0:D], stats, mv)

            def body(j, buf, pair):
                last = is_tile(j, TILES - 1)
                if not is_tile(j, 0):
                    update(j - 1)
                if not last:
                    qk_out(j + 1)
                scale_o(j)
                if not last:
                    soften(j + 1)
                if not is_tile(j, TILES - 2, TILES - 1):
                    norm(j + 2, buf)

            V.memset(v_diag[:, :, :, :, :, :], 0.0).then_inc(done["cleared"], 1)
            V.memset(ones[:, :], 1.0)
            dve.wait_ge(done["cleared"], at["cleared"] + 1)
            for h in range(2):
                ins = V.memset(v_diag[h * S:(h + 1) * S, :, :, :, h, HD0], 1.0)
                ins.then_inc(done["cleared"], 1)
            new_rstd(core, std, dve=dve)
            for s, v in loaded:
                dve.wait_ge(s, v)
            dve.wait_ge(masks_in, 48)
            V.tensor_scalar(mask_k[:, :, :], mask_k[:, :, :], 0.0, MASKED, ALU.is_equal, ALU.mult)\
                .then_inc(done["cleared"], 1)
            norm(0, 0)
            norm(1, 1)
            dve.wait_ge(done["cleared"], at["cleared"] + 4)
            qk_out(0)
            soften(0)
            over_tiles(dve, body)
            update(TILES - 1)

    core.attention_signals.phase_ends({"std_in": 1, "std": 1, "rstd": 1, "cleared": 4, "add_step": TILES * ADD_STEPS,
                      "act_piece": 0, "v_half": 0, "setup": 0, "act_read": 0, "null_ready": 0, "k_ready": 0,
                      "y_stats": 0, "y_step": 0, "pool_setup": 0, "pool_var": 0, "y_rstd": 0, "q_ready": 0}, TILES)
    if out is not None:
        store_x(core, out)


def store_x(core, out):
    nc = core.nc
    with nc.Block() as block:
        @block.sync
        def _(sp):
            sp.dma_start(out.rearrange("(t p) d -> p t d", p=P), core.x[:, :, :]).then_inc(core.out_done, 16)
            sp.wait_ge(core.out_done, 16)


H1 = 16
HD1 = 64
PAIRS1 = H1 // 2
HALF = PAIRS1 // 2
OUT_PIECES = ((0, 3), (3, 3), (6, 2))
L1_EPS = 1e-6
XT, Q0, Q1, PT0, PT1, OT0, OT1 = range(7)


def l1_attention(core, io, loaded, out=None):
    nc = core.nc
    done, at = core.attention_signals.done, core.attention_signals.at()
    scale = float(HD1) ** -0.5

    with ExitStack() as local:
        def sb(name, shape, dt=F32):
            return local.enter_context(nc.sbuf_tensor("l1a_" + name, shape, dt))

        ctx_sb = sb("ctx", [P, 2, 2, P])
        xn = sb("xn", [P, 2, D])
        xt = sb("xt", [P, P])
        qt = sb("qt", [P, PAIRS1, P])
        k_diag = sb("k_diag", [P, PAIRS1, 2, 2, S])
        v_sb = sb("v_sb", [P, 2, 2, PAIRS1, HD1 + 1])
        v_diag = sb("v_diag", [P, 2, 2, 2, PAIRS1, HD1 + 1])
        s_sb = sb("s_sb", [P, H1, S])
        probs = sb("probs", [P, H1, S])
        top = sb("top", [P, H1])
        null = sb("null", [P, H1])
        pt = sb("pt", [P, PAIRS1, P])
        den = sb("den", [P, H1])
        inv = sb("inv", [P, H1])
        o_sb = sb("o_sb", [P, H1, HD1])
        ot = sb("ot", [P, PAIRS1, P])
        ones = sb("ones", [1, P])
        row = sb("row", [1, D])
        std = sb("std", [P, TILES])
        stats = sb("stats", [P, 6])
        mv = sb("mv", [P, 2])
        y_stats = sb("y_stats", [P, 6])
        y_mv = sb("y_mv", [P, 2])
        y_var = sb("y_var", [P, 1])
        y_rstd = sb("y_rstd", [P, 1])
        minus_half = sb("minus_half", [P, 1])
        eps = sb("eps", [P, 1])
        y_sb = sb("y_sb", [P, 1, D])
        act_ps = local.enter_context(nc.psum_tensor("l1a_act_ps", [P, 2, 512], F32))
        dve_ps = local.enter_context(nc.psum_tensor("l1a_dve_ps", [P, 4, 512], F32))
        s_ps = local.enter_context(nc.psum_tensor("l1a_s_ps", [P, 2, 512], F32))
        ctx_base = core.ctx_loads
        v_in = core.v_in

        def number(j, piece):
            if is_tile(j, -1):
                return piece
            return 3 + 7 * j + piece - (3 if is_tile(j, TILES - 1) else 0)

        def out_piece(i):
            first, n = OUT_PIECES[i]
            view = dve_ps[:, i, 0:n * 2 * (HD1 + 1)].rearrange("p (h d) -> p h d", d=HD1 + 1)
            return view, 2 * first, 2 * n

        block = local.enter_context(nc.Block())

        @block.sync
        def _(sp):
            start_later_loads(core, sp, 2)

            def body(j, buf, pair):
                sp.wait_ge(done["v_projected"], at["v_projected"] + j - 1)
                sp.sem_inc(core.passed, 1)
                sp.dma_start(ctx_sb[:, buf, :, :], core.dram["ctx_t"][:, bass.ds(j, 1), :, :]
                             .rearrange("p j h t -> p (j h) t")).then_inc(core.ctx_in[buf], 16)
                if is_tile(j, 0):
                    return
                spread(j - 1, 1 - buf)

            def spread(j, buf):
                sp.wait_ge(done["v_ready"], at["v_ready"] + 2 * (j + 1))
                sp.sem_inc(core.passed, 1)
                sp.wait_ge(done["pv_done"], at["pv_done"] + j - 1)
                for b in range(2):
                    for h in range(2):
                        sp.dma_start(v_diag[h * S:(h + 1) * S, buf, b, h, :, :],
                                     v_sb[b * S:(b + 1) * S, buf, h, :, :]).then_inc(v_in[buf], 16)

            sp.wait_ge(done["cleared"], at["cleared"] + 3)
            over_tiles(sp, body)
            spread(TILES - 1, 1)

        @block.tensor
        def _(pe):
            mmul = nc.tensor.matmul

            def act_bank(j, piece):
                k = number(j, piece)
                pe.wait_ge(done["act_read"], at["act_read"] + (k if piece == XT else k - 1))
                return act_ps[:, piece % 2, :]

            def turn_x(j, buf):
                pe.wait_ge(done["normed"], at["normed"] + j + 2)
                to = act_bank(j, XT)
                nc.tensor.transpose(to[:, 0:P], xn[:, buf, :], core.ident[:, :]).then_inc(done["act_piece"], 1)

            def project(j, buf, pair):
                pe.wait_ge(done["act_read"], at["act_read"] + number(j, XT) + 1)
                for p in range(2):
                    to = act_bank(j, Q0 + p)
                    for c in range(HALF):
                        mm = mmul(to[:, c * P:(c + 1) * P], io["w_q"][:, (p * HALF + c) * P:(p * HALF + c + 1) * P],
                                  xt[:, :], start=True, stop=True)
                    mm.then_inc(done["act_piece"], 1)
                pe.wait_ge(core.ctx_in[buf], (pair + ctx_base + 1) * 16)
                pe.wait_ge(done["o_ready"], at["o_ready"] + 3 * j)
                for p in range(2):
                    for c in range(HALF):
                        col = (p * HALF + c) * P
                        for half in range(2):
                            mm = mmul(dve_ps[:, p, c * P:(c + 1) * P], io["w_k"][:, half, col:col + P],
                                      ctx_sb[:, buf, half, :], start=(half == 0), stop=(half == 1))
                    mm.then_inc(done["projected"], 1)
                for p in range(2):
                    if p == 1:
                        pe.wait_ge(done["updated"], at["updated"] + j)
                    for half in range(2):
                        mm = mmul(dve_ps[:, 2 + p, :], ctx_sb[:, buf, half, :],
                                  io["w_v"][:, half, p * 512:(p + 1) * 512], start=(half == 0), stop=(half == 1))
                    if p == 0:
                        mm.then_inc(done["v_half"], 1)
                mm.then_inc(done["v_projected"], 1)

            def scores(j):
                pe.wait_ge(done["act_read"], at["act_read"] + number(j, Q1) + 1)
                pe.wait_ge(done["k_ready"], at["k_ready"] + 2 * (j + 2))
                pe.wait_ge(done["shifted"], at["shifted"] + 2 * (j + 1))
                for p in range(2):
                    for c in range(HALF):
                        for b in range(2):
                            mm = mmul(s_ps[b * S:(b + 1) * S, p, c * P:(c + 1) * P],
                                      qt[:, p * HALF + c, b * S:(b + 1) * S], k_diag[:, p * HALF + c, b, :, :],
                                      start=True, stop=True)
                    mm.then_inc(done["scored"], 1)

            def turn_p(j):
                for p in range(2):
                    pe.wait_ge(done["exped"], at["exped"] + 2 * j + p + 1)
                    to = act_bank(j, PT0 + p)
                    for c in range(HALF):
                        h = 2 * (p * HALF + c)
                        mm = nc.tensor.transpose(to[:, c * P:(c + 1) * P], probs[:, h:h + 2, :], core.ident[:, :])
                    mm.then_inc(done["act_piece"], 1)

            def weigh_v(j, buf, pair):
                pe.wait_ge(done["act_read"], at["act_read"] + number(j, PT1) + 1)
                pe.wait_ge(v_in[buf], (pair + 1) * 64)
                ahead = min(j + 2, TILES) if isinstance(j, int) else j + 2
                pe.wait_ge(done["k_ready"], at["k_ready"] + 2 * ahead)
                pe.wait_ge(done["v_ready"], at["v_ready"] + 2 * ahead)
                for i, (first, n) in enumerate(OUT_PIECES):
                    for c in range(n):
                        for b in range(2):
                            w = 2 * (HD1 + 1)
                            mm = mmul(dve_ps[b * S:(b + 1) * S, i, c * w:(c + 1) * w],
                                      pt[:, first + c, b * S:(b + 1) * S],
                                      v_diag[:, buf, b, :, first + c, :], start=True, stop=True)
                mm.then_inc(done["pv_done"], 1)

            def turn_o(j):
                for p in range(2):
                    pe.wait_ge(done["o_ready"], at["o_ready"] + (3 * j + (2 if p == 0 else 3)))
                    to = act_bank(j, OT0 + p)
                    for c in range(HALF):
                        h = 2 * (p * HALF + c)
                        mm = nc.tensor.transpose(to[:, c * P:(c + 1) * P], o_sb[:, h:h + 2, :], core.ident[:, :])
                    mm.then_inc(done["act_piece"], 1)

            def final(j):
                pe.wait_ge(done["act_read"], at["act_read"] + number(j, OT1) + 1)
                y = dve_ps[:, 3, 0:D]
                ahead = min(j + 2, TILES) if isinstance(j, int) else j + 2
                pe.wait_ge(done["v_ready"], at["v_ready"] + 2 * ahead)
                for c in range(PAIRS1):
                    mmul(y, ot[:, c, :], io["w_o"][:, c, :], start=(c == 0), stop=False)
                mmul(y, ones[:, :], row[:, :], start=False, stop=True).then_inc(done["final"], 1)

            def body(j, buf, pair):
                last = is_tile(j, TILES - 1)
                if not last:
                    turn_x(j, 1 - buf)
                if not is_tile(j, 0):
                    final(j - 1)
                if not last:
                    project(j, 1 - buf, pair + buf)
                turn_p(j)
                weigh_v(j, buf, pair)
                if not last:
                    scores(j)
                turn_o(j)

            for s, v in loaded:
                pe.wait_ge(s, v)
            for c in range(PAIRS1):
                mm = mmul(dve_ps[0:1, 3, 0:D], io["null_v"], io["w_o"][:, c, :], start=(c == 0),
                          stop=(c == PAIRS1 - 1))
            mm.then_inc(done["setup"], 1)
            pe.wait_ge(done["cleared"], at["cleared"] + 4)
            turn_x(-1, 0)
            project(-1, 0, 0)
            scores(-1)
            over_tiles(pe, body)
            final(TILES - 1)

        @block.scalar
        def _(act_eng):
            A = nc.scalar

            def out_to(j, piece, to, func=ACT.Copy):
                act_eng.wait_ge(done["act_piece"], at["act_piece"] + number(j, piece) + 1)
                src = act_ps[:, piece % 2, 0:P if piece == XT else 512]
                A.activation(to, src, func).then_inc(done["act_read"], 1)

            def exps(j):
                for p in range(2):
                    act_eng.wait_ge(done["shifted"], at["shifted"] + 2 * (j + 1) + p + 1)
                    hs = slice(p * H1 // 2, (p + 1) * H1 // 2)
                    A.activation(probs[:, hs, :], s_sb[:, hs, :], ACT.Exp, scale=scale).then_inc(done["exped"], 1)
                A.activation(null[:, :], top[:, :], ACT.Exp, scale=-scale).then_inc(done["null_ready"], 1)

            def x_and_q(j):
                out_to(j, XT, xt[:, :])
                out_to(j, Q0, qt[:, 0:HALF, :])
                out_to(j, Q1, qt[:, HALF:PAIRS1, :])

            def body(j, buf, pair):
                last = is_tile(j, TILES - 1)
                if not last:
                    x_and_q(j)
                out_to(j, PT0, pt[:, 0:HALF, :])
                out_to(j, PT1, pt[:, HALF:PAIRS1, :])
                out_to(j, OT0, ot[:, 0:HALF, :])
                out_to(j, OT1, ot[:, HALF:PAIRS1, :])
                if not last:
                    exps(j)

            new_rstd(core, std, act_eng=act_eng)
            x_and_q(-1)
            exps(-1)
            over_tiles(act_eng, body)

        @block.gpsimd
        def _(pool):
            G = nc.gpsimd
            G.memset(minus_half[:, :], -0.5).then_inc(done["pool_setup"], 1)
            G.memset(eps[:, :], L1_EPS).then_inc(done["pool_setup"], 1)
            pool.wait_ge(done["pool_setup"], at["pool_setup"] + 2)

            def body(j, buf, pair):
                pool.wait_ge(done["y_stats"], at["y_stats"] + j + 1)
                pool.wait_ge(done["updated"], at["updated"] + j)
                G.tensor_tensor(y_var[:, :], y_mv[:, 1:2], eps[:, :], ALU.add).then_inc(done["pool_var"], 1)
                pool.wait_ge(done["pool_var"], at["pool_var"] + j + 1)
                G.tensor_tensor(y_rstd[:, :], y_var[:, :], minus_half[:, :], ALU.pow).then_inc(done["y_rstd"], 1)

            over_tiles(pool, body)

        @block.vector
        def _(dve):
            V = nc.vector

            def norm(j, buf):
                dve.wait_ge(done["projected"], at["projected"] + 2 * (j - 1))
                V.tensor_scalar(xn[:, buf, :], core.x[:, bass.ds(j, 1), :], core.mean_var[:, bass.ds(j, 1), 0],
                                core.rstd[:, bass.ds(j, 1)], ALU.subtract, ALU.mult).then_inc(done["normed"], 1)

            def k_out(j):
                for p in range(2):
                    dve.wait_ge(done["projected"], at["projected"] + 2 * j + p + 1)
                    for h in range(2):
                        rows = slice(h * S, (h + 1) * S)
                        src = dve_ps[rows, p, :].rearrange("p (c b s) -> p c b s", c=HALF, b=2)
                        ins = V.tensor_scalar(k_diag[rows, p * HALF:(p + 1) * HALF, :, h, :], src,
                                              io["null_k"][rows, :], None, ALU.subtract)
                    ins.then_inc(done["k_ready"], 1)

            def v_out(j, buf, pair):
                dve.wait_ge(v_in[buf], pair * 64)
                for p in range(2):
                    if p == 0:
                        dve.wait_ge(done["v_half"], at["v_half"] + j + 1)
                    else:
                        dve.wait_ge(done["v_projected"], at["v_projected"] + j + 1)
                    V.tensor_tensor(v_sb[:, buf, p, :, 0:HD1],
                                    dve_ps[:, 2 + p, :].rearrange("p (c d) -> p c d", d=HD1),
                                    io["null_v_row"].unsqueeze(1).broadcast_to([P, PAIRS1, HD1]), ALU.subtract)\
                        .then_inc(done["v_ready"], 1)

            def soften(j):
                link = Link(dve, done["soft_step"], at["soft_step"] + 2 * j)
                dve.wait_ge(done["null_ready"], at["null_ready"] + j)
                for p in range(2):
                    dve.wait_ge(done["scored"], at["scored"] + 2 * j + p + 1)
                    hs = slice(p * H1 // 2, (p + 1) * H1 // 2)
                    ins = V.tensor_reduce(top[:, hs], s_ps[:, p, :].rearrange("p (h s) -> p h s", s=S), AX, ALU.max)
                link(ins)
                link(V.tensor_scalar(top[:, :], top[:, :], 0.0, None, ALU.max))
                for p in range(2):
                    hs = slice(p * H1 // 2, (p + 1) * H1 // 2)
                    ins = V.tensor_tensor(s_sb[:, hs, :], s_ps[:, p, :].rearrange("p (h s) -> p h s", s=S),
                                          top[:, hs].unsqueeze(2).broadcast_to([P, H1 // 2, S]), ALU.subtract)
                    ins.then_inc(done["shifted"], 1)

            def scale_o(j):
                dve.wait_ge(done["pv_done"], at["pv_done"] + j + 1)
                dve.wait_ge(done["null_ready"], at["null_ready"] + j + 1)
                link = Link(dve, done["o_step"], at["o_step"] + 2 * j)
                for i in range(3):
                    view, h0, n = out_piece(i)
                    ins = V.tensor_tensor(den[:, h0:h0 + n], view[:, :, HD1], null[:, h0:h0 + n], ALU.add)
                link(ins)
                link(V.reciprocal(inv[:, :], den[:, :]))
                for i in range(3):
                    view, h0, n = out_piece(i)
                    V.tensor_tensor(o_sb[:, h0:h0 + n, :], view[:, :, 0:HD1],
                                    inv[:, h0:h0 + n].unsqueeze(2).broadcast_to([P, n, HD1]), ALU.mult)\
                        .then_inc(done["o_ready"], 1)

            def y_statistics(j):
                dve.wait_ge(done["final"], at["final"] + j + 1)
                dve.wait_ge(done["y_rstd"], at["y_rstd"] + j)
                V.bn_stats(y_stats[:, :], dve_ps[:, 3, 0:D]).then_inc(done["y_step"], 1)
                dve.wait_ge(done["y_step"], at["y_step"] + j + 1)
                dve.sem_inc(core.passed, 1)
                V.bn_aggr(y_mv[:, :], y_stats[:, :]).then_inc(done["y_stats"], 1)

            def update(j):
                dve.wait_ge(done["y_stats"], at["y_stats"] + j + 1)
                dve.wait_ge(done["y_rstd"], at["y_rstd"] + j + 1)
                link = Link(dve, done["add_step"], at["add_step"] + j * 5)
                xj = core.x[:, bass.ds(j, 1), :]
                y = dve_ps[:, 3, 0:D].unsqueeze(1)
                link(V.scalar_tensor_tensor(y_sb[:, :, :], y, y_mv[:, 0:1], io["ln_scale"].unsqueeze(1),
                                            ALU.subtract, ALU.mult))
                link(V.scalar_tensor_tensor(y_sb[:, :, :], y_sb[:, :, :], y_rstd[:, :],
                                            io["ln_bias"].unsqueeze(1), ALU.mult, ALU.add))
                add_to_x(core, dve, link, j, y_sb[:, 0, :], stats, mv)

            def body(j, buf, pair):
                last = is_tile(j, TILES - 1)
                if not is_tile(j, 0):
                    y_statistics(j - 1)
                if not last:
                    k_out(j + 1)
                if not is_tile(j, 0):
                    update(j - 1)
                if not last:
                    v_out(j + 1, 1 - buf, pair + buf)
                scale_o(j)
                if not last:
                    soften(j + 1)
                if not is_tile(j, TILES - 2, TILES - 1):
                    norm(j + 2, buf)

            V.memset(v_diag[:, :, :, :, :, :], 0.0).then_inc(done["cleared"], 1)
            V.memset(k_diag[:, :, :, :, :], 0.0).then_inc(done["cleared"], 1)
            V.memset(ones[:, :], 1.0)
            V.memset(v_sb[:, :, :, :, :], 1.0).then_inc(done["cleared"], 1)
            new_rstd(core, std, dve=dve)
            for s, v in loaded:
                dve.wait_ge(s, v)
            dve.wait_ge(done["setup"], at["setup"] + 1)
            V.tensor_copy(row[:, :], dve_ps[0:1, 3, 0:D]).then_inc(done["cleared"], 1)
            dve.wait_ge(done["cleared"], at["cleared"] + 4)
            norm(0, 0)
            norm(1, 1)
            k_out(0)
            v_out(0, 0, 0)
            soften(0)
            over_tiles(dve, body)
            y_statistics(TILES - 1)
            update(TILES - 1)

    two, three, one = 2 * TILES, 3 * TILES, 1
    core.attention_signals.phase_ends({
                      "std_in": one, "std": one, "rstd": one, "cleared": 4, "setup": one, "pool_setup": 2,
                      "act_read": 7 * TILES, "act_piece": 7 * TILES, "projected": two, "scored": two,
                      "k_ready": two, "v_ready": two, "exped": two, "shifted": two, "o_ready": three,
                      "soft_step": two, "o_step": two, "add_step": 5 * TILES,
                      "x_turned": 0, "p_turned": 0, "o_turned": 0, "xt_ready": 0, "pt_ready": 0, "ot_ready": 0,
                      "proj_read": 0, "s_read": 0, "q_ready": 0}, TILES)
    core.ctx_loads += TILES // 2
    if out is not None:
        store_x(core, out)


RMS_EPS2 = 1e-5
LOG_P = -0.001


def l2_depool(core, io, loaded, out=None):
    nc = core.nc
    done, at = core.depool_signals.done, core.depool_signals.at()

    with ExitStack() as local:
        def sb(name, shape, dt=F32):
            return local.enter_context(nc.sbuf_tensor("l2d_" + name, shape, dt))

        def pb(name, shape):
            return local.enter_context(nc.psum_tensor("l2d_" + name, shape, F32))

        lens = sb("lens", [B, S], I32)
        count = sb("count", [B, S])
        ones_row = sb("ones_row", [B, S])
        last = sb("last", [B, S])
        wrap = sb("wrap", [B, S])
        plug = sb("plug", [B, S])
        cube = sb("cube", [B, S, S])
        all_ones = sb("all_ones", [B, S])
        spread_m = sb("spread_m", [P, TILES, P])
        w_in = sb("w_in", [P, D])
        ms = sb("ms", [P, TILES])
        std = sb("std", [P, TILES])
        xn = sb("xn", [P, 2, GT, D])
        xt = sb("xt", [P, GN])
        ctx_sb = sb("ctx", [P, 2, GT, CTX])
        squares = sb("squares", [P, CTX])
        ssq = sb("ssq", [P, GT])
        msq = sb("msq", [P, GT])
        scale_c = sb("scale_c", [P, GT])
        minus_half = sb("minus_half", [P, GT])
        patch = sb("patch", [P, GT, D])
        y_sb = sb("y_sb", [P, GN])
        stats = sb("stats", [P, GT, 6])
        mv = sb("mv", [P, GT, 2])
        m_ps = pb("m_ps", [P, 2, 512])
        x_ps = pb("x_ps", [P, GN])
        y_ps = pb("y_ps", [P, 2, GN])
        t_ps = pb("t_ps", [P, GN])
        base = core.ctx_loads

        block = local.enter_context(nc.Block())

        @block.sync
        def _(sp):
            sp.dma_start(lens[:, :], core.dram["lens"]).then_inc(core.lens_in, 16)
            start_later_loads(core, sp, 4)
            tokens = core.dram["ctx_tok"].rearrange("(t p) f -> p t f", p=P)

            def body(g, buf):
                sp.wait_ge(done["patches"], at["patches"] + g - 1)
                sp.sem_inc(core.passed, 1)
                sp.dma_start(ctx_sb[:, buf, :, :], tokens[:, bass.ds(g * GT, GT), :]).then_inc(core.ctx_in[buf], 16)

            in_pairs(sp, body)

        @block.tensor
        def _(pe):
            mmul = nc.tensor.matmul

            def turn_x(g, buf):
                pe.wait_ge(done["normed"], at["normed"] + g + 1)
                pe.wait_ge(done["xt_ready"], at["xt_ready"] + g)
                for t in range(GT):
                    mm = nc.tensor.transpose(x_ps[:, t * P:(t + 1) * P], xn[:, buf, t, :], core.ident[:, :])
                mm.then_inc(done["x_turned"], 1)

            def mix(g, buf):
                pe.wait_ge(done["xt_ready"], at["xt_ready"] + g + 1)
                pe.wait_ge(done["patches"], at["patches"] + g + 1)
                pe.wait_ge(done["y_out"], at["y_out"] + g - 1)
                for t in range(GT):
                    to = y_ps[:, buf, t * P:(t + 1) * P]
                    mmul(to, w_in[:, :], xt[:, t * P:(t + 1) * P], start=True, stop=False)
                    mm = mmul(to, patch[:, t, :], spread_m[:, bass.ds(g * GT + t, 1), :]
                              .rearrange("p a s -> p (a s)"), start=False, stop=True)
                mm.then_inc(done["mixed"], 1)

            def turn_y(g):
                pe.wait_ge(done["y_out"], at["y_out"] + g + 1)
                pe.wait_ge(done["updated"], at["updated"] + g)
                for t in range(GT):
                    mm = nc.tensor.transpose(t_ps[:, t * P:(t + 1) * P], y_sb[:, t * P:(t + 1) * P], core.ident[:, :])
                mm.then_inc(done["y_turned"], 1)

            def body(g, buf):
                if not is_group(g, GROUPS - 1):
                    turn_x(g + 1, 1 - buf)
                mix(g, buf)
                if not is_group(g, 0):
                    turn_y(g - 1)

            for s, v in loaded:
                pe.wait_ge(s, v)
            pe.wait_ge(done["plugged"], at["plugged"] + 1)
            flat = cube[:, :, :].rearrange("p b s -> p (b s)")
            for n in range(8):
                pe.wait_ge(done["compared"], at["compared"] + n - 1)
                mmul(m_ps[0:S, n % 2, :], all_ones[:, :], flat[:, n * 512:(n + 1) * 512], start=True, stop=True)\
                    .then_inc(done["spread"], 1)
            for n in range(8):
                pe.wait_ge(done["compared"], at["compared"] + 8)
                pe.wait_ge(done["m_out"], at["m_out"] + n - 1)
                mmul(m_ps[:, n % 2, :], io["decay"], flat[:, n * 512:(n + 1) * 512], start=True, stop=True)\
                    .then_inc(done["m_made"], 1)
            turn_x(0, 0)
            pe.wait_ge(done["m_out"], at["m_out"] + 8)
            in_pairs(pe, body)
            turn_y(GROUPS - 1)

        @block.scalar
        def _(act_eng):
            A = nc.scalar

            def y_out(g, buf):
                act_eng.wait_ge(done["mixed"], at["mixed"] + g + 1)
                act_eng.wait_ge(done["y_turned"], at["y_turned"] + g)
                A.activation(y_sb[:, :], y_ps[:, buf, :], ACT.Identity, bias=io["b_in"]).then_inc(done["y_out"], 1)

            def group(g, buf, pair):
                y_out(g, buf)
                if not is_group(g, GROUPS - 1):
                    act_eng.wait_ge(done["x_turned"], at["x_turned"] + g + 2)
                    A.activation(xt[:, :], x_ps[:, :], ACT.Copy).then_inc(done["xt_ready"], 1)
                if not is_group(g, GROUPS - 2, GROUPS - 1):
                    squares_of(g + 2, buf, pair + 1)

            def squares_of(g, buf, pair):
                act_eng.wait_ge(core.ctx_in[buf], (pair + base + 1) * 16)
                act_eng.wait_ge(done["msq"], at["msq"] + g)
                for t in range(GT):
                    A.activation(squares[:, :], ctx_sb[:, buf, t, :], ACT.Square, accum_out=ssq[:, t:t + 1])\
                        .then_inc(done["square_step"], 1)
                    act_eng.wait_ge(done["square_step"], at["square_step"] + g * GT + t + 1)

            act_eng.wait_ge(done["std_in"], at["std_in"] + 1)
            A.activation(std[:, :], std[:, :], ACT.Sqrt).then_inc(done["std"], 1)
            act_eng.wait_ge(done["std_in"], at["std_in"] + 2)
            A.activation(ms[:, :], ms[:, :], ACT.Sqrt).then_inc(done["std"], 1)
            for s, v in loaded:
                act_eng.wait_ge(s, v)
            squares_of(0, 0, 0)
            squares_of(1, 1, 0)
            act_eng.wait_ge(done["x_turned"], at["x_turned"] + 1)
            A.activation(xt[:, :], x_ps[:, :], ACT.Copy).then_inc(done["xt_ready"], 1)
            group(0, 0, 0)
            group(1, 1, 0)
            with act_eng.Fori(1, GROUPS // 2 - 1) as pair:
                group(pair * 2, 0, pair)
                group(pair * 2 + 1, 1, pair)
            group(GROUPS - 2, 0, GROUPS // 2 - 1)
            group(GROUPS - 1, 1, GROUPS // 2 - 1)

        @block.gpsimd
        def _(pool):
            G = nc.gpsimd
            G.memset(minus_half[:, :], -0.5).then_inc(done["pool_setup"], 1)
            pool.wait_ge(done["pool_setup"], at["pool_setup"] + 1)

            def body(g, buf):
                pool.wait_ge(done["msq"], at["msq"] + g + 1)
                pool.wait_ge(done["patches"], at["patches"] + g)
                G.tensor_tensor(scale_c[:, :], msq[:, :], minus_half[:, :], ALU.pow).then_inc(done["scale_c"], 1)

            in_pairs(pool, body)

        @block.vector
        def _(dve):
            V = nc.vector

            def norm(g, buf):
                dve.wait_ge(done["x_turned"], at["x_turned"] + g - 1)
                for t in range(GT):
                    i = g * GT + t
                    ins = V.tensor_scalar(xn[:, buf, t, :], core.x[:, bass.ds(i, 1), :],
                                          core.mean_var[:, bass.ds(i, 1), 0], core.rstd[:, bass.ds(i, 1)],
                                          ALU.subtract, ALU.mult)
                ins.then_inc(done["normed"], 1)

            def mean_squares(g):
                dve.wait_ge(done["square_step"], at["square_step"] + (g + 1) * GT)
                dve.wait_ge(done["scale_c"], at["scale_c"] + g)
                V.tensor_scalar(msq[:, :], ssq[:, :], 1.0 / CTX, RMS_EPS2, ALU.mult, ALU.add)\
                    .then_inc(done["msq"], 1)

            def patches(g, buf):
                dve.wait_ge(done["scale_c"], at["scale_c"] + g + 1)
                dve.wait_ge(done["mixed"], at["mixed"] + g)
                for t in range(GT):
                    ins = V.scalar_tensor_tensor(patch[:, t, :], ctx_sb[:, buf, t, 0:D], scale_c[:, t:t + 1],
                                                 io["g_init"], ALU.mult, ALU.mult)
                ins.then_inc(done["patches"], 1)

            def update(g):
                dve.wait_ge(done["y_turned"], at["y_turned"] + g + 1)
                link = Link(dve, done["update_step"], at["update_step"] + g * UPDATE_STEPS)
                x4 = core.x[:, bass.ds(g * GT, GT), :]
                link(V.tensor_tensor(x4, x4, t_ps[:, :].rearrange("p (t d) -> p t d", d=D), ALU.add))
                dve.sem_inc(core.passed, 1)
                for t in range(GT):
                    ins = V.bn_stats(stats[:, t, :], core.x[:, bass.ds(g * GT + t, 1), :])
                link(ins)
                dve.sem_inc(core.passed, 1)
                for t in range(GT):
                    ins = V.bn_aggr(mv[:, t, :], stats[:, t, :])
                link(ins)
                V.tensor_copy(core.mean_var[:, bass.ds(g * GT, GT), :], mv[:, :, :]).then_inc(done["updated"], 1)

            def body(g, buf):
                if not is_group(g, GROUPS - 1):
                    mean_squares(g + 1)
                    patches(g + 1, 1 - buf)
                if not is_group(g, 0):
                    update(g - 1)
                if not is_group(g, GROUPS - 2, GROUPS - 1):
                    norm(g + 2, buf)

            link = Link(dve, done["setup_step"], at["setup_step"])
            link(V.tensor_scalar(std[:, :], core.mean_var[:, :, 1], LN_EPS, None, ALU.add))
            V.memset(ones_row[:, :], 1.0).then_inc(done["std_in"], 1)
            link(V.memset(all_ones[:, :], 1.0))
            link(V.memset(spread_m[:, :, :], 0.0))
            dve.wait_ge(done["std"], at["std"] + 1)
            link(V.reciprocal(core.rstd[:, :], std[:, :]))
            link(V.tensor_tensor(ms[:, :], core.rstd[:, :], core.rstd[:, :], ALU.mult))
            link(V.tensor_tensor(ms[:, :], ms[:, :], core.mean_var[:, :, 1], ALU.mult))
            V.tensor_scalar(ms[:, :], ms[:, :], RMS_EPS2, None, ALU.add).then_inc(done["std_in"], 1)
            dve.wait_ge(done["std"], at["std"] + 2)
            link(V.reciprocal(ms[:, :], ms[:, :]))
            link(V.tensor_tensor(core.rstd[:, :], core.rstd[:, :], ms[:, :], ALU.mult))
            for s, v in loaded:
                dve.wait_ge(s, v)
            norm(0, 0)
            norm(1, 1)
            link(V.tensor_scalar(w_in[:, :], io["w_in"], io["g_res"], None, ALU.mult))
            dve.wait_ge(core.lens_in, 16)
            link(V.tensor_copy(count[:, :], lens[:, :]))
            link(V.tensor_tensor_scan(last[:, :], ones_row[:, :], count[:, :], 0.0, ALU.mult, ALU.add))
            link(V.tensor_scalar(last[:, :], last[:, :], -1.0, None, ALU.add))
            link(V.tensor_scalar(wrap[:, :], last[:, :], 0.0, float(S), ALU.is_lt, ALU.mult))
            link(V.tensor_tensor(last[:, :], last[:, :], wrap[:, :], ALU.add))
            link(V.tensor_tensor(cube[:, :, :], last[:, :].unsqueeze(1).broadcast_to([B, S, S]),
                                 io["token"].unsqueeze(2).broadcast_to([B, S, S]), ALU.is_equal))
            link(V.tensor_reduce(wrap[:, :], cube[:, :, :], AX, ALU.max))
            link(V.tensor_tensor_scan(count[:, :], ones_row[:, :], wrap[:, :], 0.0, ALU.mult, ALU.add))
            link(V.tensor_scalar(plug[:, :], count[:, :], -1.0, 0.0, ALU.add, ALU.max))
            link(V.tensor_scalar(plug[:, :], plug[:, :], float(S - 1), None, ALU.min))
            V.tensor_tensor(cube[:, :, :], plug[:, :].unsqueeze(1).broadcast_to([B, B, S]),
                            core.ident[0:B, 0:B].unsqueeze(2).broadcast_to([B, B, S]), ALU.mult)\
                .then_inc(done["plugged"], 1)
            flat = cube[:, :, :].rearrange("p b s -> p (b s)")
            for n in range(8):
                dve.wait_ge(done["spread"], at["spread"] + n + 1)
                V.tensor_scalar(flat[:, n * 512:(n + 1) * 512], m_ps[0:S, n % 2, :], io["number"], None, ALU.is_equal)\
                    .then_inc(done["compared"], 1)
            for n in range(8):
                dve.wait_ge(done["m_made"], at["m_made"] + n + 1)
                got = m_ps[:, n % 2, :].rearrange("p (t b s) -> p t b s", b=2, s=S)
                for b in range(2):
                    rows = slice(b * S, (b + 1) * S)
                    ins = V.tensor_copy(spread_m[rows, n * GT:(n + 1) * GT, b * S:(b + 1) * S], got[rows, :, b, :])
                ins.then_inc(done["m_out"], 1)
            mean_squares(0)
            patches(0, 0)
            in_pairs(dve, body)
            update(GROUPS - 1)

    core.ctx_loads += GROUPS // 2
    if out is not None:
        store_x(core, out)


DEPOOL_SIGNALS = {
    "PE": ("x_turned", "mixed", "y_turned", "spread", "m_made"),
    "ACT": ("xt_ready", "y_out", "square_step", "std"),
    "Pool": ("pool_setup", "scale_c"),
    "DVE": ("normed", "patches", "msq", "updated", "update_step", "std_in", "setup_step", "plugged", "compared",
            "m_out"),
}


H3 = 16
HD3 = D // H3
KEYS3 = 2 * S
BANK_HEADS = 512 // KEYS3
BANKS3 = H3 // BANK_HEADS


def l3_attention(core, io, loaded, out=None):
    nc = core.nc
    done, at = core.attention_signals.done, core.attention_signals.at()
    scale = float(HD3) ** -0.5
    X, P0, O = 0, 1, 1 + BANKS3
    PIECES = 2 + BANKS3

    with ExitStack() as local:
        def sb(name, shape, dt=F32):
            return local.enter_context(nc.sbuf_tensor("l3a_" + name, shape, dt))

        def pb(name, shape):
            return local.enter_context(nc.psum_tensor("l3a_" + name, shape, F32))

        k_all = sb("k_all", [P, 2, 2, 2, S])
        ctx_v = sb("ctx_v", [S, 2, 2, D])
        v_all = sb("v_all", [P, 2, 2, H3, HD3 + 1])
        xn = sb("xn", [P, 2, D])
        xt = sb("xt", [P, P])
        qt = sb("qt", [P, P])
        q_head = sb("q_head", [P, 2, H3, S])
        s_sb = sb("s_sb", [P, H3, KEYS3])
        probs = sb("probs", [P, H3, KEYS3])
        top = sb("top", [P, H3])
        pt = sb("pt", [P, H3, P])
        inv = sb("inv", [P, H3])
        o_sb = sb("o_sb", [P, H3, HD3])
        ot = sb("ot", [P, P])
        ones = sb("ones", [1, P])
        std = sb("std", [P, TILES])
        stats = sb("stats", [P, 6])
        mv = sb("mv", [P, 2])
        act_ps = pb("act_ps", [P, 2, 512])
        s_ps = pb("s_ps", [P, BANKS3, BANK_HEADS, KEYS3])
        qkv_ps = pb("qkv_ps", [P, 4, P])
        o_ps = pb("o_ps", [P, 512])
        o_view = o_ps[:, 0:H3 * (HD3 + 1)].rearrange("p (h d) -> p h d", d=HD3 + 1)
        ctx_base = core.ctx_loads

        def number(j, piece):
            if is_tile(j, -1):
                return 0
            return 1 + PIECES * j + piece - (1 if is_tile(j, TILES - 1) else 0)

        def heads_of(p):
            return slice(p * BANK_HEADS, (p + 1) * BANK_HEADS)

        block = local.enter_context(nc.Block())

        @block.sync
        def _(sp):
            tokens = core.dram["ctx_tok"].rearrange("(j b s) f -> s j b f", b=2, s=S)

            def body(j, buf, pair):
                sp.wait_ge(done["pv_done"], at["pv_done"] + j - 1)
                sp.sem_inc(core.passed, 1)
                keys = core.dram["ctx_t"][:, bass.ds(j, 1), 0, :].rearrange("p j (b s) -> p (j b) s", b=2)
                sp.dma_start(k_all[:, buf, :, 0, :], keys).then_inc(core.ctx_in[buf], 16)
                sp.dma_start(ctx_v[:, buf, :, :], tokens[:, bass.ds(j, 1), :, D:2 * D]
                             .rearrange("s j b f -> s (j b) f")).then_inc(core.ctx_in[buf], 16)

            over_tiles(sp, body)

        @block.tensor
        def _(pe):
            mmul = nc.tensor.matmul

            def act_bank(j, piece):
                k = number(j, piece)
                same = piece == P0 and is_tile(j, TILES - 1)
                pe.wait_ge(done["act_read"], at["act_read"] + (k if same else k - 1))
                return act_ps[:, (piece + 1) % 2, :]

            def turn_x(j, buf):
                pe.wait_ge(done["normed"], at["normed"] + j + 2)
                to = act_bank(j, X)
                nc.tensor.transpose(to[:, 0:P], xn[:, buf, :], core.ident[:, :]).then_inc(done["act_piece"], 1)

            def project(j):
                pe.wait_ge(done["act_read"], at["act_read"] + number(j, X) + 1)
                pe.wait_ge(done["k_ready"], at["k_ready"] + j + 1)
                for i in range(2):
                    mmul(qkv_ps[:, i, :], io["w_qkv"][:, i * D:(i + 1) * D], xt[:, :], start=True, stop=True)
                for b in range(2):
                    mm = mmul(qkv_ps[S:P, 2 + b, :], xt[:, b * S:(b + 1) * S], io["w_qkv"][:, 2 * D:3 * D],
                              start=True, stop=True)
                mm.then_inc(done["projected"], 1)

            def scores(j, buf, pair):
                pe.wait_ge(done["q_ready"], at["q_ready"] + j + 2)
                pe.wait_ge(core.ctx_in[buf], (2 * pair + ctx_base + 2) * 16)
                pe.wait_ge(done["shifted"], at["shifted"] + BANKS3 * (j + 1))
                for p in range(BANKS3):
                    for h in range(BANK_HEADS):
                        for b in range(2):
                            mm = mmul(s_ps[b * S:(b + 1) * S, p, h, :], q_head[:, b, p * BANK_HEADS + h, :],
                                      k_all[:, buf, b, :, :], start=True, stop=True)
                    mm.then_inc(done["scored"], 1)

            def turn_p(j):
                for p in range(BANKS3):
                    pe.wait_ge(done["exped"], at["exped"] + BANKS3 * j + p + 1)
                    to = act_bank(j, P0 + p)
                    for h in range(BANK_HEADS):
                        mm = nc.tensor.transpose(to[:, h * P:(h + 1) * P], probs[:, p * BANK_HEADS + h, :],
                                                 core.ident[:, :])
                    mm.then_inc(done["act_piece"], 1)

            def weigh_v(j, buf):
                pe.wait_ge(done["v_ready"], at["v_ready"] + j + 1)
                pe.wait_ge(done["k_ready"], at["k_ready"] + j + 1)
                pe.wait_ge(done["updated"], at["updated"] + j)
                for p in range(BANKS3):
                    pe.wait_ge(done["act_read"], at["act_read"] + number(j, P0 + p) + 1)
                    for h in range(p * BANK_HEADS, (p + 1) * BANK_HEADS):
                        for b in range(2):
                            mm = mmul(o_ps[b * S:(b + 1) * S, h * (HD3 + 1):(h + 1) * (HD3 + 1)],
                                      pt[:, h, b * S:(b + 1) * S], v_all[:, buf, b, h, :], start=True, stop=True)
                mm.then_inc(done["pv_done"], 1)

            def turn_o(j):
                pe.wait_ge(done["o_ready"], at["o_ready"] + j + 1)
                to = act_bank(j, O)
                nc.tensor.transpose(to[:, 0:P], o_sb[:, :, :], core.ident[:, :]).then_inc(done["act_piece"], 1)

            def final(j):
                pe.wait_ge(done["act_read"], at["act_read"] + number(j, O) + 1)
                mmul(o_ps[:, 0:D], ot[:, :], io["w_proj"], start=True, stop=False)
                mmul(o_ps[:, 0:D], ones[:, :], io["b_proj"], start=False, stop=True).then_inc(done["final"], 1)

            def body(j, buf, pair):
                last = is_tile(j, TILES - 1)
                if not last:
                    turn_x(j, 1 - buf)
                if not is_tile(j, 0):
                    final(j - 1)
                if not last:
                    project(j)
                turn_p(j)
                weigh_v(j, buf)
                if not last:
                    scores(j, 1 - buf, pair + buf)
                turn_o(j)

            for s, v in loaded:
                pe.wait_ge(s, v)
            pe.wait_ge(done["cleared"], at["cleared"] + 1)
            turn_x(-1, 0)
            project(-1)
            scores(-1, 0, 0)
            over_tiles(pe, body)
            final(TILES - 1)

        @block.scalar
        def _(act_eng):
            A = nc.scalar

            def out_to(j, piece, to):
                act_eng.wait_ge(done["act_piece"], at["act_piece"] + number(j, piece) + 1)
                src = act_ps[:, (piece + 1) % 2, 0:P if piece in (X, O) else 512]
                A.activation(to, src, ACT.Copy).then_inc(done["act_read"], 1)

            def exps(j):
                for p in range(BANKS3):
                    act_eng.wait_ge(done["shifted"], at["shifted"] + BANKS3 * (j + 1) + p + 1)
                    A.activation(probs[:, heads_of(p), :], s_sb[:, heads_of(p), :], ACT.Exp, scale=scale)\
                        .then_inc(done["exped"], 1)

            def body(j, buf, pair):
                last = is_tile(j, TILES - 1)
                if not last:
                    out_to(j, X, xt[:, :])
                for p in range(BANKS3):
                    out_to(j, P0 + p, pt[:, heads_of(p), :])
                out_to(j, O, ot[:, :])
                if not last:
                    exps(j)

            new_rstd(core, std, act_eng=act_eng)
            out_to(-1, X, xt[:, :])
            exps(-1)
            over_tiles(act_eng, body)

        @block.gpsimd
        def _(pool):
            G = nc.gpsimd

            def body(j, buf, pair):
                pool.wait_ge(core.ctx_in[buf], (2 * pair + ctx_base + 2) * 16)
                pool.sem_inc(core.passed, 1)
                G.tensor_copy(v_all[0:S, buf, :, :, 0:HD3],
                              ctx_v[:, buf, :, :].rearrange("p b (h d) -> p b h d", d=HD3)).then_inc(done["v_ready"], 1)
                pool.wait_ge(done["k_ready"], at["k_ready"] + j + 1)
                pool.wait_ge(done["scored"], at["scored"] + BANKS3 * j)
                for b in range(2):
                    ins = G.tensor_tensor(q_head[:, b, :, :],
                                          qt[:, b * S:(b + 1) * S].unsqueeze(1).broadcast_to([P, H3, S]),
                                          io["heads"].unsqueeze(2).broadcast_to([P, H3, S]), ALU.mult)
                ins.then_inc(done["q_ready"], 1)

            for s, v in loaded:
                pool.wait_ge(s, v)
            pool.wait_ge(done["cleared"], at["cleared"] + 2)
            over_tiles(pool, body)

        @block.vector
        def _(dve):
            V = nc.vector

            def norm(j, buf):
                dve.wait_ge(done["projected"], at["projected"] + j - 1)
                V.tensor_scalar(xn[:, buf, :], core.x[:, bass.ds(j, 1), :], core.mean_var[:, bass.ds(j, 1), 0],
                                core.rstd[:, bass.ds(j, 1)], ALU.subtract, ALU.mult).then_inc(done["normed"], 1)

            def qkv_out(j, buf):
                dve.wait_ge(done["projected"], at["projected"] + j + 1)
                dve.wait_ge(done["q_ready"], at["q_ready"] + j)
                dve.wait_ge(done["pv_done"], at["pv_done"] + j - 1)
                V.tensor_copy(qt[:, :], qkv_ps[:, 0, :])
                V.tensor_copy(k_all[:, buf, :, 1, :], qkv_ps[:, 1, :].rearrange("p (b s) -> p b s", b=2))
                V.tensor_copy(v_all[S:P, buf, :, :, 0:HD3],
                              qkv_ps[S:P, 2:4, :].rearrange("p b (h d) -> p b h d", d=HD3))\
                    .then_inc(done["k_ready"], 1)

            def soften(j):
                link = Link(dve, done["soft_step"], at["soft_step"] + BANKS3 * j)
                dve.wait_ge(done["exped"], at["exped"] + BANKS3 * j)
                for p in range(BANKS3):
                    dve.wait_ge(done["scored"], at["scored"] + BANKS3 * j + p + 1)
                    link(V.tensor_reduce(top[:, heads_of(p)], s_ps[:, p, :, :], AX, ALU.max))
                    V.tensor_tensor(s_sb[:, heads_of(p), :], s_ps[:, p, :, :],
                                    top[:, heads_of(p)].unsqueeze(2).broadcast_to([P, BANK_HEADS, KEYS3]),
                                    ALU.subtract).then_inc(done["shifted"], 1)

            def scale_o(j):
                dve.wait_ge(done["pv_done"], at["pv_done"] + j + 1)
                link = Link(dve, done["o_step"], at["o_step"] + j)
                link(V.reciprocal(inv[:, :], o_view[:, :, HD3]))
                V.tensor_tensor(o_sb[:, :, :], o_view[:, :, 0:HD3],
                                inv[:, :].unsqueeze(2).broadcast_to([P, H3, HD3]), ALU.mult)\
                    .then_inc(done["o_ready"], 1)

            def update(j):
                dve.wait_ge(done["final"], at["final"] + j + 1)
                add_to_x(core, dve, Link(dve, done["add_step"], at["add_step"] + j * ADD_STEPS), j, o_ps[:, 0:D], stats, mv)

            def body(j, buf, pair):
                last = is_tile(j, TILES - 1)
                if not is_tile(j, 0):
                    update(j - 1)
                if not last:
                    qkv_out(j + 1, 1 - buf)
                scale_o(j)
                if not last:
                    soften(j + 1)
                if not is_tile(j, TILES - 2, TILES - 1):
                    norm(j + 2, buf)

            V.memset(ones[:, :], 1.0).then_inc(done["cleared"], 1)
            V.memset(v_all[:, :, :, :, :], 1.0).then_inc(done["cleared"], 1)
            dve.wait_ge(done["cleared"], at["cleared"] + 2)
            new_rstd(core, std, dve=dve)
            for s, v in loaded:
                dve.wait_ge(s, v)
            norm(0, 0)
            norm(1, 1)
            qkv_out(0, 0)
            soften(0)
            over_tiles(dve, body)
            update(TILES - 1)

    core.ctx_loads += TILES
    if out is not None:
        store_x(core, out)


L0_FFN = Experts("l0f", 32, 4, ACT.Gelu, top=1, b1=True, b2=True, br=True)
L1_FFN = Experts("l1f", 14, 1, ACT.Silu, top=2, gated=True)
L1_FFN.shared = True
L2_FFN = Experts("l2f", 16, 2, ACT.Silu, top=2, gated=True, br=True)
L3_FFN = Experts("l3f", 16, 2, ACT.Relu, top=1, b1=True, b2=True, br=True, times_prob=True)


WEIGHT_SLOTS = {1: "a", 5: "a", 3: "b", 7: "b"}
LOADED_IN = {5: 2, 7: 4}
SLOT_WORDS = {"a": 2 * L0_FFN.chunks * P, "b": 3 * L1_FFN.chunks * P}

PART_ROWS = (0, 32, 64)
SHARED_ROW = 96


def opening(core, src, loads):
    nc = core.nc
    kinds = (core.expert_signals, core.attention_signals, core.depool_signals)
    with ExitStack() as local:
        stats = local.enter_context(nc.sbuf_tensor("open_stats", [P, GT, 6], F32))
        mv = local.enter_context(nc.sbuf_tensor("open_mv", [P, GT, 2], F32))
        block = local.enter_context(nc.Block())

        @block.sync
        def _(sp):
            for g in range(GROUPS):
                sp.dma_start(core.x[:, g * GT:(g + 1) * GT, :],
                             src[g * GN:(g + 1) * GN, :].rearrange("(t p) d -> p t d", p=P))\
                    .then_inc(core.x_in[g], 16)
            for dst, dram, sem in loads:
                sp.dma_start(dst, dram).then_inc(sem, 16)

        @block.tensor
        def _(pe):
            for kind in kinds:
                for semaphore in kind.semaphores.get("PE", ()):
                    pe.sem_inc(semaphore, HEADROOM)

        @block.scalar
        def _(act_eng):
            for kind in kinds:
                for semaphore in kind.semaphores.get("ACT", ()):
                    act_eng.sem_inc(semaphore, HEADROOM)

        @block.gpsimd
        def _(pool):
            for kind in kinds:
                for semaphore in kind.semaphores.get("Pool", ()):
                    pool.sem_inc(semaphore, HEADROOM)

        @block.vector
        def _(dve):
            V = nc.vector
            for kind in kinds:
                for semaphore in kind.semaphores.get("DVE", ()):
                    dve.sem_inc(semaphore, HEADROOM)
            link = Link(dve, core.statistics_step, 0)
            for g in range(GROUPS):
                dve.wait_ge(core.x_in[g], 16)
                for t in range(GT):
                    ins = V.bn_stats(stats[:, t, :], core.x[:, g * GT + t, :])
                link(ins)
                for t in range(GT):
                    ins = V.bn_aggr(mv[:, t, :], stats[:, t, :])
                link(ins)
                link(V.tensor_copy(core.mean_var[:, g * GT:(g + 1) * GT, :], mv[:, :, :]))


def program(nc, dram, out, phases="01234567"):
    with ExitStack() as ctx:
        core = Core(nc, ctx)
        core.expert_signals = Signals(nc, ctx, "experts", EXPERT_SIGNALS)
        core.attention_signals = Signals(nc, ctx, "attention", ATTENTION_SIGNALS)
        core.depool_signals = Signals(nc, ctx, "depool", DEPOOL_SIGNALS)
        core.statistics_step = ctx.enter_context(nc.semaphore("statistics_step"))
        core.dram = dram
        core.ctx_in = [ctx.enter_context(nc.semaphore(f"ctx_in_{b}")) for b in range(2)]
        core.v_in = [ctx.enter_context(nc.semaphore(f"v_in_{b}")) for b in range(2)]
        core.lens_in = ctx.enter_context(nc.semaphore("lens_in"))
        core.masks_in = ctx.enter_context(nc.semaphore("masks_in"))
        core.x_in = [ctx.enter_context(nc.semaphore(f"x_in_{g}")) for g in range(GROUPS)]
        core.passed = ctx.enter_context(nc.semaphore("passed"))
        core.out_done = ctx.enter_context(nc.semaphore("out_done"))
        loads, io = [], {}

        slots = {name: core.sb(f"weight_slot_{name}", [P, size]) for name, size in SLOT_WORDS.items()}
        later = {after: [] for after in LOADED_IN.values()}
        core.later = later

        def load(phase, *names):
            taken = [0]
            if str(phase) not in phases:
                return
            sem = ctx.enter_context(nc.semaphore(f"loaded_{phase}"))
            for name in names:
                a = dram[name]
                part = name.split("_", 1)[1]
                if phase in WEIGHT_SLOTS and part in ("w_in", "w_up", "w_out"):
                    words = int(np.prod(a.shape[1:]))
                    held = slots[WEIGHT_SLOTS[phase]][:, taken[0]:taken[0] + words]
                    taken[0] += words
                    if part == "w_out":
                        held = held.rearrange("p (c d) -> p c d", d=D)
                else:
                    held = core.sb("s_" + name, list(a.shape), a.dtype)[:]
                after = LOADED_IN.get(phase)
                (later[after] if str(after) in phases else loads).append((held, a[:], sem))
                io[name] = held
            return (sem, 16 * len(names))

        sem0 = ctx.enter_context(nc.semaphore("loaded_consts"))
        for t, name in ((core.ident, "ident"),):
            loads.append((t[:], dram[name][:], sem0))
        falling = core.sb("s_falling", [P, GT, NE])
        loads.append((falling[:], dram["falling"][:], sem0))
        consts = (sem0, 32)

        def tensors(phase, tag, names):
            got = load(phase, *[tag + "_" + n for n in names])
            if got is None:
                return
            return got, {**{n: io[tag + "_" + n] for n in names}, "falling": falling[:]}

        plan = {
            1: (L0_FFN, ("w_in", "w_out", "w_router", "pick", "b_in", "b_out", "b_router")),
            3: (L1_FFN, ("w_in", "w_up", "w_out", "w_router", "pick")),
            5: (L2_FFN, ("w_in", "w_up", "w_out", "w_router", "pick", "b_router")),
            7: (L3_FFN, ("w_in", "w_out", "w_router", "pick", "b_in", "b_out", "b_router")),
        }
        attention = {
            2: (l1_attention, "l1a", ("w_q", "w_k", "w_v", "w_o", "null_k", "null_v", "null_v_row", "ln_scale",
                                      "ln_bias")),
            4: (l2_depool, "l2d", ("w_in", "b_in", "g_res", "g_init", "token", "number", "decay")),
            6: (l3_attention, "l3a", ("w_qkv", "w_proj", "b_proj", "heads")),
            0: (l0_attention, "l0a", ("w_q", "w_k", "w_v", "w_o", "b_q", "b_k", "b_v", "b_o", "heads")),
        }
        ready = {p: tensors(p, cfg.tag, names) for p, (cfg, names) in plan.items()}
        ready.update({p: tensors(p, tag, names) for p, (_, tag, names) in attention.items()})
        opening(core, dram["x"], loads)
        last = phases[-1]
        for p in sorted(int(c) for c in phases):
            got, held = ready[p]
            to = out if str(p) == last else None
            if p in plan:
                experts_phase(core, plan[p][0], held, [consts, got], to)
            else:
                attention[p][0](core, held, [consts, got], to)


def laid_out(inputs):
    import numpy as np

    a = {k: np.asarray(v) for k, v in inputs.items()}
    c = np.ascontiguousarray
    bf16 = np.dtype("bfloat16")
    out = {"x": c(a["x"].reshape(B * S, D)), "ident": np.eye(P, dtype=np.float32)}

    def everywhere(v):
        return c(np.broadcast_to(v, (P, GT, NE)))

    out["falling"] = everywhere(np.arange(NE, 0, -1, dtype=np.float32))

    ctx = a["ctx_2048"].reshape(TILES, P, 2, P)
    out["ctx_t"] = c(ctx.transpose(3, 0, 2, 1))
    out["mask"] = c(a["mask_BxS2_fk1"])

    def halves(w):
        return c(w.reshape(-1, P, w.shape[1]).transpose(1, 0, 2))

    def column(v):
        return c(v.reshape(-1, 1))

    w_src = a["L0_xattn_W_src"].T
    out["l0a_w_q"] = c(a["L0_xattn_W_tgt"].T)
    out["l0a_w_k"] = halves(w_src[:, :D])
    out["l0a_w_v"] = halves(w_src[:, D:])
    out["l0a_w_o"] = halves(a["L0_xattn_W_out"].T)
    out["l0a_b_q"] = column(a["L0_xattn_b_tgt"])
    out["l0a_b_k"] = column(a["L0_xattn_b_src"][:D])
    out["l0a_b_v"] = column(a["L0_xattn_b_src"][D:])
    out["l0a_b_o"] = c(a["L0_xattn_b_out"].reshape(1, D))
    out["l0a_heads"] = np.repeat(np.eye(H0, dtype=np.float32), HD0, axis=0)

    w_kv = a["L1_xattn_Wkv"]
    w_v = w_kv[:, H1 * HD1:].reshape(CTX, PAIRS1, 2, HD1).transpose(0, 2, 1, 3).reshape(CTX, -1)
    out["l1a_w_q"] = c(a["L1_xattn_Wq"])
    out["l1a_w_k"] = halves(w_kv[:, :H1 * HD1])
    out["l1a_w_v"] = halves(w_v)
    out["l1a_w_o"] = halves(a["L1_xattn_Wout"])
    null = a["L1_xattn_null_kv"]
    out["l1a_null_k"] = column(np.concatenate([null[0], null[0]]))
    out["l1a_null_v"] = column(np.concatenate([null[1], null[1]]))
    out["l1a_null_v_row"] = c(np.broadcast_to(null[1], (P, HD1)))
    out["l1a_ln_scale"] = c(np.broadcast_to(a["L1_xattn_ln_scale"], (P, D)))
    out["l1a_ln_bias"] = c(np.broadcast_to(a["L1_xattn_ln_bias"], (P, D)))

    out["ctx_tok"] = c(a["ctx_2048"].reshape(B * S, CTX))
    out["lens"] = c(a["mask_BxS2_if0"].astype(np.int32, copy=False))
    out["l2d_w_in"] = c(a["L2_xattn_W_in"].T)
    out["l2d_b_in"] = column(a["L2_xattn_b_in"])
    out["l2d_g_res"] = column(a["L2_xattn_g_res"])
    out["l2d_g_init"] = c(np.broadcast_to(a["L2_xattn_g_init"][:D], (P, D)))
    out["l2d_token"] = c(np.broadcast_to(np.arange(S, dtype=np.float32), (B, S)))
    out["l2d_number"] = column(np.arange(S, dtype=np.float32))
    step = np.arange(S)[:, None] - np.arange(S)[None, :]
    decay = np.where(step >= 0, np.exp(LOG_P) * (-np.expm1(LOG_P)) ** np.maximum(step, 0), 0.0)
    out["l2d_decay"] = c(np.concatenate([decay, decay], 1).astype(np.float32))

    out["l3a_w_qkv"] = c(a["L3_xattn_w_qkv"].T)
    out["l3a_w_proj"] = c(a["L3_xattn_w_proj"].T)
    out["l3a_b_proj"] = c(a["L3_xattn_b_proj"].reshape(1, D))
    out["l3a_heads"] = np.repeat(np.eye(H3, dtype=np.float32), HD3, axis=0)

    def rows(w):
        return c(w.reshape(-1, P, D).transpose(1, 0, 2))

    def pick(cfg, width):
        m = np.zeros((P, cfg.spreads, P), bf16)
        for s in range(cfg.spreads):
            for i in range(P):
                unit = s * P * cfg.per + (i if cfg.per == 1 else 0)
                if unit < width * NE:
                    for r in PART_ROWS:
                        m[r + unit // width, s, i] = 1
                else:
                    m[SHARED_ROW, s, i] = 1
        return m

    def flat(w):
        return w.transpose(1, 0, 2).reshape(D, -1)

    out["l0f_w_in"] = c(flat(a["L0_ffn_w1"]))
    out["l0f_w_out"] = rows(a["L0_ffn_w2"])
    out["l0f_w_router"] = c(a["L0_ffn_w_router"])
    out["l0f_pick"] = pick(L0_FFN, 512)
    out["l0f_b_in"] = c(a["L0_ffn_b1"].reshape(-1, P).T)
    out["l0f_b_out"] = c(a["L0_ffn_b2"])
    out["l0f_b_router"] = everywhere(a["L0_ffn_b_router"])

    units = L1_FFN.chunks * P

    def padded(w, axis):
        pad = [(0, 0), (0, 0)]
        pad[axis] = (0, units - w.shape[axis])
        return c(np.pad(w, pad))

    out["l1f_w_in"] = padded(np.concatenate([flat(a["L1_ffn_W1"]), a["L1_ffn_Ws1"]], 1), 1)
    out["l1f_w_up"] = padded(np.concatenate([flat(a["L1_ffn_W2"]), a["L1_ffn_Ws2"]], 1), 1)
    out["l1f_w_out"] = rows(padded(np.concatenate([a["L1_ffn_W3"].reshape(-1, D), a["L1_ffn_Ws3"]], 0), 0))
    out["l1f_w_router"] = c(a["L1_ffn_Wg"])
    out["l1f_pick"] = pick(L1_FFN, 176)

    out["l2f_w_in"] = c(flat(a["L2_ffn_gate_w"]))
    out["l2f_w_up"] = c(flat(a["L2_ffn_up_w"]))
    out["l2f_w_out"] = rows(a["L2_ffn_down_w"])
    out["l2f_w_router"] = c(a["L2_ffn_router_w"].T)
    out["l2f_pick"] = pick(L2_FFN, 256)
    out["l2f_b_router"] = everywhere(a["L2_ffn_router_b"])

    out["l3f_w_in"] = c(flat(a["L3_ffn_W1"]))
    out["l3f_w_out"] = rows(a["L3_ffn_W2"])
    out["l3f_w_router"] = c(a["L3_ffn_Wr"])
    out["l3f_pick"] = pick(L3_FFN, 256)
    out["l3f_b_in"] = c(a["L3_ffn_b1"].reshape(-1, P).T)
    out["l3f_b_out"] = c(a["L3_ffn_b2"])
    out["l3f_b_router"] = everywhere(a["L3_ffn_br"])
    return out


def kernel(**inputs):
    import numpy as _np
    import concourse.bacc as _bacc
    from concourse import mybir as _mybir
    from concourse.bass_utils import run_bass_kernel_spmd as _run

    nc = _bacc.Bacc("TRN2", target_bir_lowering=False, num_devices=1)
    arrays = laid_out(inputs)
    dram = {n: nc.dram_tensor("in_" + n, a.shape, _mybir.dt.from_np(a.dtype), kind="ExternalInput").ap()
            for n, a in arrays.items()}
    out = nc.dram_tensor("out", (B * S, D), _mybir.dt.float32, kind="ExternalOutput").ap()
    program(nc, dram, out)
    r = _run(nc, [{"in_" + n: a for n, a in arrays.items()}], core_ids=[0])
    return r.results[0]["out"].reshape(B, S, D)
```

```python
from contextlib import ExitStack

import concourse.bass as bass
import numpy as np
from concourse import mybir

F32 = mybir.dt.float32
BF16 = mybir.dt.bfloat16
I32 = mybir.dt.int32
ALU = mybir.AluOpType
ACT = mybir.ActivationFunctionType
AX = mybir.AxisListType.X

P = 128
B, S, D, CTX = 64, 64, 128, 256
TILES = B * S // P
GT = 4
GROUPS = TILES // GT
GN = GT * P
NE = 8
LN_EPS = 1e-5
SLOTS = 4
HEADROOM = 16


class Signals:

    def __init__(self, nc, ctx, kind, by_engine):
        named = {name: ctx.enter_context(nc.semaphore(f"{kind}_{name}"))
                 for engine in by_engine for name in by_engine[engine]}
        self.done = named
        self.semaphores = {engine: [named[name] for name in by_engine[engine]] for engine in by_engine}
        self.values = {name: HEADROOM for name in named}

    def at(self):
        return dict(self.values)

    def phase_ends(self, counts, default):
        for name in self.values:
            self.values[name] += counts.get(name, default)


class Link:

    def __init__(self, eng, semaphore, value):
        self.eng, self.semaphore, self.value = eng, semaphore, value

    def __call__(self, instruction):
        self.value = self.value + 1
        instruction.then_inc(self.semaphore, 1)
        self.eng.wait_ge(self.semaphore, self.value)


class Core:

    def __init__(self, nc, ctx):
        self.nc, self.ctx = nc, ctx
        self.x = self.sb("x_tok", [P, TILES, D])
        self.mean_var = self.sb("mean_var", [P, TILES, 2])
        self.rstd = self.sb("rstd", [P, TILES])
        self.ident = self.sb("ident", [P, P])
        self.ctx_loads = 0

    def sb(self, name, shape, dt=F32):
        return self.ctx.enter_context(self.nc.sbuf_tensor(name, shape, dt))


class Experts:

    def __init__(self, tag, chunks, per, act, top, gated=False, b1=False, b2=False, br=False,
                 times_prob=False):
        self.shared = False
        self.tag, self.chunks, self.per, self.act, self.top = tag, chunks, per, act, top
        self.gated, self.b1, self.b2, self.br, self.times_prob = gated, b1, b2, br, times_prob
        self.spreads = chunks // per
        self.whole = top == 1 and not times_prob
        self.route_steps = (19 if top == 2 else 8 if times_prob else 6) + (1 if self.whole else 6)


PE_TURN_X, ACT_XT = 0, 2
PE_LOGITS, DVE_ROUTE_A = 3, 4
ACT_ROUTE, DVE_ROUTE_B = 6, 6
PE_TURN_W, DVE_WEIGHTS = 8, 9
PE_TURN_Y, DVE_UPDATE = 10, 12
UPDATE_STEPS = 3


def in_pairs(eng, body):
    body(0, 0)
    body(1, 1)
    with eng.Fori(1, GROUPS // 2 - 1) as pair:
        body(pair * 2, 0)
        body(pair * 2 + 1, 1)
    body(GROUPS - 2, 0)
    body(GROUPS - 1, 1)


def is_group(g, *which):
    return isinstance(g, int) and g in which


def experts_phase(core, cfg, io, loaded, out=None):
    nc = core.nc
    n, per = cfg.chunks, cfg.per
    done, at = core.expert_signals.done, core.expert_signals.at()

    with ExitStack() as local:
        def sb(name, shape, dt=F32):
            return local.enter_context(nc.sbuf_tensor(f"{cfg.tag}_{name}", shape, dt))

        def pb(name, shape):
            return local.enter_context(nc.psum_tensor(f"{cfg.tag}_{name}", shape, F32))

        xn = sb("xn", [P, 2, GT, D])
        xt = sb("xt", [P, 2, GN])
        act = sb("act", [P, 2, GN])
        prod = sb("prod", [P, GN])
        hid = sb("hid", [P, 2, GN])
        y_sb = sb("y_sb", [P, GN])
        logit = sb("logit", [P, GT, NE])
        others = sb("others", [P, GT, NE])
        hits = sb("hits", [P, GT, NE])
        first = sb("first", [P, GT, NE])
        second = sb("second", [P, GT, NE])
        best = sb("best", [P, GT])
        col = sb("col", [P, 4, GT])
        gap = sb("gap", [P, GT])
        fn = sb("fn", [P, GT, NE])
        w_tok = sb("w_tok", [P, GT, NE])
        w_t = sb("w_t", [NE, 2, GN])
        rest = sb("rest", [NE, 2, GN])
        w_parts = sb("w_parts", [P, 2, GN], BF16)
        std = sb("std", [P, TILES])
        stats = sb("stats", [P, GT, 6])
        mv = sb("mv", [P, GT, 2])

        g_ps = pb("g_ps", [P, 2, GN])
        u_ps = pb("u_ps", [P, 2, GN]) if cfg.gated else None
        w_ps = pb("w_ps", [P, 2, GN])
        y_ps = pb("y_ps", [P, GN])
        side = pb("side", [P, GN])

        block = local.enter_context(nc.Block())

        @block.tensor
        def _(pe):
            def turn_x(g, buf):
                pe.wait_ge(done["normed"], at["normed"] + g + 1)
                pe.wait_ge(done["x_updated"], at["x_updated"] + g - 2)
                for t in range(GT):
                    mm = nc.tensor.transpose(side[:, t * P:(t + 1) * P], xn[:, buf, t, :], core.ident[:, :])
                mm.then_inc(done["x_turned"], 1)

            def logits(g, buf):
                pe.wait_ge(done["xt_ready"], at["xt_ready"] + g + 1)
                for t in range(GT):
                    mm = nc.tensor.matmul(side[:, t * NE:(t + 1) * NE], xt[:, buf, t * P:(t + 1) * P],
                                          io["w_router"], start=True, stop=True)
                mm.then_inc(done["logits"], 1)

            def turn_w(g):
                pe.wait_ge(done["routed"], at["routed"] + g + 1)
                for t in range(GT):
                    mm = nc.tensor.transpose(side[0:NE, t * P:(t + 1) * P], w_tok[:, t, :], core.ident[:, :])
                mm.then_inc(done["w_turned"], 1)

            def turn_y(g):
                pe.wait_ge(done["y_out"], at["y_out"] + g + 1)
                pe.wait_ge(done["x_updated"], at["x_updated"] + g)
                ahead = min(g + 3, GROUPS) if isinstance(g, int) else g + 3
                pe.wait_ge(done["parts_ready"], at["parts_ready"] + ahead)
                for t in range(GT):
                    mm = nc.tensor.transpose(side[:, t * P:(t + 1) * P], y_sb[:, t * P:(t + 1) * P],
                                             core.ident[:, :])
                mm.then_inc(done["y_turned"], 1)

            def project(g, buf, c):
                k = g * n + c
                pe.wait_ge(done["activated"], at["activated"] + k - 1)
                nc.tensor.matmul(g_ps[:, c % 2, :], io["w_in"][:, c * P:(c + 1) * P], xt[:, buf, :],
                                 start=True, stop=True).then_inc(done["projected"], 1)
                if cfg.gated:
                    pe.wait_ge(done["gated"], at["gated"] + k - 1)
                    nc.tensor.matmul(u_ps[:, c % 2, :], io["w_up"][:, c * P:(c + 1) * P], xt[:, buf, :],
                                     start=True, stop=True).then_inc(done["up_projected"], 1)
                if c % per == 0:
                    s = c // per
                    if c == 0:
                        pe.wait_ge(done["parts_ready"], at["parts_ready"] + g + 1)
                    pe.wait_ge(done["weighted"], at["weighted"] + k - per)
                    nc.tensor.matmul(w_ps[:, s % 2, :], io["pick"][:, s, :], w_parts[:, buf, :],
                                     start=True, stop=True).then_inc(done["spread"], 1)

            def add(g, buf, c):
                if c == 0:
                    pe.wait_ge(done["y_out"], at["y_out"] + g)
                    if cfg.b2:
                        nc.tensor.matmul(y_ps[:, :], io["b_out"], w_t[:, buf, :], start=True, stop=False)
                pe.wait_ge(done["weighted"], at["weighted"] + g * n + c + 1)
                nc.tensor.matmul(y_ps[:, :], io["w_out"][:, c, :], hid[:, c % 2, :],
                                 start=(c == 0 and not cfg.b2), stop=(c == n - 1))\
                    .then_inc(done["summed"], 1)

            def body(g, buf):
                last = is_group(g, GROUPS - 1)
                for c in range(n):
                    if c + 2 < n:
                        project(g, buf, c + 2)
                    elif not last:
                        project(g + 1, 1 - buf, c + 2 - n)
                    add(g, buf, c)
                    if c == PE_TURN_X and not last:
                        turn_x(g + 1, 1 - buf)
                    if c == PE_LOGITS and not last:
                        logits(g + 1, 1 - buf)
                    if c == PE_TURN_W and not last:
                        turn_w(g + 1)
                    if c == PE_TURN_Y and not is_group(g, 0):
                        turn_y(g - 1)

            for s, v in loaded:
                pe.wait_ge(s, v)
            turn_x(0, 0)
            logits(0, 0)
            turn_w(0)
            project(0, 0, 0)
            project(0, 0, 1)
            in_pairs(pe, body)
            turn_y(GROUPS - 1)

        @block.scalar
        def _(act_eng):
            def xt_out(g, buf):
                act_eng.wait_ge(done["x_turned"], at["x_turned"] + g + 1)
                nc.scalar.activation(xt[:, buf, :], side[:, :], ACT.Copy).then_inc(done["xt_ready"], 1)

            def route_fn(g):
                if cfg.top == 2:
                    act_eng.wait_ge(done["gap_ready"], at["gap_ready"] + g + 1)
                    nc.scalar.activation(fn[:, :, 0], gap[:, :], ACT.Tanh, scale=0.5)\
                        .then_inc(done["fn_ready"], 1)
                elif cfg.times_prob:
                    act_eng.wait_ge(done["gap_ready"], at["gap_ready"] + g + 1)
                    nc.scalar.activation(fn[:, :, :], others[:, :, :], ACT.Exp).then_inc(done["fn_ready"], 1)

            def y_out(g):
                act_eng.wait_ge(done["summed"], at["summed"] + (g + 1) * n)
                act_eng.wait_ge(done["y_turned"], at["y_turned"] + g)
                nc.scalar.activation(y_sb[:, :], y_ps[:, :], ACT.Copy).then_inc(done["y_out"], 1)

            def activate(g, c):
                k = g * n + c
                act_eng.wait_ge(done["projected"], at["projected"] + k + 1)
                if cfg.gated:
                    act_eng.wait_ge(done["gated"], at["gated"] + k - 1)
                else:
                    act_eng.wait_ge(done["weighted"], at["weighted"] + k - 1)
                bias = io["b_in"][:, c:c + 1] if cfg.b1 else 0.0
                nc.scalar.activation(act[:, c % 2, :], g_ps[:, c % 2, :], cfg.act, bias=bias)\
                    .then_inc(done["activated"], 1)

            def body(g, buf):
                last = is_group(g, GROUPS - 1)
                for c in range(n):
                    activate(g, c)
                    if c == 1 and not is_group(g, 0):
                        y_out(g - 1)
                    if c == ACT_XT and not last:
                        xt_out(g + 1, 1 - buf)
                    if c == ACT_ROUTE and not last:
                        route_fn(g + 1)

            act_eng.wait_ge(done["std_in"], at["std_in"] + 1)
            nc.scalar.activation(std[:, :], std[:, :], ACT.Sqrt).then_inc(done["std"], 1)
            for s, v in loaded:
                act_eng.wait_ge(s, v)
            xt_out(0, 0)
            route_fn(0)
            in_pairs(act_eng, body)
            y_out(GROUPS - 1)

        @block.vector
        def _(dve):
            V = nc.vector

            def per_token(ap):
                return ap.unsqueeze(2).broadcast_to([P, GT, NE])

            def norm(g, buf):
                dve.wait_ge(done["x_turned"], at["x_turned"] + g - 1)
                for t in range(GT):
                    i = g * GT + t
                    ins = V.tensor_scalar(xn[:, buf, t, :], core.x[:, bass.ds(i, 1), :],
                                          core.mean_var[:, bass.ds(i, 1), 0], core.rstd[:, bass.ds(i, 1)],
                                          ALU.subtract, ALU.mult)
                ins.then_inc(done["normed"], 1)

            def one_hot(link, values, out):
                link(V.tensor_reduce(col[:, 0, :], values, AX, ALU.max))
                link(V.tensor_tensor(hits[:, :, :], values, per_token(col[:, 0, :]), ALU.is_equal))
                link(V.tensor_tensor(hits[:, :, :], hits[:, :, :], io["falling"], ALU.mult))
                link(V.tensor_reduce(col[:, 1, :], hits[:, :, :], AX, ALU.max))
                link(V.tensor_tensor(out, hits[:, :, :], per_token(col[:, 1, :]), ALU.is_equal))

            def route_a(g):
                dve.wait_ge(done["logits"], at["logits"] + g + 1)
                dve.wait_ge(done["w_turned"], at["w_turned"] + g)
                link = Link(dve, done["route_step"], at["route_step"] + g * cfg.route_steps)
                got = side[:, 0:GT * NE].rearrange("p (t e) -> p t e", e=NE)
                if cfg.br:
                    link(V.tensor_tensor(logit[:, :, :], got, io["b_router"], ALU.add))
                else:
                    link(V.tensor_copy(logit[:, :, :], got))
                one_hot(link, logit[:, :, :], first[:, :, :])
                if cfg.top == 2:
                    link(V.tensor_copy(best[:, :], col[:, 0, :]))
                    link(V.tensor_scalar(others[:, :, :], first[:, :, :], -1.0, 1.0, ALU.mult, ALU.add))
                    link(V.tensor_tensor(others[:, :, :], others[:, :, :], logit[:, :, :], ALU.mult))
                    link(V.scalar_tensor_tensor(others[:, :, :], first[:, :, :], -3e38, others[:, :, :],
                                                ALU.mult, ALU.add))
                    one_hot(link, others[:, :, :], second[:, :, :])
                    V.tensor_tensor(gap[:, :], best[:, :], col[:, 0, :], ALU.subtract)\
                        .then_inc(done["gap_ready"], 1)
                elif cfg.times_prob:
                    V.tensor_tensor(others[:, :, :], logit[:, :, :], per_token(col[:, 0, :]), ALU.subtract)\
                        .then_inc(done["gap_ready"], 1)
                else:
                    V.tensor_copy(w_tok[:, :, :], first[:, :, :]).then_inc(done["routed"], 1)
                return link

            def route_b(g, link):
                if cfg.top == 2:
                    dve.wait_ge(done["fn_ready"], at["fn_ready"] + g + 1)
                    link(V.tensor_scalar(col[:, 2, :], fn[:, :, 0], 0.5, 0.5, ALU.mult, ALU.add))
                    link(V.tensor_scalar(col[:, 3, :], fn[:, :, 0], -0.5, 0.5, ALU.mult, ALU.add))
                    link(V.tensor_tensor(first[:, :, :], first[:, :, :], per_token(col[:, 2, :]), ALU.mult))
                    link(V.tensor_tensor(second[:, :, :], second[:, :, :], per_token(col[:, 3, :]), ALU.mult))
                    V.tensor_tensor(w_tok[:, :, :], first[:, :, :], second[:, :, :], ALU.add)\
                        .then_inc(done["routed"], 1)
                elif cfg.times_prob:
                    dve.wait_ge(done["fn_ready"], at["fn_ready"] + g + 1)
                    link(V.tensor_reduce(col[:, 2, :], fn[:, :, :], AX, ALU.add))
                    link(V.reciprocal(col[:, 3, :], col[:, 2, :]))
                    V.tensor_tensor(w_tok[:, :, :], first[:, :, :], per_token(col[:, 3, :]), ALU.mult)\
                        .then_inc(done["routed"], 1)

            def weights_out(g, buf, link):
                dve.wait_ge(done["w_turned"], at["w_turned"] + g + 1)
                parts = w_parts[:, buf, :]
                link(V.tensor_copy(w_t[:, buf, :], side[0:NE, :]))
                if not cfg.whole:
                    link(V.tensor_copy(parts[0:NE, :], w_t[:, buf, :]))
                    link(V.tensor_tensor(rest[:, 0, :], w_t[:, buf, :], parts[0:NE, :], ALU.subtract))
                    link(V.tensor_copy(parts[32:32 + NE, :], rest[:, 0, :]))
                    link(V.tensor_copy(rest[:, 1, :], parts[32:32 + NE, :]))
                    link(V.tensor_tensor(rest[:, 1, :], rest[:, 0, :], rest[:, 1, :], ALU.subtract))
                    V.tensor_copy(parts[64:64 + NE, :], rest[:, 1, :]).then_inc(done["parts_ready"], 1)
                else:
                    V.tensor_copy(parts[0:NE, :], w_t[:, buf, :]).then_inc(done["parts_ready"], 1)

            def update_x(g):
                dve.wait_ge(done["y_turned"], at["y_turned"] + g + 1)
                link = Link(dve, done["update_step"], at["update_step"] + g * UPDATE_STEPS)
                x4 = core.x[:, bass.ds(g * GT, GT), :]
                link(V.tensor_tensor(x4, x4, side[:, :].rearrange("p (t d) -> p t d", d=D), ALU.add))
                dve.sem_inc(core.passed, 1)
                for t in range(GT):
                    ins = V.bn_stats(stats[:, t, :], core.x[:, bass.ds(g * GT + t, 1), :])
                link(ins)
                dve.sem_inc(core.passed, 1)
                for t in range(GT):
                    ins = V.bn_aggr(mv[:, t, :], stats[:, t, :])
                link(ins)
                V.tensor_copy(core.mean_var[:, bass.ds(g * GT, GT), :], mv[:, :, :])\
                    .then_inc(done["x_updated"], 1)

            def weight(g, c):
                k = g * n + c
                dve.wait_ge(done["activated"], at["activated"] + k + 1)
                got = act[:, c % 2, :]
                if cfg.gated:
                    dve.wait_ge(done["up_projected"], at["up_projected"] + k + 1)
                    dve.wait_ge(done["weighted"], at["weighted"] + k)
                    V.tensor_tensor(prod[:, :], got, u_ps[:, c % 2, :], ALU.mult).then_inc(done["gated"], 1)
                    dve.wait_ge(done["gated"], at["gated"] + k + 1)
                    got = prod[:, :]
                dve.wait_ge(done["spread"], at["spread"] + g * cfg.spreads + c // per + 1)
                dve.wait_ge(done["summed"], at["summed"] + k - 1)
                V.tensor_tensor(hid[:, c % 2, :], got, w_ps[:, (c // per) % 2, :], ALU.mult)\
                    .then_inc(done["weighted"], 1)

            def body(g, buf):
                last = is_group(g, GROUPS - 1)
                for c in range(n):
                    weight(g, c)
                    if c == DVE_ROUTE_A and not last:
                        link = route_a(g + 1)
                    if c == DVE_ROUTE_B and not last:
                        route_b(g + 1, link)
                    if c == DVE_WEIGHTS and not last:
                        weights_out(g + 1, 1 - buf, link)
                    if c == DVE_UPDATE:
                        if not is_group(g, 0):
                            update_x(g - 1)
                        if not is_group(g, GROUPS - 2, GROUPS - 1):
                            norm(g + 2, buf)

            V.tensor_scalar(std[:, :], core.mean_var[:, :, 1], LN_EPS, None, ALU.add).then_inc(done["std_in"], 1)
            V.memset(w_parts[:, :, :], 0.0).then_inc(done["cleared"], 1)
            dve.wait_ge(done["cleared"], at["cleared"] + 1)
            if cfg.shared:
                V.memset(w_parts[96:97, :, :], 1.0)
            dve.wait_ge(done["std"], at["std"] + 1)
            V.reciprocal(core.rstd[:, :], std[:, :]).then_inc(done["rstd"], 1)
            dve.wait_ge(done["rstd"], at["rstd"] + 1)
            for s, v in loaded:
                dve.wait_ge(s, v)
            norm(0, 0)
            norm(1, 1)
            link = route_a(0)
            route_b(0, link)
            weights_out(0, 0, link)
            in_pairs(dve, body)
            update_x(GROUPS - 1)

        @block.sync
        def _(sp):
            if out is None:
                return
            for g in range(GROUPS):
                sp.wait_ge(done["x_updated"], at["x_updated"] + g + 1)
                sp.dma_start(out[g * GN:(g + 1) * GN, :].rearrange("(t p) d -> p t d", p=P),
                             core.x[:, g * GT:(g + 1) * GT, :]).then_inc(core.out_done, 16)
            sp.wait_ge(core.out_done, 16 * GROUPS)

    counts = {"projected": GROUPS * n, "activated": GROUPS * n, "weighted": GROUPS * n, "summed": GROUPS * n,
              "spread": GROUPS * cfg.spreads, "route_step": GROUPS * cfg.route_steps,
              "update_step": GROUPS * UPDATE_STEPS, "std_in": 1, "std": 1, "rstd": 1, "cleared": 1,
              "up_projected": GROUPS * n * cfg.gated, "gated": GROUPS * n * cfg.gated,
              "gap_ready": GROUPS * (not cfg.whole), "fn_ready": GROUPS * (not cfg.whole)}
    core.expert_signals.phase_ends(counts, GROUPS)


EXPERT_SIGNALS = {
    "PE": ("x_turned", "logits", "w_turned", "y_turned", "projected", "up_projected", "spread", "summed"),
    "ACT": ("xt_ready", "fn_ready", "y_out", "activated", "std"),
    "DVE": ("normed", "routed", "parts_ready", "x_updated", "gated", "weighted", "std_in", "rstd",
            "cleared", "route_step", "update_step", "gap_ready"),
}


H0 = 8
HD0 = D // H0
PAIRS0 = H0 // 2
MASKED = -1e30


def over_slots(eng, step):
    for slot in range(SLOTS):
        step(slot, slot, 0)
    with eng.Fori(1, TILES // SLOTS - 1) as quad:
        for slot in range(SLOTS):
            step(quad * SLOTS + slot, slot, quad)
    for slot in range(SLOTS):
        step(TILES - SLOTS + slot, slot, TILES // SLOTS - 1)


def start_later_loads(core, sp, phase):
    for dst, dram, sem in core.later[phase]:
        sp.dma_start(dst, dram).then_inc(sem, 16)


def up_to_last(j):
    return min(j, TILES - 1) if isinstance(j, int) else j


def is_tile(j, *which):
    return isinstance(j, int) and j in which


def new_rstd(core, std, act_eng=None, dve=None):
    nc, done, at = core.nc, core.attention_signals.done, core.attention_signals.at()
    if act_eng is not None:
        act_eng.wait_ge(done["std_in"], at["std_in"] + 1)
        nc.scalar.activation(std[:, :], std[:, :], ACT.Sqrt).then_inc(done["std"], 1)
    if dve is not None:
        nc.vector.tensor_scalar(std[:, :], core.mean_var[:, :, 1], LN_EPS, None, ALU.add)\
            .then_inc(done["std_in"], 1)
        dve.wait_ge(done["std"], at["std"] + 1)
        nc.vector.reciprocal(core.rstd[:, :], std[:, :]).then_inc(done["rstd"], 1)
        dve.wait_ge(done["rstd"], at["rstd"] + 1)


def add_to_x(core, dve, link, j, result, stats, mv):
    V = core.nc.vector
    xj = core.x[:, bass.ds(j, 1), :]
    link(V.tensor_tensor(xj, xj, result, ALU.add))
    dve.sem_inc(core.passed, 1)
    link(V.bn_stats(stats[:, :], xj))
    dve.sem_inc(core.passed, 1)
    link(V.bn_aggr(mv[:, :], stats[:, :]))
    V.tensor_copy(core.mean_var[:, bass.ds(j, 1), :], mv[:, :].unsqueeze(1))\
        .then_inc(core.attention_signals.done["updated"], 1)


ADD_STEPS = 3
ATTENTION_SIGNALS = {
    "PE": ("x_turned", "projected", "v_projected", "scored", "p_turned", "pv_done", "o_turned", "final",
           "q_projected", "setup"),
    "ACT": ("xt_ready", "v_ready", "exped", "pt_ready", "ot_ready", "std", "qt_ready",
            "null_ready"),
    "DVE": ("normed", "proj_read", "s_read", "shifted", "o_ready", "updated", "std_in", "rstd", "cleared",
            "soft_step", "o_step", "add_step", "k_ready", "y_stats", "y_step"),
    "Pool": ("pool_setup", "pool_var", "y_rstd", "q_ready"),
}


def l0_attention(core, io, loaded, out=None):
    nc = core.nc
    done, at = core.attention_signals.done, core.attention_signals.at()
    scale = float(HD0) ** -0.5

    with ExitStack() as local:
        def sb(name, shape, dt=F32):
            return local.enter_context(nc.sbuf_tensor("l0a_" + name, shape, dt))

        def pb(name, shape):
            return local.enter_context(nc.psum_tensor("l0a_" + name, shape, F32))

        ctx_sb = sb("ctx", [P, SLOTS, 4, 2, S])
        mask_q = sb("mask_q", [P, B * S])
        mask_k = sb("mask_k", [P, TILES, S])
        xn = sb("xn", [P, SLOTS, D])
        xt = sb("xt", [P, SLOTS, P])
        qt = sb("qt", [P, P])
        k_diag = sb("k_diag", [P, 2, H0, S])
        v_diag = sb("v_diag", [P, 2, 2, PAIRS0, 2, HD0 + 1])
        s_sb = sb("s_sb", [P, H0, S])
        probs = sb("probs", [P, H0, S])
        top = sb("top", [P, H0])
        pt = sb("pt", [P, PAIRS0, P])
        o_sb = sb("o_sb", [P, H0, HD0])
        inv = sb("inv", [P, H0])
        ot = sb("ot", [P, P])
        ones = sb("ones", [1, P])
        std = sb("std", [P, TILES])
        stats = sb("stats", [P, 6])
        mv = sb("mv", [P, 2])

        x_ps = pb("x_ps", [P, 512])
        qk_ps = pb("qk_ps", [P, 512])
        v_ps = pb("v_ps", [P, 512])
        s_ps = pb("s_ps", [P, H0, S])
        pt_ps = pb("pt_ps", [P, PAIRS0, P])
        o_ps = pb("o_ps", [P, 512])
        ot_ps = pb("ot_ps", [P, 512])
        y_ps = pb("y_ps", [P, 512])
        o_view = o_ps[:, 0:H0 * (HD0 + 1)].rearrange("p (h d) -> p h d", d=HD0 + 1)
        loads_before = core.slot_loads
        masks_in = core.masks_in

        block = local.enter_context(nc.Block())

        @block.sync
        def _(sp):
            sp.dma_start(mask_q[:, :], core.dram["mask"].rearrange("b s -> (b s)").unsqueeze(0)
                         .broadcast_to([P, B * S])).then_inc(masks_in, 16)
            for b in range(2):
                keys = core.dram["mask"].rearrange("(j b) s -> b j s", b=2)[b:b + 1, :, :]
                sp.dma_start(mask_k[b * S:(b + 1) * S, :, :], keys.broadcast_to([S, TILES, S]))\
                    .then_inc(masks_in, 16)

            def step(j, slot, quad):
                sp.wait_ge(done["v_projected"], at["v_projected"] + j - 3)
                sp.sem_inc(core.passed, 1)
                src = core.dram["ctx_t"][:, bass.ds(j, 1), :, :].rearrange("p j h (b s) -> p (j h b) s", b=2)
                for copy in range(2):
                    sp.dma_start(ctx_sb[:, slot, :, copy, :], src).then_inc(core.slot_in[slot], 16)

            over_slots(sp, step)

        @block.tensor
        def _(pe):
            mmul = nc.tensor.matmul

            def context_here(slot, quad):
                pe.wait_ge(core.slot_in[slot], (quad * 2 + loads_before + 2) * 16)

            def turn_x(i, slot):
                pe.wait_ge(done["normed"], at["normed"] + i + 1)
                pe.wait_ge(done["xt_ready"], at["xt_ready"] + i)
                nc.tensor.transpose(x_ps[:, 0:P], xn[:, slot, :], core.ident[:, :]).then_inc(done["x_turned"], 1)

            def project_qk(i, slot, quad):
                pe.wait_ge(done["xt_ready"], at["xt_ready"] + i + 1)
                pe.wait_ge(done["proj_read"], at["proj_read"] + i)
                context_here(slot, quad)
                mmul(qk_ps[:, 0:P], io["w_q"], xt[:, slot, :], start=True, stop=True)
                for half in range(2):
                    mm = mmul(qk_ps[:, P:2 * P], io["w_k"][:, half, :], ctx_sb[:, slot, 2 * half:2 * half + 2, 0, :],
                              start=(half == 0), stop=(half == 1))
                mm.then_inc(done["projected"], 1)

            def project_v(i, slot):
                pe.wait_ge(done["v_ready"], at["v_ready"] + i)
                for b in range(2):
                    for half in range(2):
                        tok = ctx_sb[:, slot, 2 * half + b, :, :]
                        mm = mmul(v_ps[:, b * P:(b + 1) * P], tok, io["w_v"][:, half, :],
                                  start=(half == 0), stop=(half == 1))
                mm.then_inc(done["v_projected"], 1)

            def scores(j):
                pe.wait_ge(done["proj_read"], at["proj_read"] + j + 1)
                pe.wait_ge(done["s_read"], at["s_read"] + j)
                for b in range(2):
                    mm = mmul(s_ps[b * S:(b + 1) * S, :, :], qt[:, b * S:(b + 1) * S], k_diag[:, b, :, :],
                              start=True, stop=True)
                mm.then_inc(done["scored"], 1)

            def turn_p(j):
                pe.wait_ge(done["exped"], at["exped"] + j + 1)
                pe.wait_ge(done["pt_ready"], at["pt_ready"] + j)
                for c in range(PAIRS0):
                    mm = nc.tensor.transpose(pt_ps[:, c, :], probs[:, 2 * c:2 * c + 2, :], core.ident[:, :])
                mm.then_inc(done["p_turned"], 1)

            def weigh_v(j, slot):
                pe.wait_ge(done["pt_ready"], at["pt_ready"] + j + 1)
                pe.wait_ge(done["v_ready"], at["v_ready"] + j + 1)
                pe.wait_ge(done["o_ready"], at["o_ready"] + j)
                for c in range(PAIRS0):
                    for b in range(2):
                        mm = mmul(o_ps[b * S:(b + 1) * S, c * 2 * (HD0 + 1):(c + 1) * 2 * (HD0 + 1)],
                                  pt[:, c, b * S:(b + 1) * S], v_diag[:, slot % 2, b, c, :, :], start=True, stop=True)
                mm.then_inc(done["pv_done"], 1)

            def turn_o(j):
                pe.wait_ge(done["o_ready"], at["o_ready"] + j + 1)
                pe.wait_ge(done["ot_ready"], at["ot_ready"] + j)
                nc.tensor.transpose(ot_ps[:, 0:P], o_sb[:, :, :], core.ident[:, :]).then_inc(done["o_turned"], 1)

            def final(i, slot):
                pe.wait_ge(done["ot_ready"], at["ot_ready"] + i + 1)
                pe.wait_ge(done["add_step"], at["add_step"] + ADD_STEPS * (i - 1) + 1)
                mmul(y_ps[:, 0:D], xt[:, slot, :], io["w_o"][:, 0, :], start=True, stop=False)
                mmul(y_ps[:, 0:D], ot[:, :], io["w_o"][:, 1, :], start=False, stop=False)
                mmul(y_ps[:, 0:D], ones[:, :], io["b_o"], start=False, stop=True).then_inc(done["final"], 1)

            def step(j, slot, quad):
                to_start = is_tile(j, -2, -1)
                if not is_tile(j, -2, TILES - 1):
                    scores(j + 1)
                    project_v(j + 1, (slot + 1) % SLOTS)
                if not (to_start or is_tile(j, 0)):
                    turn_o(j - 1)
                if not to_start:
                    turn_p(j)
                if not is_tile(j, TILES - 2, TILES - 1):
                    project_qk(j + 2, (slot + 2) % SLOTS, quad + (slot + 2) // SLOTS)
                if not (to_start or is_tile(j, 0)):
                    final(j - 1, (slot - 1) % SLOTS)
                if not is_tile(j, TILES - 3, TILES - 2, TILES - 1):
                    turn_x(j + 3, (slot + 3) % SLOTS)
                if not to_start:
                    weigh_v(j, slot)

            for s, v in loaded:
                pe.wait_ge(s, v)
            turn_x(0, 0)
            step(-2, 2, -1)
            step(-1, 3, -1)
            over_slots(pe, step)
            turn_o(TILES - 1)
            final(TILES - 1, SLOTS - 1)

        @block.scalar
        def _(act_eng):
            A = nc.scalar

            def xt_out(j, slot):
                act_eng.wait_ge(done["x_turned"], at["x_turned"] + j + 1)
                act_eng.wait_ge(done["final"], at["final"] + j - 3)
                A.activation(xt[:, slot, :], x_ps[:, 0:P], ACT.Copy).then_inc(done["xt_ready"], 1)

            def v_out(j, buf):
                act_eng.wait_ge(done["v_projected"], at["v_projected"] + j + 1)
                act_eng.wait_ge(done["pv_done"], at["pv_done"] + j - 1)
                for b in range(2):
                    for h in range(2):
                        rows = slice(h * S, (h + 1) * S)
                        src = v_ps[rows, b * P:(b + 1) * P].rearrange("p (c h d) -> p c h d", h=2, d=HD0)
                        ins = A.activation(v_diag[rows, buf, b, :, h, 0:HD0], src[:, :, h, :], ACT.Copy)
                ins.then_inc(done["v_ready"], 1)

            def pt_out(j):
                act_eng.wait_ge(done["p_turned"], at["p_turned"] + j + 1)
                act_eng.wait_ge(done["pv_done"], at["pv_done"] + j)
                A.activation(pt[:, :, :], pt_ps[:, :, :], ACT.Copy).then_inc(done["pt_ready"], 1)

            def ot_out(j):
                act_eng.wait_ge(done["o_turned"], at["o_turned"] + j + 1)
                act_eng.wait_ge(done["final"], at["final"] + j)
                A.activation(ot[:, :], ot_ps[:, 0:P], ACT.Identity, bias=io["b_v"]).then_inc(done["ot_ready"], 1)

            def exps(j):
                act_eng.wait_ge(done["shifted"], at["shifted"] + j + 1)
                act_eng.wait_ge(done["p_turned"], at["p_turned"] + j)
                A.activation(probs[:, :, :], s_sb[:, :, :], ACT.Exp, scale=scale).then_inc(done["exped"], 1)

            def step(j, slot, quad):
                to_start = is_tile(j, -2, -1)
                if not is_tile(j, -2, TILES - 1):
                    v_out(j + 1, (slot + 1) % 2)
                if not (to_start or is_tile(j, 0)):
                    ot_out(j - 1)
                if not to_start:
                    pt_out(j)
                if not is_tile(j, -2, TILES - 1):
                    exps(j + 1)
                if not is_tile(j, TILES - 3, TILES - 2, TILES - 1):
                    xt_out(j + 3, (slot + 3) % SLOTS)

            new_rstd(core, std, act_eng=act_eng)
            for s, v in loaded:
                act_eng.wait_ge(s, v)
            act_eng.wait_ge(done["cleared"], at["cleared"] + 3)
            xt_out(0, 0)
            step(-2, 2, -1)
            step(-1, 3, -1)
            over_slots(act_eng, step)
            ot_out(TILES - 1)

        @block.vector
        def _(dve):
            V = nc.vector

            def norm(j, slot):
                dve.wait_ge(done["x_turned"], at["x_turned"] + j - 3)
                V.tensor_scalar(xn[:, slot, :], core.x[:, bass.ds(j, 1), :], core.mean_var[:, bass.ds(j, 1), 0],
                                core.rstd[:, bass.ds(j, 1)], ALU.subtract, ALU.mult).then_inc(done["normed"], 1)

            def qk_out(j):
                dve.wait_ge(done["projected"], at["projected"] + j + 1)
                dve.wait_ge(done["scored"], at["scored"] + j)
                V.scalar_tensor_tensor(qt[:, :], qk_ps[:, 0:P], io["b_q"], mask_q[:, bass.ds(j * P, P)],
                                       ALU.add, ALU.mult)
                head = io["heads"].unsqueeze(2).broadcast_to([P, H0, S])
                for b in range(2):
                    keys = qk_ps[:, P + b * S:P + (b + 1) * S].unsqueeze(1).broadcast_to([P, H0, S])
                    ins = V.scalar_tensor_tensor(k_diag[:, b, :, :], keys, io["b_k"], head, ALU.add, ALU.mult)
                ins.then_inc(done["proj_read"], 1)

            def soften(j):
                dve.wait_ge(done["scored"], at["scored"] + j + 1)
                dve.wait_ge(done["exped"], at["exped"] + j)
                link = Link(dve, done["soft_step"], at["soft_step"] + j)
                neg = mask_k[:, bass.ds(j, 1), :].broadcast_to([P, H0, S])
                V.tensor_tensor(s_sb[:, :, :], s_ps[:, :, :], neg, ALU.add).then_inc(done["s_read"], 1)
                dve.wait_ge(done["s_read"], at["s_read"] + j + 1)
                link(V.tensor_reduce(top[:, :], s_sb[:, :, :], AX, ALU.max))
                V.tensor_tensor(s_sb[:, :, :], s_sb[:, :, :], top[:, :].unsqueeze(2).broadcast_to([P, H0, S]),
                                ALU.subtract).then_inc(done["shifted"], 1)

            def scale_o(j):
                dve.wait_ge(done["pv_done"], at["pv_done"] + j + 1)
                dve.wait_ge(done["o_turned"], at["o_turned"] + j)
                link = Link(dve, done["o_step"], at["o_step"] + j)
                link(V.reciprocal(inv[:, :], o_view[:, :, HD0]))
                V.tensor_tensor(o_sb[:, :, :], o_view[:, :, 0:HD0],
                                inv[:, :].unsqueeze(2).broadcast_to([P, H0, HD0]), ALU.mult)\
                    .then_inc(done["o_ready"], 1)

            def update(j):
                dve.wait_ge(done["final"], at["final"] + j + 1)
                add_to_x(core, dve, Link(dve, done["add_step"], at["add_step"] + j * ADD_STEPS), j, y_ps[:, 0:D], stats, mv)

            def step(j, slot, quad):
                to_start = is_tile(j, -2, -1)
                if not is_tile(j, -2, TILES - 1):
                    soften(j + 1)
                if not is_tile(j, TILES - 2, TILES - 1):
                    qk_out(j + 2)
                if not (to_start or is_tile(j, 0)):
                    update(j - 1)
                if not to_start:
                    scale_o(j)
                if not (to_start or is_tile(j, *range(TILES - SLOTS, TILES))):
                    norm(j + 4, slot)

            V.memset(v_diag[:, :, :, :, :, :], 0.0).then_inc(done["cleared"], 1)
            V.memset(ones[:, :], 1.0)
            dve.wait_ge(done["cleared"], at["cleared"] + 1)
            for h in range(2):
                ins = V.memset(v_diag[h * S:(h + 1) * S, :, :, :, h, HD0], 1.0)
                ins.then_inc(done["cleared"], 1)
            new_rstd(core, std, dve=dve)
            for s, v in loaded:
                dve.wait_ge(s, v)
            dve.wait_ge(masks_in, 48)
            V.tensor_scalar(mask_k[:, :, :], mask_k[:, :, :], 0.0, MASKED, ALU.is_equal, ALU.mult)\
                .then_inc(done["cleared"], 1)
            for i in range(SLOTS):
                norm(i, i)
            dve.wait_ge(done["cleared"], at["cleared"] + 4)
            step(-2, 2, -1)
            step(-1, 3, -1)
            over_slots(dve, step)
            update(TILES - 1)

    core.attention_signals.phase_ends({
        **{name: TILES for name in ("x_turned", "projected", "v_projected", "scored", "p_turned", "pv_done",
                                    "o_turned", "final", "xt_ready", "v_ready", "exped", "pt_ready", "ot_ready",
                                    "normed", "proj_read", "s_read", "shifted", "o_ready", "updated",
                                    "soft_step", "o_step")},
        "std_in": 1, "std": 1, "rstd": 1, "cleared": 4, "add_step": TILES * ADD_STEPS}, 0)
    core.slot_loads += 2 * TILES // SLOTS
    if out is not None:
        store_x(core, out)


def store_x(core, out):
    nc = core.nc
    with nc.Block() as block:
        @block.sync
        def _(sp):
            sp.dma_start(out.rearrange("(t p) d -> p t d", p=P), core.x[:, :, :]).then_inc(core.out_done, 16)
            sp.wait_ge(core.out_done, 16)


H1 = 16
HD1 = 64
PAIRS1 = H1 // 2
HALF = PAIRS1 // 2
OUT_PIECES = ((0, 3), (3, 3), (6, 2))
L1_EPS = 1e-6
Y_STEPS = 2 + ADD_STEPS


def l1_attention(core, io, loaded, out=None):
    nc = core.nc
    done, at = core.attention_signals.done, core.attention_signals.at()
    scale = float(HD1) ** -0.5

    with ExitStack() as local:
        def sb(name, shape, dt=F32):
            return local.enter_context(nc.sbuf_tensor("l1a_" + name, shape, dt))

        ctx_sb = sb("ctx", [P, SLOTS, 2, P])
        xn = sb("xn", [P, SLOTS, D])
        xt = sb("xt", [P, 2, P])
        qt = sb("qt", [P, PAIRS1, P])
        k_diag = sb("k_diag", [P, PAIRS1, 2, 2, S])
        v_sb = sb("v_sb", [P, 2, 2, PAIRS1, HD1 + 1])
        v_diag = sb("v_diag", [P, 2, 2, 2, PAIRS1, HD1 + 1])
        s_sb = sb("s_sb", [P, H1, S])
        probs = sb("probs", [P, H1, S])
        top = sb("top", [P, H1])
        null = sb("null", [P, 2, H1])
        pt = sb("pt", [P, PAIRS1, P])
        den = sb("den", [P, H1])
        inv = sb("inv", [P, H1])
        o_sb = sb("o_sb", [P, H1, HD1])
        ot = sb("ot", [P, PAIRS1, P])
        ones = sb("ones", [1, P])
        row = sb("row", [1, D])
        std = sb("std", [P, TILES])
        stats = sb("stats", [P, 6])
        mv = sb("mv", [P, 2])
        y_stats = sb("y_stats", [P, 6])
        y_mv = sb("y_mv", [P, 2])
        y_var = sb("y_var", [P, 1])
        y_rstd = sb("y_rstd", [P, 1])
        minus_half = sb("minus_half", [P, 1])
        eps = sb("eps", [P, 1])
        y_sb = sb("y_sb", [P, 1, D])
        act_ps = local.enter_context(nc.psum_tensor("l1a_act_ps", [P, 2, 512], F32))
        dve_ps = local.enter_context(nc.psum_tensor("l1a_dve_ps", [P, 4, 512], F32))
        s_ps = local.enter_context(nc.psum_tensor("l1a_s_ps", [P, 2, 512], F32))
        loads_before = core.slot_loads
        v_in = core.v_in

        def out_piece(i):
            first, n = OUT_PIECES[i]
            view = dve_ps[:, i + 1, 0:n * 2 * (HD1 + 1)].rearrange("p (h d) -> p h d", d=HD1 + 1)
            return view, 2 * first, 2 * n

        block = local.enter_context(nc.Block())

        @block.sync
        def _(sp):
            start_later_loads(core, sp, 2)

            def load(i, slot):
                sp.wait_ge(done["v_projected"], at["v_projected"] + 2 * (i - 3))
                sp.sem_inc(core.passed, 1)
                sp.dma_start(ctx_sb[:, slot, :, :], core.dram["ctx_t"][:, bass.ds(i, 1), :, :]
                             .rearrange("p j h t -> p (j h) t")).then_inc(core.slot_in[slot], 16)

            def spread(i, buf):
                sp.wait_ge(done["v_ready"], at["v_ready"] + 2 * (i + 1))
                sp.sem_inc(core.passed, 1)
                sp.wait_ge(done["pv_done"], at["pv_done"] + i - 1)
                for b in range(2):
                    for h in range(2):
                        sp.dma_start(v_diag[h * S:(h + 1) * S, buf, b, h, :, :],
                                     v_sb[b * S:(b + 1) * S, buf, h, :, :]).then_inc(v_in[buf], 16)

            def step(j, slot, quad):
                if not is_tile(j, TILES - 1):
                    spread(j + 1, (slot + 1) % 2)
                if not is_tile(j, *range(TILES - SLOTS, TILES)):
                    load(j + SLOTS, slot)

            for i in range(SLOTS):
                load(i, i)
            sp.wait_ge(done["cleared"], at["cleared"] + 3)
            spread(0, 0)
            over_slots(sp, step)

        @block.tensor
        def _(pe):
            mmul = nc.tensor.matmul

            def turn_x(i, slot):
                pe.wait_ge(done["normed"], at["normed"] + i + 1)
                pe.wait_ge(done["qt_ready"], at["qt_ready"] + 2 * (i - 1))
                pe.wait_ge(done["xt_ready"], at["xt_ready"] + i)
                nc.tensor.transpose(act_ps[:, 0, 0:P], xn[:, slot, :], core.ident[:, :])\
                    .then_inc(done["x_turned"], 1)

            def project_q(i, slot, p):
                pe.wait_ge(done["xt_ready"], at["xt_ready"] + i + 1)
                pe.wait_ge(done["ot_ready"], at["ot_ready"] + 2 * (i - 3) + p + 1)
                if is_tile(i, 0, 1):
                    pe.wait_ge(done["qt_ready"], at["qt_ready"] + 2 * (i - 1) + p + 1)
                    pe.wait_ge(done["xt_ready"], at["xt_ready"] + i + 2)
                if is_tile(i, 2):
                    pe.wait_ge(done["pt_ready"], at["pt_ready"] + p + 1)
                for c in range(HALF):
                    cols = slice((p * HALF + c) * P, (p * HALF + c + 1) * P)
                    mm = mmul(act_ps[:, 1 - p, c * P:(c + 1) * P], io["w_q"][:, cols], xt[:, slot % 2, :],
                              start=True, stop=True)
                mm.then_inc(done["q_projected"], 1)

            def project_k(i, slot, quad, p):
                if p == 0:
                    pe.wait_ge(core.slot_in[slot], (quad + loads_before + 1) * 16)
                pe.wait_ge(done["o_ready"], at["o_ready"] + 3 * (i - 3) + 2 + p)
                for c in range(HALF):
                    col = (p * HALF + c) * P
                    for half in range(2):
                        mm = mmul(dve_ps[:, 2 + p, c * P:(c + 1) * P], io["w_k"][:, half, col:col + P],
                                  ctx_sb[:, slot, half, :], start=(half == 0), stop=(half == 1))
                mm.then_inc(done["projected"], 1)

            def project_v(i, slot, p):
                if p == 0:
                    pe.wait_ge(done["add_step"], at["add_step"] + Y_STEPS * (i - 3) + 1)
                else:
                    pe.wait_ge(done["o_ready"], at["o_ready"] + 3 * (i - 2) + 1)
                if is_tile(i, 1, 2):
                    pe.wait_ge(done["v_ready"], at["v_ready"] + 2 * (i - 1) + p + 1)
                for half in range(2):
                    mm = mmul(dve_ps[:, p, :], ctx_sb[:, slot, half, :], io["w_v"][:, half, p * 512:(p + 1) * 512],
                              start=(half == 0), stop=(half == 1))
                mm.then_inc(done["v_projected"], 1)

            def scores(i, p):
                pe.wait_ge(done["qt_ready"], at["qt_ready"] + 2 * i + p + 1)
                pe.wait_ge(done["k_ready"], at["k_ready"] + 2 * i + p + 1)
                pe.wait_ge(done["shifted"], at["shifted"] + 2 * (i - 1) + p + 1)
                for c in range(HALF):
                    for b in range(2):
                        mm = mmul(s_ps[b * S:(b + 1) * S, p, c * P:(c + 1) * P],
                                  qt[:, p * HALF + c, b * S:(b + 1) * S], k_diag[:, p * HALF + c, b, :, :],
                                  start=True, stop=True)
                mm.then_inc(done["scored"], 1)

            def turn_p(j, p):
                pe.wait_ge(done["exped"], at["exped"] + 2 * j + p + 1)
                if p == 0 or is_tile(j, TILES - 3, TILES - 2, TILES - 1):
                    pe.wait_ge(done["qt_ready"], at["qt_ready"] + 2 * up_to_last(j + 1) + p + 1)
                if p == 1:
                    pe.wait_ge(done["xt_ready"], at["xt_ready"] + up_to_last(j + 3) + 1)
                if is_tile(j, TILES - 1):
                    pe.wait_ge(done["ot_ready"], at["ot_ready"] + 2 * (j - 2) + p + 1)
                for c in range(HALF):
                    h = 2 * (p * HALF + c)
                    mm = nc.tensor.transpose(act_ps[:, 1 - p, c * P:(c + 1) * P], probs[:, h:h + 2, :],
                                             core.ident[:, :])
                mm.then_inc(done["p_turned"], 1)

            def turn_o(i, p):
                pe.wait_ge(done["o_ready"], at["o_ready"] + 3 * i + 2 + p)
                pe.wait_ge(done["pt_ready"], at["pt_ready"] + 2 * up_to_last(i + 1) + p + 1)
                if is_tile(i, TILES - 1):
                    pe.wait_ge(done["ot_ready"], at["ot_ready"] + 2 * (i - 1) + p + 1)
                for c in range(HALF):
                    h = 2 * (p * HALF + c)
                    mm = nc.tensor.transpose(act_ps[:, 1 - p, c * P:(c + 1) * P], o_sb[:, h:h + 2, :],
                                             core.ident[:, :])
                mm.then_inc(done["o_turned"], 1)

            def final(i):
                pe.wait_ge(done["v_ready"], at["v_ready"] + 2 * up_to_last(i + 2) + 1)
                if is_tile(i, TILES - 2, TILES - 1):
                    pe.wait_ge(done["updated"], at["updated"] + i)
                y = dve_ps[:, 0, 0:D]
                for c in range(PAIRS1):
                    if c % HALF == 0:
                        pe.wait_ge(done["ot_ready"], at["ot_ready"] + 2 * i + c // HALF + 1)
                    mmul(y, ot[:, c, :], io["w_o"][:, c, :], start=(c == 0), stop=False)
                mmul(y, ones[:, :], row[:, :], start=False, stop=True).then_inc(done["final"], 1)

            def weigh_v(j, slot, quad):
                buf = slot % 2
                pe.wait_ge(done["pt_ready"], at["pt_ready"] + 2 * (j + 1))
                pe.wait_ge(v_in[buf], (quad * 2 + slot // 2 + 1) * 64)
                pe.wait_ge(done["v_ready"], at["v_ready"] + 2 * (up_to_last(j + 1) + 1))
                pe.wait_ge(done["o_ready"], at["o_ready"] + 3 * j)
                for i, (first, n) in enumerate(OUT_PIECES):
                    if i > 0:
                        pe.wait_ge(done["k_ready"], at["k_ready"] + 2 * up_to_last(j + 2) + i)
                    for c in range(n):
                        for b in range(2):
                            w = 2 * (HD1 + 1)
                            mm = mmul(dve_ps[b * S:(b + 1) * S, i + 1, c * w:(c + 1) * w],
                                      pt[:, first + c, b * S:(b + 1) * S],
                                      v_diag[:, buf, b, :, first + c, :], start=True, stop=True)
                mm.then_inc(done["pv_done"], 1)

            def step(j, slot, quad):
                to_start = is_tile(j, -2, -1)
                v_next = is_tile(j, -2, TILES - 1)
                qk_next = is_tile(j, TILES - 2, TILES - 1)
                if not v_next:
                    scores(j + 1, 0)
                    scores(j + 1, 1)
                if not is_tile(j, TILES - 3, TILES - 2, TILES - 1):
                    turn_x(j + 3, (slot + 3) % SLOTS)
                for p in range(2):
                    if not to_start:
                        turn_p(j, p)
                    if not v_next:
                        project_v(j + 1, (slot + 1) % SLOTS, p)
                for p in range(2):
                    if not (to_start or is_tile(j, 0)):
                        turn_o(j - 1, p)
                    if not qk_next:
                        project_k(j + 2, (slot + 2) % SLOTS, quad + (slot + 2) // SLOTS, p)
                if not qk_next:
                    project_q(j + 2, (slot + 2) % SLOTS, 0)
                if not (to_start or is_tile(j, 0)):
                    final(j - 1)
                if not qk_next:
                    project_q(j + 2, (slot + 2) % SLOTS, 1)
                if not to_start:
                    weigh_v(j, slot, quad)

            for s, v in loaded:
                pe.wait_ge(s, v)
            for c in range(PAIRS1):
                mm = mmul(dve_ps[0:1, 0, 0:D], io["null_v"], io["w_o"][:, c, :], start=(c == 0),
                          stop=(c == PAIRS1 - 1))
            mm.then_inc(done["setup"], 1)
            pe.wait_ge(done["cleared"], at["cleared"] + 4)
            turn_x(0, 0)
            step(-2, 2, -1)
            step(-1, 3, -1)
            over_slots(pe, step)
            turn_o(TILES - 1, 0)
            turn_o(TILES - 1, 1)
            final(TILES - 1)

        @block.scalar
        def _(act_eng):
            A = nc.scalar

            def halves_of(p):
                return slice(p * HALF, (p + 1) * HALF), slice(p * H1 // 2, (p + 1) * H1 // 2)

            def xt_out(i, slot):
                act_eng.wait_ge(done["x_turned"], at["x_turned"] + i + 1)
                act_eng.wait_ge(done["q_projected"], at["q_projected"] + 2 * (i - 1))
                A.activation(xt[:, slot % 2, :], act_ps[:, 0, 0:P], ACT.Copy).then_inc(done["xt_ready"], 1)

            def pt_out(j, p):
                act_eng.wait_ge(done["p_turned"], at["p_turned"] + 2 * j + p + 1)
                act_eng.wait_ge(done["pv_done"], at["pv_done"] + j)
                A.activation(pt[:, halves_of(p)[0], :], act_ps[:, 1 - p, :], ACT.Copy).then_inc(done["pt_ready"], 1)

            def ot_out(i, p):
                act_eng.wait_ge(done["o_turned"], at["o_turned"] + 2 * i + p + 1)
                act_eng.wait_ge(done["final"], at["final"] + i)
                A.activation(ot[:, halves_of(p)[0], :], act_ps[:, 1 - p, :], ACT.Copy).then_inc(done["ot_ready"], 1)

            def qt_out(i, p):
                act_eng.wait_ge(done["q_projected"], at["q_projected"] + 2 * i + p + 1)
                act_eng.wait_ge(done["scored"], at["scored"] + 2 * i)
                A.activation(qt[:, halves_of(p)[0], :], act_ps[:, 1 - p, :], ACT.Copy).then_inc(done["qt_ready"], 1)

            def exps(i, slot, p):
                heads = halves_of(p)[1]
                act_eng.wait_ge(done["shifted"], at["shifted"] + 2 * i + p + 1)
                act_eng.wait_ge(done["p_turned"], at["p_turned"] + 2 * (i - 1) + p + 1)
                A.activation(probs[:, heads, :], s_sb[:, heads, :], ACT.Exp, scale=scale).then_inc(done["exped"], 1)
                if p == 1:
                    act_eng.wait_ge(done["o_ready"], at["o_ready"] + 3 * (i - 1))
                    A.activation(null[:, slot % 2, :], top[:, :], ACT.Exp, scale=-scale).then_inc(done["null_ready"], 1)

            def step(j, slot, quad):
                to_start = is_tile(j, -2, -1)
                if not is_tile(j, TILES - 3, TILES - 2, TILES - 1):
                    xt_out(j + 3, (slot + 3) % SLOTS)
                if not to_start:
                    pt_out(j, 0)
                    pt_out(j, 1)
                for p in range(2):
                    if not (to_start or is_tile(j, 0)):
                        ot_out(j - 1, p)
                    if not is_tile(j, -2, TILES - 1):
                        exps(j + 1, (slot + 1) % SLOTS, p)
                if not is_tile(j, TILES - 2, TILES - 1):
                    qt_out(j + 2, 0)
                    qt_out(j + 2, 1)

            new_rstd(core, std, act_eng=act_eng)
            xt_out(0, 0)
            step(-2, 2, -1)
            step(-1, 3, -1)
            over_slots(act_eng, step)
            ot_out(TILES - 1, 0)
            ot_out(TILES - 1, 1)

        @block.gpsimd
        def _(pool):
            G = nc.gpsimd
            G.memset(minus_half[:, :], -0.5).then_inc(done["pool_setup"], 1)
            G.memset(eps[:, :], L1_EPS).then_inc(done["pool_setup"], 1)
            pool.wait_ge(done["pool_setup"], at["pool_setup"] + 2)

            def step(j, slot, quad):
                pool.wait_ge(done["y_stats"], at["y_stats"] + j + 1)
                pool.wait_ge(done["updated"], at["updated"] + j)
                G.tensor_tensor(y_var[:, :], y_mv[:, 1:2], eps[:, :], ALU.add).then_inc(done["pool_var"], 1)
                pool.wait_ge(done["pool_var"], at["pool_var"] + j + 1)
                G.tensor_tensor(y_rstd[:, :], y_var[:, :], minus_half[:, :], ALU.pow).then_inc(done["y_rstd"], 1)

            over_slots(pool, step)

        @block.vector
        def _(dve):
            V = nc.vector

            def norm(i, slot):
                dve.wait_ge(done["x_turned"], at["x_turned"] + i - 3)
                V.tensor_scalar(xn[:, slot, :], core.x[:, bass.ds(i, 1), :], core.mean_var[:, bass.ds(i, 1), 0],
                                core.rstd[:, bass.ds(i, 1)], ALU.subtract, ALU.mult).then_inc(done["normed"], 1)

            def k_out(i):
                dve.wait_ge(done["scored"], at["scored"] + 2 * i)
                for p in range(2):
                    dve.wait_ge(done["projected"], at["projected"] + 2 * i + p + 1)
                    for h in range(2):
                        rows = slice(h * S, (h + 1) * S)
                        src = dve_ps[rows, 2 + p, :].rearrange("p (c b s) -> p c b s", c=HALF, b=2)
                        ins = V.tensor_scalar(k_diag[rows, p * HALF:(p + 1) * HALF, :, h, :], src,
                                              io["null_k"][rows, :], None, ALU.subtract)
                    ins.then_inc(done["k_ready"], 1)

            def v_out(i, slot, quad):
                dve.wait_ge(v_in[slot % 2], (quad * 2 + slot // 2) * 64)
                for p in range(2):
                    dve.wait_ge(done["v_projected"], at["v_projected"] + 2 * i + p + 1)
                    V.tensor_tensor(v_sb[:, slot % 2, p, :, 0:HD1],
                                    dve_ps[:, p, :].rearrange("p (c d) -> p c d", d=HD1),
                                    io["null_v_row"].unsqueeze(1).broadcast_to([P, PAIRS1, HD1]), ALU.subtract)\
                        .then_inc(done["v_ready"], 1)

            def soften(j):
                link = Link(dve, done["soft_step"], at["soft_step"] + 2 * j)
                dve.wait_ge(done["null_ready"], at["null_ready"] + j)
                for p in range(2):
                    dve.wait_ge(done["scored"], at["scored"] + 2 * j + p + 1)
                    hs = slice(p * H1 // 2, (p + 1) * H1 // 2)
                    ins = V.tensor_reduce(top[:, hs], s_ps[:, p, :].rearrange("p (h s) -> p h s", s=S), AX, ALU.max)
                link(ins)
                link(V.tensor_scalar(top[:, :], top[:, :], 0.0, None, ALU.max))
                for p in range(2):
                    hs = slice(p * H1 // 2, (p + 1) * H1 // 2)
                    ins = V.tensor_tensor(s_sb[:, hs, :], s_ps[:, p, :].rearrange("p (h s) -> p h s", s=S),
                                          top[:, hs].unsqueeze(2).broadcast_to([P, H1 // 2, S]), ALU.subtract)
                    ins.then_inc(done["shifted"], 1)

            def scale_o(j, slot):
                dve.wait_ge(done["pv_done"], at["pv_done"] + j + 1)
                dve.wait_ge(done["null_ready"], at["null_ready"] + j + 1)
                dve.wait_ge(done["o_turned"], at["o_turned"] + 2 * j)
                link = Link(dve, done["o_step"], at["o_step"] + 2 * j)
                for i in range(3):
                    view, h0, n = out_piece(i)
                    ins = V.tensor_tensor(den[:, h0:h0 + n], view[:, :, HD1], null[:, slot % 2, h0:h0 + n],
                                          ALU.add)
                link(ins)
                link(V.reciprocal(inv[:, :], den[:, :]))
                for i in range(3):
                    view, h0, n = out_piece(i)
                    V.tensor_tensor(o_sb[:, h0:h0 + n, :], view[:, :, 0:HD1],
                                    inv[:, h0:h0 + n].unsqueeze(2).broadcast_to([P, n, HD1]), ALU.mult)\
                        .then_inc(done["o_ready"], 1)

            def y_statistics(j):
                dve.wait_ge(done["final"], at["final"] + j + 1)
                dve.wait_ge(done["y_rstd"], at["y_rstd"] + j)
                V.bn_stats(y_stats[:, :], dve_ps[:, 0, 0:D]).then_inc(done["y_step"], 1)
                dve.wait_ge(done["y_step"], at["y_step"] + j + 1)
                dve.sem_inc(core.passed, 1)
                V.bn_aggr(y_mv[:, :], y_stats[:, :]).then_inc(done["y_stats"], 1)

            def update(j):
                dve.wait_ge(done["y_stats"], at["y_stats"] + j + 1)
                dve.wait_ge(done["y_rstd"], at["y_rstd"] + j + 1)
                link = Link(dve, done["add_step"], at["add_step"] + j * Y_STEPS)
                xj = core.x[:, bass.ds(j, 1), :]
                y = dve_ps[:, 0, 0:D].unsqueeze(1)
                link(V.scalar_tensor_tensor(y_sb[:, :, :], y, y_mv[:, 0:1], io["ln_scale"].unsqueeze(1),
                                            ALU.subtract, ALU.mult))
                link(V.scalar_tensor_tensor(y_sb[:, :, :], y_sb[:, :, :], y_rstd[:, :],
                                            io["ln_bias"].unsqueeze(1), ALU.mult, ALU.add))
                add_to_x(core, dve, link, j, y_sb[:, 0, :], stats, mv)

            def step(j, slot, quad):
                to_start = is_tile(j, -2, -1)
                if not is_tile(j, -2, TILES - 1):
                    soften(j + 1)
                    v_out(j + 1, (slot + 1) % SLOTS, quad + (slot + 1) // SLOTS)
                if not is_tile(j, TILES - 2, TILES - 1):
                    k_out(j + 2)
                if not (to_start or is_tile(j, 0)):
                    y_statistics(j - 1)
                if not (to_start or is_tile(j, *range(TILES - SLOTS, TILES))):
                    norm(j + 4, slot)
                if not (to_start or is_tile(j, 0)):
                    update(j - 1)
                if not to_start:
                    scale_o(j, slot)

            V.memset(v_diag[:, :, :, :, :, :], 0.0).then_inc(done["cleared"], 1)
            V.memset(k_diag[:, :, :, :, :], 0.0).then_inc(done["cleared"], 1)
            V.memset(ones[:, :], 1.0)
            V.memset(v_sb[:, :, :, :, :], 1.0).then_inc(done["cleared"], 1)
            new_rstd(core, std, dve=dve)
            for s, v in loaded:
                dve.wait_ge(s, v)
            dve.wait_ge(done["setup"], at["setup"] + 1)
            V.tensor_copy(row[:, :], dve_ps[0:1, 0, 0:D]).then_inc(done["cleared"], 1)
            dve.wait_ge(done["cleared"], at["cleared"] + 4)
            for i in range(SLOTS):
                norm(i, i)
            step(-2, 2, -1)
            step(-1, 3, -1)
            over_slots(dve, step)
            y_statistics(TILES - 1)
            update(TILES - 1)

    one, two = TILES, 2 * TILES
    core.attention_signals.phase_ends({
        "x_turned": one, "q_projected": two, "projected": two, "v_projected": two, "scored": two,
        "p_turned": two, "pv_done": one, "o_turned": two, "final": one, "setup": 1,
        "xt_ready": one, "qt_ready": two, "pt_ready": two, "ot_ready": two, "exped": two, "null_ready": one,
        "std": 1, "std_in": 1, "rstd": 1, "cleared": 4, "normed": one, "shifted": two, "k_ready": two,
        "v_ready": two, "o_ready": 3 * TILES, "soft_step": two, "o_step": two, "y_stats": one, "y_step": one,
        "updated": one, "add_step": Y_STEPS * TILES, "pool_setup": 2, "pool_var": one, "y_rstd": one}, 0)
    core.slot_loads += TILES // SLOTS
    if out is not None:
        store_x(core, out)


RMS_EPS2 = 1e-5
LOG_P = -0.001


def l2_depool(core, io, loaded, out=None):
    nc = core.nc
    done, at = core.depool_signals.done, core.depool_signals.at()

    with ExitStack() as local:
        def sb(name, shape, dt=F32):
            return local.enter_context(nc.sbuf_tensor("l2d_" + name, shape, dt))

        def pb(name, shape):
            return local.enter_context(nc.psum_tensor("l2d_" + name, shape, F32))

        lens = sb("lens", [B, S], I32)
        count = sb("count", [B, S])
        ones_row = sb("ones_row", [B, S])
        last = sb("last", [B, S])
        wrap = sb("wrap", [B, S])
        plug = sb("plug", [B, S])
        cube = sb("cube", [B, S, S])
        all_ones = sb("all_ones", [B, S])
        spread_m = sb("spread_m", [P, TILES, P])
        w_in = sb("w_in", [P, D])
        ms = sb("ms", [P, TILES])
        std = sb("std", [P, TILES])
        xn = sb("xn", [P, 2, GT, D])
        xt = sb("xt", [P, GN])
        ctx_sb = sb("ctx", [P, 2, GT, CTX])
        squares = sb("squares", [P, CTX])
        ssq = sb("ssq", [P, GT])
        msq = sb("msq", [P, GT])
        scale_c = sb("scale_c", [P, GT])
        minus_half = sb("minus_half", [P, GT])
        patch = sb("patch", [P, GT, D])
        y_sb = sb("y_sb", [P, GN])
        stats = sb("stats", [P, GT, 6])
        mv = sb("mv", [P, GT, 2])
        m_ps = pb("m_ps", [P, 2, 512])
        x_ps = pb("x_ps", [P, GN])
        y_ps = pb("y_ps", [P, 2, GN])
        t_ps = pb("t_ps", [P, GN])
        base = core.ctx_loads

        block = local.enter_context(nc.Block())

        @block.sync
        def _(sp):
            sp.dma_start(lens[:, :], core.dram["lens"]).then_inc(core.lens_in, 16)
            start_later_loads(core, sp, 4)
            tokens = core.dram["ctx_tok"].rearrange("(t p) f -> p t f", p=P)

            def body(g, buf):
                sp.wait_ge(done["patches"], at["patches"] + g - 1)
                sp.sem_inc(core.passed, 1)
                sp.dma_start(ctx_sb[:, buf, :, :], tokens[:, bass.ds(g * GT, GT), :]).then_inc(core.ctx_in[buf], 16)

            in_pairs(sp, body)

        @block.tensor
        def _(pe):
            mmul = nc.tensor.matmul

            def turn_x(g, buf):
                pe.wait_ge(done["normed"], at["normed"] + g + 1)
                pe.wait_ge(done["xt_ready"], at["xt_ready"] + g)
                for t in range(GT):
                    mm = nc.tensor.transpose(x_ps[:, t * P:(t + 1) * P], xn[:, buf, t, :], core.ident[:, :])
                mm.then_inc(done["x_turned"], 1)

            def mix(g, buf):
                pe.wait_ge(done["xt_ready"], at["xt_ready"] + g + 1)
                pe.wait_ge(done["patches"], at["patches"] + g + 1)
                pe.wait_ge(done["y_out"], at["y_out"] + g - 1)
                for t in range(GT):
                    to = y_ps[:, buf, t * P:(t + 1) * P]
                    mmul(to, w_in[:, :], xt[:, t * P:(t + 1) * P], start=True, stop=False)
                    mm = mmul(to, patch[:, t, :], spread_m[:, bass.ds(g * GT + t, 1), :]
                              .rearrange("p a s -> p (a s)"), start=False, stop=True)
                mm.then_inc(done["mixed"], 1)

            def turn_y(g):
                pe.wait_ge(done["y_out"], at["y_out"] + g + 1)
                pe.wait_ge(done["updated"], at["updated"] + g)
                for t in range(GT):
                    mm = nc.tensor.transpose(t_ps[:, t * P:(t + 1) * P], y_sb[:, t * P:(t + 1) * P], core.ident[:, :])
                mm.then_inc(done["y_turned"], 1)

            def body(g, buf):
                if not is_group(g, GROUPS - 1):
                    turn_x(g + 1, 1 - buf)
                mix(g, buf)
                if not is_group(g, 0):
                    turn_y(g - 1)

            for s, v in loaded:
                pe.wait_ge(s, v)
            pe.wait_ge(done["plugged"], at["plugged"] + 1)
            flat = cube[:, :, :].rearrange("p b s -> p (b s)")
            for n in range(8):
                pe.wait_ge(done["compared"], at["compared"] + n - 1)
                mmul(m_ps[0:S, n % 2, :], all_ones[:, :], flat[:, n * 512:(n + 1) * 512], start=True, stop=True)\
                    .then_inc(done["spread"], 1)
            for n in range(8):
                pe.wait_ge(done["compared"], at["compared"] + 8)
                pe.wait_ge(done["m_out"], at["m_out"] + n - 1)
                mmul(m_ps[:, n % 2, :], io["decay"], flat[:, n * 512:(n + 1) * 512], start=True, stop=True)\
                    .then_inc(done["m_made"], 1)
            turn_x(0, 0)
            pe.wait_ge(done["m_out"], at["m_out"] + 8)
            in_pairs(pe, body)
            turn_y(GROUPS - 1)

        @block.scalar
        def _(act_eng):
            A = nc.scalar

            def y_out(g, buf):
                act_eng.wait_ge(done["mixed"], at["mixed"] + g + 1)
                act_eng.wait_ge(done["y_turned"], at["y_turned"] + g)
                A.activation(y_sb[:, :], y_ps[:, buf, :], ACT.Identity, bias=io["b_in"]).then_inc(done["y_out"], 1)

            def group(g, buf, pair):
                y_out(g, buf)
                if not is_group(g, GROUPS - 1):
                    act_eng.wait_ge(done["x_turned"], at["x_turned"] + g + 2)
                    A.activation(xt[:, :], x_ps[:, :], ACT.Copy).then_inc(done["xt_ready"], 1)
                if not is_group(g, GROUPS - 2, GROUPS - 1):
                    squares_of(g + 2, buf, pair + 1)

            def squares_of(g, buf, pair):
                act_eng.wait_ge(core.ctx_in[buf], (pair + base + 1) * 16)
                act_eng.wait_ge(done["msq"], at["msq"] + g)
                for t in range(GT):
                    A.activation(squares[:, :], ctx_sb[:, buf, t, :], ACT.Square, accum_out=ssq[:, t:t + 1])\
                        .then_inc(done["square_step"], 1)
                    act_eng.wait_ge(done["square_step"], at["square_step"] + g * GT + t + 1)

            act_eng.wait_ge(done["std_in"], at["std_in"] + 1)
            A.activation(std[:, :], std[:, :], ACT.Sqrt).then_inc(done["std"], 1)
            act_eng.wait_ge(done["std_in"], at["std_in"] + 2)
            A.activation(ms[:, :], ms[:, :], ACT.Sqrt).then_inc(done["std"], 1)
            for s, v in loaded:
                act_eng.wait_ge(s, v)
            squares_of(0, 0, 0)
            squares_of(1, 1, 0)
            act_eng.wait_ge(done["x_turned"], at["x_turned"] + 1)
            A.activation(xt[:, :], x_ps[:, :], ACT.Copy).then_inc(done["xt_ready"], 1)
            group(0, 0, 0)
            group(1, 1, 0)
            with act_eng.Fori(1, GROUPS // 2 - 1) as pair:
                group(pair * 2, 0, pair)
                group(pair * 2 + 1, 1, pair)
            group(GROUPS - 2, 0, GROUPS // 2 - 1)
            group(GROUPS - 1, 1, GROUPS // 2 - 1)

        @block.gpsimd
        def _(pool):
            G = nc.gpsimd
            G.memset(minus_half[:, :], -0.5).then_inc(done["pool_setup"], 1)
            pool.wait_ge(done["pool_setup"], at["pool_setup"] + 1)

            def body(g, buf):
                pool.wait_ge(done["msq"], at["msq"] + g + 1)
                pool.wait_ge(done["patches"], at["patches"] + g)
                G.tensor_tensor(scale_c[:, :], msq[:, :], minus_half[:, :], ALU.pow).then_inc(done["scale_c"], 1)

            in_pairs(pool, body)

        @block.vector
        def _(dve):
            V = nc.vector

            def norm(g, buf):
                dve.wait_ge(done["x_turned"], at["x_turned"] + g - 1)
                for t in range(GT):
                    i = g * GT + t
                    ins = V.tensor_scalar(xn[:, buf, t, :], core.x[:, bass.ds(i, 1), :],
                                          core.mean_var[:, bass.ds(i, 1), 0], core.rstd[:, bass.ds(i, 1)],
                                          ALU.subtract, ALU.mult)
                ins.then_inc(done["normed"], 1)

            def mean_squares(g):
                dve.wait_ge(done["square_step"], at["square_step"] + (g + 1) * GT)
                dve.wait_ge(done["scale_c"], at["scale_c"] + g)
                V.tensor_scalar(msq[:, :], ssq[:, :], 1.0 / CTX, RMS_EPS2, ALU.mult, ALU.add)\
                    .then_inc(done["msq"], 1)

            def patches(g, buf):
                dve.wait_ge(done["scale_c"], at["scale_c"] + g + 1)
                dve.wait_ge(done["mixed"], at["mixed"] + g)
                for t in range(GT):
                    ins = V.scalar_tensor_tensor(patch[:, t, :], ctx_sb[:, buf, t, 0:D], scale_c[:, t:t + 1],
                                                 io["g_init"], ALU.mult, ALU.mult)
                ins.then_inc(done["patches"], 1)

            def update(g):
                dve.wait_ge(done["y_turned"], at["y_turned"] + g + 1)
                link = Link(dve, done["update_step"], at["update_step"] + g * UPDATE_STEPS)
                x4 = core.x[:, bass.ds(g * GT, GT), :]
                link(V.tensor_tensor(x4, x4, t_ps[:, :].rearrange("p (t d) -> p t d", d=D), ALU.add))
                dve.sem_inc(core.passed, 1)
                for t in range(GT):
                    ins = V.bn_stats(stats[:, t, :], core.x[:, bass.ds(g * GT + t, 1), :])
                link(ins)
                dve.sem_inc(core.passed, 1)
                for t in range(GT):
                    ins = V.bn_aggr(mv[:, t, :], stats[:, t, :])
                link(ins)
                V.tensor_copy(core.mean_var[:, bass.ds(g * GT, GT), :], mv[:, :, :]).then_inc(done["updated"], 1)

            def body(g, buf):
                if not is_group(g, GROUPS - 1):
                    mean_squares(g + 1)
                    patches(g + 1, 1 - buf)
                if not is_group(g, 0):
                    update(g - 1)
                if not is_group(g, GROUPS - 2, GROUPS - 1):
                    norm(g + 2, buf)

            link = Link(dve, done["setup_step"], at["setup_step"])
            link(V.tensor_scalar(std[:, :], core.mean_var[:, :, 1], LN_EPS, None, ALU.add))
            V.memset(ones_row[:, :], 1.0).then_inc(done["std_in"], 1)
            link(V.memset(all_ones[:, :], 1.0))
            link(V.memset(spread_m[:, :, :], 0.0))
            dve.wait_ge(done["std"], at["std"] + 1)
            link(V.reciprocal(core.rstd[:, :], std[:, :]))
            link(V.tensor_tensor(ms[:, :], core.rstd[:, :], core.rstd[:, :], ALU.mult))
            link(V.tensor_tensor(ms[:, :], ms[:, :], core.mean_var[:, :, 1], ALU.mult))
            V.tensor_scalar(ms[:, :], ms[:, :], RMS_EPS2, None, ALU.add).then_inc(done["std_in"], 1)
            dve.wait_ge(done["std"], at["std"] + 2)
            link(V.reciprocal(ms[:, :], ms[:, :]))
            link(V.tensor_tensor(core.rstd[:, :], core.rstd[:, :], ms[:, :], ALU.mult))
            for s, v in loaded:
                dve.wait_ge(s, v)
            norm(0, 0)
            norm(1, 1)
            link(V.tensor_scalar(w_in[:, :], io["w_in"], io["g_res"], None, ALU.mult))
            dve.wait_ge(core.lens_in, 16)
            link(V.tensor_copy(count[:, :], lens[:, :]))
            link(V.tensor_tensor_scan(last[:, :], ones_row[:, :], count[:, :], 0.0, ALU.mult, ALU.add))
            link(V.tensor_scalar(last[:, :], last[:, :], -1.0, None, ALU.add))
            link(V.tensor_scalar(wrap[:, :], last[:, :], 0.0, float(S), ALU.is_lt, ALU.mult))
            link(V.tensor_tensor(last[:, :], last[:, :], wrap[:, :], ALU.add))
            link(V.tensor_tensor(cube[:, :, :], last[:, :].unsqueeze(1).broadcast_to([B, S, S]),
                                 io["token"].unsqueeze(2).broadcast_to([B, S, S]), ALU.is_equal))
            link(V.tensor_reduce(wrap[:, :], cube[:, :, :], AX, ALU.max))
            link(V.tensor_tensor_scan(count[:, :], ones_row[:, :], wrap[:, :], 0.0, ALU.mult, ALU.add))
            link(V.tensor_scalar(plug[:, :], count[:, :], -1.0, 0.0, ALU.add, ALU.max))
            link(V.tensor_scalar(plug[:, :], plug[:, :], float(S - 1), None, ALU.min))
            V.tensor_tensor(cube[:, :, :], plug[:, :].unsqueeze(1).broadcast_to([B, B, S]),
                            core.ident[0:B, 0:B].unsqueeze(2).broadcast_to([B, B, S]), ALU.mult)\
                .then_inc(done["plugged"], 1)
            flat = cube[:, :, :].rearrange("p b s -> p (b s)")
            for n in range(8):
                dve.wait_ge(done["spread"], at["spread"] + n + 1)
                V.tensor_scalar(flat[:, n * 512:(n + 1) * 512], m_ps[0:S, n % 2, :], io["number"], None, ALU.is_equal)\
                    .then_inc(done["compared"], 1)
            for n in range(8):
                dve.wait_ge(done["m_made"], at["m_made"] + n + 1)
                got = m_ps[:, n % 2, :].rearrange("p (t b s) -> p t b s", b=2, s=S)
                for b in range(2):
                    rows = slice(b * S, (b + 1) * S)
                    ins = V.tensor_copy(spread_m[rows, n * GT:(n + 1) * GT, b * S:(b + 1) * S], got[rows, :, b, :])
                ins.then_inc(done["m_out"], 1)
            mean_squares(0)
            patches(0, 0)
            in_pairs(dve, body)
            update(GROUPS - 1)

    core.ctx_loads += GROUPS // 2
    if out is not None:
        store_x(core, out)


DEPOOL_SIGNALS = {
    "PE": ("x_turned", "mixed", "y_turned", "spread", "m_made"),
    "ACT": ("xt_ready", "y_out", "square_step", "std"),
    "Pool": ("pool_setup", "scale_c"),
    "DVE": ("normed", "patches", "msq", "updated", "update_step", "std_in", "setup_step", "plugged", "compared",
            "m_out"),
}


H3 = 16
HD3 = D // H3
KEYS3 = 2 * S
BANK_HEADS = 512 // KEYS3
BANKS3 = H3 // BANK_HEADS


def l3_attention(core, io, loaded, out=None):
    nc = core.nc
    done, at = core.attention_signals.done, core.attention_signals.at()
    scale = float(HD3) ** -0.5

    with ExitStack() as local:
        def sb(name, shape, dt=F32):
            return local.enter_context(nc.sbuf_tensor("l3a_" + name, shape, dt))

        def pb(name, shape):
            return local.enter_context(nc.psum_tensor("l3a_" + name, shape, F32))

        k_all = sb("k_all", [P, SLOTS, 2, 2, S])
        ctx_v = sb("ctx_v", [S, SLOTS, 2, D])
        v_all = sb("v_all", [P, SLOTS, 2, H3, HD3 + 1])
        xn = sb("xn", [P, SLOTS, D])
        xt = sb("xt", [P, P])
        qt = sb("qt", [P, P])
        q_head = sb("q_head", [P, 2, H3, S])
        s_sb = sb("s_sb", [P, H3, KEYS3])
        probs = sb("probs", [P, H3, KEYS3])
        top = sb("top", [P, H3])
        pt = sb("pt", [P, H3, P])
        inv = sb("inv", [P, H3])
        o_sb = sb("o_sb", [P, H3, HD3])
        ot = sb("ot", [P, P])
        ones = sb("ones", [1, P])
        std = sb("std", [P, TILES])
        stats = sb("stats", [P, 6])
        mv = sb("mv", [P, 2])
        act_ps = pb("act_ps", [P, 2, 512])
        s_ps = pb("s_ps", [P, BANKS3, BANK_HEADS, KEYS3])
        qkv_ps = pb("qkv_ps", [P, 4, P])
        o_ps = pb("o_ps", [P, 512])
        o_view = o_ps[:, 0:H3 * (HD3 + 1)].rearrange("p (h d) -> p h d", d=HD3 + 1)
        y_ps = qkv_ps[:, 0, :]
        loads_before = core.slot_loads

        def heads_of(p):
            return slice(p * BANK_HEADS, (p + 1) * BANK_HEADS)

        def context_loads(quad):
            return (2 * quad + loads_before + 2) * 16

        block = local.enter_context(nc.Block())

        @block.sync
        def _(sp):
            tokens = core.dram["ctx_tok"].rearrange("(j b s) f -> s j b f", b=2, s=S)

            def step(j, slot, quad):
                sp.wait_ge(done["pv_done"], at["pv_done"] + j - 3)
                sp.sem_inc(core.passed, 1)
                keys = core.dram["ctx_t"][:, bass.ds(j, 1), 0, :].rearrange("p j (b s) -> p (j b) s", b=2)
                sp.dma_start(k_all[:, slot, :, 0, :], keys).then_inc(core.slot_in[slot], 16)
                sp.dma_start(ctx_v[:, slot, :, :], tokens[:, bass.ds(j, 1), :, D:2 * D]
                             .rearrange("s j b f -> s (j b) f")).then_inc(core.slot_in[slot], 16)

            over_slots(sp, step)

        @block.tensor
        def _(pe):
            mmul = nc.tensor.matmul

            def project(i):
                pe.wait_ge(done["xt_ready"], at["xt_ready"] + i + 1)
                pe.wait_ge(done["k_ready"], at["k_ready"] + i)
                pe.wait_ge(done["updated"], at["updated"] + i - 3)
                for part in range(2):
                    mmul(qkv_ps[:, part, :], io["w_qkv"][:, part * D:(part + 1) * D], xt[:, :], start=True, stop=True)
                for b in range(2):
                    mm = mmul(qkv_ps[S:P, 2 + b, :], xt[:, b * S:(b + 1) * S], io["w_qkv"][:, 2 * D:3 * D],
                              start=True, stop=True)
                mm.then_inc(done["projected"], 1)

            def turn_x(i, slot):
                pe.wait_ge(done["normed"], at["normed"] + i + 1)
                pe.wait_ge(done["xt_ready"], at["xt_ready"] + i)
                if not is_tile(i, 0, 1, 2):
                    pe.wait_ge(done["pt_ready"], at["pt_ready"] + BANKS3 * (i - 3))
                nc.tensor.transpose(act_ps[:, 1, 0:P], xn[:, slot, :], core.ident[:, :])\
                    .then_inc(done["x_turned"], 1)

            def scores(i, slot, quad, p):
                if p == 0:
                    pe.wait_ge(done["q_ready"], at["q_ready"] + i + 1)
                    pe.wait_ge(core.slot_in[slot], context_loads(quad))
                pe.wait_ge(done["shifted"], at["shifted"] + BANKS3 * (i - 1) + p + 1)
                for h in range(BANK_HEADS):
                    for b in range(2):
                        mm = mmul(s_ps[b * S:(b + 1) * S, p, h, :], q_head[:, b, p * BANK_HEADS + h, :],
                                  k_all[:, slot, b, :, :], start=True, stop=True)
                mm.then_inc(done["scored"], 1)

            def turn_p(j, p):
                pe.wait_ge(done["exped"], at["exped"] + BANKS3 * j + p + 1)
                if p == 0:
                    pe.wait_ge(done["ot_ready"], at["ot_ready"] + j)
                elif p == 1:
                    pe.wait_ge(done["xt_ready"], at["xt_ready"] + up_to_last(j + 3) + 1)
                else:
                    pe.wait_ge(done["pt_ready"], at["pt_ready"] + BANKS3 * j + p - 1)
                for h in range(BANK_HEADS):
                    mm = nc.tensor.transpose(act_ps[:, p % 2, h * P:(h + 1) * P],
                                             probs[:, p * BANK_HEADS + h, :], core.ident[:, :])
                mm.then_inc(done["p_turned"], 1)

            def turn_o(i):
                pe.wait_ge(done["o_ready"], at["o_ready"] + i + 1)
                pe.wait_ge(done["pt_ready"], at["pt_ready"] + BANKS3 * i + BANKS3 - 1)
                nc.tensor.transpose(act_ps[:, 0, 0:P], o_sb[:, :, :], core.ident[:, :]).then_inc(done["o_turned"], 1)

            def weigh_v(j, slot):
                pe.wait_ge(done["v_ready"], at["v_ready"] + j + 1)
                pe.wait_ge(done["o_ready"], at["o_ready"] + j)
                for p in range(BANKS3):
                    pe.wait_ge(done["pt_ready"], at["pt_ready"] + BANKS3 * j + p + 1)
                    for h in range(p * BANK_HEADS, (p + 1) * BANK_HEADS):
                        for b in range(2):
                            mm = mmul(o_ps[b * S:(b + 1) * S, h * (HD3 + 1):(h + 1) * (HD3 + 1)],
                                      pt[:, h, b * S:(b + 1) * S], v_all[:, slot, b, h, :], start=True, stop=True)
                mm.then_inc(done["pv_done"], 1)

            def final(i):
                pe.wait_ge(done["ot_ready"], at["ot_ready"] + i + 1)
                pe.wait_ge(done["k_ready"], at["k_ready"] + up_to_last(i + 3) + 1)
                mmul(y_ps, ot[:, :], io["w_proj"], start=True, stop=False)
                mmul(y_ps, ones[:, :], io["b_proj"], start=False, stop=True).then_inc(done["final"], 1)

            def step(j, slot, quad):
                if not is_tile(j, TILES - 2, TILES - 1):
                    project(j + 2)
                if not is_tile(j, TILES - 3, TILES - 2, TILES - 1):
                    turn_x(j + 3, (slot + 3) % SLOTS)
                if not is_tile(j, 0):
                    turn_o(j - 1)
                for p in range(BANKS3):
                    if not is_tile(j, TILES - 1):
                        scores(j + 1, (slot + 1) % SLOTS, quad + (slot + 1) // SLOTS, p)
                    turn_p(j, p)
                if not is_tile(j, 0):
                    final(j - 1)
                weigh_v(j, slot)

            for s, v in loaded:
                pe.wait_ge(s, v)
            pe.wait_ge(done["cleared"], at["cleared"] + 1)
            turn_x(0, 0)
            project(0)
            turn_x(1, 1)
            project(1)
            turn_x(2, 2)
            for p in range(BANKS3):
                scores(0, 0, 0, p)
            over_slots(pe, step)
            turn_o(TILES - 1)
            final(TILES - 1)

        @block.scalar
        def _(act_eng):
            A = nc.scalar

            def xt_out(i):
                act_eng.wait_ge(done["x_turned"], at["x_turned"] + i + 1)
                act_eng.wait_ge(done["projected"], at["projected"] + i)
                A.activation(xt[:, :], act_ps[:, 1, 0:P], ACT.Copy).then_inc(done["xt_ready"], 1)

            def pt_out(j):
                act_eng.wait_ge(done["pv_done"], at["pv_done"] + j)
                for p in range(BANKS3):
                    act_eng.wait_ge(done["p_turned"], at["p_turned"] + BANKS3 * j + p + 1)
                    A.activation(pt[:, heads_of(p), :], act_ps[:, p % 2, :], ACT.Copy).then_inc(done["pt_ready"], 1)

            def ot_out(i):
                act_eng.wait_ge(done["o_turned"], at["o_turned"] + i + 1)
                act_eng.wait_ge(done["final"], at["final"] + i)
                A.activation(ot[:, :], act_ps[:, 0, 0:P], ACT.Copy).then_inc(done["ot_ready"], 1)

            def exps(i):
                for p in range(BANKS3):
                    act_eng.wait_ge(done["shifted"], at["shifted"] + BANKS3 * i + p + 1)
                    act_eng.wait_ge(done["p_turned"], at["p_turned"] + BANKS3 * (i - 1) + p + 1)
                    A.activation(probs[:, heads_of(p), :], s_sb[:, heads_of(p), :], ACT.Exp, scale=scale)\
                        .then_inc(done["exped"], 1)

            def step(j, slot, quad):
                if not is_tile(j, TILES - 3, TILES - 2, TILES - 1):
                    xt_out(j + 3)
                if not is_tile(j, 0):
                    ot_out(j - 1)
                pt_out(j)
                if not is_tile(j, TILES - 1):
                    exps(j + 1)

            new_rstd(core, std, act_eng=act_eng)
            for i in range(3):
                xt_out(i)
            exps(0)
            over_slots(act_eng, step)
            ot_out(TILES - 1)

        @block.gpsimd
        def _(pool):
            G = nc.gpsimd

            def q_and_v(i, slot, quad):
                pool.wait_ge(done["pv_done"], at["pv_done"] + i - 3)
                pool.wait_ge(core.slot_in[slot], context_loads(quad))
                pool.sem_inc(core.passed, 1)
                G.tensor_copy(v_all[0:S, slot, :, :, 0:HD3],
                              ctx_v[:, slot, :, :].rearrange("p b (h d) -> p b h d", d=HD3))\
                    .then_inc(done["v_ready"], 1)
                pool.wait_ge(done["k_ready"], at["k_ready"] + i + 1)
                pool.wait_ge(done["scored"], at["scored"] + BANKS3 * i)
                for b in range(2):
                    ins = G.tensor_tensor(q_head[:, b, :, :],
                                          qt[:, b * S:(b + 1) * S].unsqueeze(1).broadcast_to([P, H3, S]),
                                          io["heads"].unsqueeze(2).broadcast_to([P, H3, S]), ALU.mult)
                ins.then_inc(done["q_ready"], 1)

            def step(j, slot, quad):
                if not is_tile(j, TILES - 2, TILES - 1):
                    q_and_v(j + 2, (slot + 2) % SLOTS, quad + (slot + 2) // SLOTS)

            for s, v in loaded:
                pool.wait_ge(s, v)
            pool.wait_ge(done["cleared"], at["cleared"] + 2)
            q_and_v(0, 0, 0)
            q_and_v(1, 1, 0)
            over_slots(pool, step)

        @block.vector
        def _(dve):
            V = nc.vector

            def norm(i, slot):
                dve.wait_ge(done["x_turned"], at["x_turned"] + i - 3)
                V.tensor_scalar(xn[:, slot, :], core.x[:, bass.ds(i, 1), :], core.mean_var[:, bass.ds(i, 1), 0],
                                core.rstd[:, bass.ds(i, 1)], ALU.subtract, ALU.mult).then_inc(done["normed"], 1)

            def qkv_out(i, slot):
                dve.wait_ge(done["projected"], at["projected"] + i + 1)
                dve.wait_ge(done["q_ready"], at["q_ready"] + i)
                dve.wait_ge(done["pv_done"], at["pv_done"] + i - 3)
                V.tensor_copy(qt[:, :], qkv_ps[:, 0, :])
                V.tensor_copy(k_all[:, slot, :, 1, :], qkv_ps[:, 1, :].rearrange("p (b s) -> p b s", b=2))
                V.tensor_copy(v_all[S:P, slot, :, :, 0:HD3],
                              qkv_ps[S:P, 2:4, :].rearrange("p b (h d) -> p b h d", d=HD3))\
                    .then_inc(done["k_ready"], 1)

            def soften(i):
                link = Link(dve, done["soft_step"], at["soft_step"] + BANKS3 * i)
                for p in range(BANKS3):
                    dve.wait_ge(done["scored"], at["scored"] + BANKS3 * i + p + 1)
                    dve.wait_ge(done["exped"], at["exped"] + BANKS3 * (i - 1) + p + 1)
                    link(V.tensor_reduce(top[:, heads_of(p)], s_ps[:, p, :, :], AX, ALU.max))
                    V.tensor_tensor(s_sb[:, heads_of(p), :], s_ps[:, p, :, :],
                                    top[:, heads_of(p)].unsqueeze(2).broadcast_to([P, BANK_HEADS, KEYS3]),
                                    ALU.subtract).then_inc(done["shifted"], 1)

            def scale_o(j):
                dve.wait_ge(done["pv_done"], at["pv_done"] + j + 1)
                dve.wait_ge(done["o_turned"], at["o_turned"] + j)
                link = Link(dve, done["o_step"], at["o_step"] + j)
                link(V.reciprocal(inv[:, :], o_view[:, :, HD3]))
                V.tensor_tensor(o_sb[:, :, :], o_view[:, :, 0:HD3],
                                inv[:, :].unsqueeze(2).broadcast_to([P, H3, HD3]), ALU.mult)\
                    .then_inc(done["o_ready"], 1)

            def update(i):
                dve.wait_ge(done["final"], at["final"] + i + 1)
                add_to_x(core, dve, Link(dve, done["add_step"], at["add_step"] + i * ADD_STEPS), i, y_ps, stats, mv)

            def step(j, slot, quad):
                if not is_tile(j, TILES - 2, TILES - 1):
                    qkv_out(j + 2, (slot + 2) % SLOTS)
                if not is_tile(j, TILES - 1):
                    soften(j + 1)
                if not is_tile(j, TILES - 4, TILES - 3, TILES - 2, TILES - 1):
                    norm(j + 4, slot)
                if not is_tile(j, 0):
                    update(j - 1)
                scale_o(j)

            V.memset(ones[:, :], 1.0).then_inc(done["cleared"], 1)
            V.memset(v_all[:, :, :, :, :], 1.0).then_inc(done["cleared"], 1)
            dve.wait_ge(done["cleared"], at["cleared"] + 2)
            new_rstd(core, std, dve=dve)
            for s, v in loaded:
                dve.wait_ge(s, v)
            for i in range(SLOTS):
                norm(i, i)
            qkv_out(0, 0)
            qkv_out(1, 1)
            soften(0)
            over_slots(dve, step)
            update(TILES - 1)

    core.slot_loads += 2 * TILES // SLOTS
    if out is not None:
        store_x(core, out)


L0_FFN = Experts("l0f", 32, 4, ACT.Gelu, top=1, b1=True, b2=True, br=True)
L1_FFN = Experts("l1f", 14, 1, ACT.Silu, top=2, gated=True)
L1_FFN.shared = True
L2_FFN = Experts("l2f", 16, 2, ACT.Silu, top=2, gated=True, br=True)
L3_FFN = Experts("l3f", 16, 2, ACT.Relu, top=1, b1=True, b2=True, br=True, times_prob=True)


WEIGHT_SLOTS = {1: "a", 5: "a", 3: "b", 7: "b"}
LOADED_IN = {5: 2, 7: 4}
SLOT_WORDS = {"a": 2 * L0_FFN.chunks * P, "b": 3 * L1_FFN.chunks * P}

PART_ROWS = (0, 32, 64)
SHARED_ROW = 96


def opening(core, src, loads):
    nc = core.nc
    kinds = (core.expert_signals, core.attention_signals, core.depool_signals)
    with ExitStack() as local:
        stats = local.enter_context(nc.sbuf_tensor("open_stats", [P, GT, 6], F32))
        mv = local.enter_context(nc.sbuf_tensor("open_mv", [P, GT, 2], F32))
        block = local.enter_context(nc.Block())

        @block.sync
        def _(sp):
            for g in range(GROUPS):
                sp.dma_start(core.x[:, g * GT:(g + 1) * GT, :],
                             src[g * GN:(g + 1) * GN, :].rearrange("(t p) d -> p t d", p=P))\
                    .then_inc(core.x_in[g], 16)
            for dst, dram, sem in loads:
                sp.dma_start(dst, dram).then_inc(sem, 16)

        @block.tensor
        def _(pe):
            for kind in kinds:
                for semaphore in kind.semaphores.get("PE", ()):
                    pe.sem_inc(semaphore, HEADROOM)

        @block.scalar
        def _(act_eng):
            for kind in kinds:
                for semaphore in kind.semaphores.get("ACT", ()):
                    act_eng.sem_inc(semaphore, HEADROOM)

        @block.gpsimd
        def _(pool):
            for kind in kinds:
                for semaphore in kind.semaphores.get("Pool", ()):
                    pool.sem_inc(semaphore, HEADROOM)

        @block.vector
        def _(dve):
            V = nc.vector
            for kind in kinds:
                for semaphore in kind.semaphores.get("DVE", ()):
                    dve.sem_inc(semaphore, HEADROOM)
            link = Link(dve, core.statistics_step, 0)
            for g in range(GROUPS):
                dve.wait_ge(core.x_in[g], 16)
                for t in range(GT):
                    ins = V.bn_stats(stats[:, t, :], core.x[:, g * GT + t, :])
                link(ins)
                for t in range(GT):
                    ins = V.bn_aggr(mv[:, t, :], stats[:, t, :])
                link(ins)
                link(V.tensor_copy(core.mean_var[:, g * GT:(g + 1) * GT, :], mv[:, :, :]))


def program(nc, dram, out, phases="01234567"):
    with ExitStack() as ctx:
        core = Core(nc, ctx)
        core.expert_signals = Signals(nc, ctx, "experts", EXPERT_SIGNALS)
        core.attention_signals = Signals(nc, ctx, "attention", ATTENTION_SIGNALS)
        core.depool_signals = Signals(nc, ctx, "depool", DEPOOL_SIGNALS)
        core.statistics_step = ctx.enter_context(nc.semaphore("statistics_step"))
        core.dram = dram
        core.ctx_in = [ctx.enter_context(nc.semaphore(f"ctx_in_{b}")) for b in range(2)]
        core.slot_in = [ctx.enter_context(nc.semaphore(f"slot_in_{slot}")) for slot in range(SLOTS)]
        core.slot_loads = 0
        core.v_in = [ctx.enter_context(nc.semaphore(f"v_in_{b}")) for b in range(2)]
        core.lens_in = ctx.enter_context(nc.semaphore("lens_in"))
        core.masks_in = ctx.enter_context(nc.semaphore("masks_in"))
        core.x_in = [ctx.enter_context(nc.semaphore(f"x_in_{g}")) for g in range(GROUPS)]
        core.passed = ctx.enter_context(nc.semaphore("passed"))
        core.out_done = ctx.enter_context(nc.semaphore("out_done"))
        loads, io = [], {}

        slots = {name: core.sb(f"weight_slot_{name}", [P, size]) for name, size in SLOT_WORDS.items()}
        later = {after: [] for after in LOADED_IN.values()}
        core.later = later

        def load(phase, *names):
            taken = [0]
            if str(phase) not in phases:
                return
            sem = ctx.enter_context(nc.semaphore(f"loaded_{phase}"))
            for name in names:
                a = dram[name]
                part = name.split("_", 1)[1]
                if phase in WEIGHT_SLOTS and part in ("w_in", "w_up", "w_out"):
                    words = int(np.prod(a.shape[1:]))
                    held = slots[WEIGHT_SLOTS[phase]][:, taken[0]:taken[0] + words]
                    taken[0] += words
                    if part == "w_out":
                        held = held.rearrange("p (c d) -> p c d", d=D)
                else:
                    held = core.sb("s_" + name, list(a.shape), a.dtype)[:]
                after = LOADED_IN.get(phase)
                (later[after] if str(after) in phases else loads).append((held, a[:], sem))
                io[name] = held
            return (sem, 16 * len(names))

        sem0 = ctx.enter_context(nc.semaphore("loaded_consts"))
        for t, name in ((core.ident, "ident"),):
            loads.append((t[:], dram[name][:], sem0))
        falling = core.sb("s_falling", [P, GT, NE])
        loads.append((falling[:], dram["falling"][:], sem0))
        consts = (sem0, 32)

        def tensors(phase, tag, names):
            got = load(phase, *[tag + "_" + n for n in names])
            if got is None:
                return
            return got, {**{n: io[tag + "_" + n] for n in names}, "falling": falling[:]}

        plan = {
            1: (L0_FFN, ("w_in", "w_out", "w_router", "pick", "b_in", "b_out", "b_router")),
            3: (L1_FFN, ("w_in", "w_up", "w_out", "w_router", "pick")),
            5: (L2_FFN, ("w_in", "w_up", "w_out", "w_router", "pick", "b_router")),
            7: (L3_FFN, ("w_in", "w_out", "w_router", "pick", "b_in", "b_out", "b_router")),
        }
        attention = {
            2: (l1_attention, "l1a", ("w_q", "w_k", "w_v", "w_o", "null_k", "null_v", "null_v_row", "ln_scale",
                                      "ln_bias")),
            4: (l2_depool, "l2d", ("w_in", "b_in", "g_res", "g_init", "token", "number", "decay")),
            6: (l3_attention, "l3a", ("w_qkv", "w_proj", "b_proj", "heads")),
            0: (l0_attention, "l0a", ("w_q", "w_k", "w_v", "w_o", "b_q", "b_k", "b_v", "b_o", "heads")),
        }
        ready = {p: tensors(p, cfg.tag, names) for p, (cfg, names) in plan.items()}
        ready.update({p: tensors(p, tag, names) for p, (_, tag, names) in attention.items()})
        opening(core, dram["x"], loads)
        last = phases[-1]
        for p in sorted(int(c) for c in phases):
            got, held = ready[p]
            to = out if str(p) == last else None
            if p in plan:
                experts_phase(core, plan[p][0], held, [consts, got], to)
            else:
                attention[p][0](core, held, [consts, got], to)


def laid_out(inputs):
    import numpy as np

    a = {k: np.asarray(v) for k, v in inputs.items()}
    c = np.ascontiguousarray
    bf16 = np.dtype("bfloat16")
    out = {"x": c(a["x"].reshape(B * S, D)), "ident": np.eye(P, dtype=np.float32)}

    def everywhere(v):
        return c(np.broadcast_to(v, (P, GT, NE)))

    out["falling"] = everywhere(np.arange(NE, 0, -1, dtype=np.float32))

    ctx = a["ctx_2048"].reshape(TILES, P, 2, P)
    out["ctx_t"] = c(ctx.transpose(3, 0, 2, 1))
    out["mask"] = c(a["mask_BxS2_fk1"])

    def halves(w):
        return c(w.reshape(-1, P, w.shape[1]).transpose(1, 0, 2))

    def column(v):
        return c(v.reshape(-1, 1))

    w_src = a["L0_xattn_W_src"].T
    out["l0a_w_q"] = c(a["L0_xattn_W_tgt"].T)
    out["l0a_w_k"] = halves(w_src[:, :D])
    out["l0a_w_v"] = halves(w_src[:, D:])
    out["l0a_w_o"] = halves(a["L0_xattn_W_out"].T)
    out["l0a_b_q"] = column(a["L0_xattn_b_tgt"])
    out["l0a_b_k"] = column(a["L0_xattn_b_src"][:D])
    out["l0a_b_v"] = column(a["L0_xattn_b_src"][D:])
    out["l0a_b_o"] = c(a["L0_xattn_b_out"].reshape(1, D))
    out["l0a_heads"] = np.repeat(np.eye(H0, dtype=np.float32), HD0, axis=0)

    w_kv = a["L1_xattn_Wkv"]
    w_v = w_kv[:, H1 * HD1:].reshape(CTX, PAIRS1, 2, HD1).transpose(0, 2, 1, 3).reshape(CTX, -1)
    out["l1a_w_q"] = c(a["L1_xattn_Wq"])
    out["l1a_w_k"] = halves(w_kv[:, :H1 * HD1])
    out["l1a_w_v"] = halves(w_v)
    out["l1a_w_o"] = halves(a["L1_xattn_Wout"])
    null = a["L1_xattn_null_kv"]
    out["l1a_null_k"] = column(np.concatenate([null[0], null[0]]))
    out["l1a_null_v"] = column(np.concatenate([null[1], null[1]]))
    out["l1a_null_v_row"] = c(np.broadcast_to(null[1], (P, HD1)))
    out["l1a_ln_scale"] = c(np.broadcast_to(a["L1_xattn_ln_scale"], (P, D)))
    out["l1a_ln_bias"] = c(np.broadcast_to(a["L1_xattn_ln_bias"], (P, D)))

    out["ctx_tok"] = c(a["ctx_2048"].reshape(B * S, CTX))
    out["lens"] = c(a["mask_BxS2_if0"].astype(np.int32, copy=False))
    out["l2d_w_in"] = c(a["L2_xattn_W_in"].T)
    out["l2d_b_in"] = column(a["L2_xattn_b_in"])
    out["l2d_g_res"] = column(a["L2_xattn_g_res"])
    out["l2d_g_init"] = c(np.broadcast_to(a["L2_xattn_g_init"][:D], (P, D)))
    out["l2d_token"] = c(np.broadcast_to(np.arange(S, dtype=np.float32), (B, S)))
    out["l2d_number"] = column(np.arange(S, dtype=np.float32))
    step = np.arange(S)[:, None] - np.arange(S)[None, :]
    decay = np.where(step >= 0, np.exp(LOG_P) * (-np.expm1(LOG_P)) ** np.maximum(step, 0), 0.0)
    out["l2d_decay"] = c(np.concatenate([decay, decay], 1).astype(np.float32))

    out["l3a_w_qkv"] = c(a["L3_xattn_w_qkv"].T)
    out["l3a_w_proj"] = c(a["L3_xattn_w_proj"].T)
    out["l3a_b_proj"] = c(a["L3_xattn_b_proj"].reshape(1, D))
    out["l3a_heads"] = np.repeat(np.eye(H3, dtype=np.float32), HD3, axis=0)

    def rows(w):
        return c(w.reshape(-1, P, D).transpose(1, 0, 2))

    def pick(cfg, width):
        m = np.zeros((P, cfg.spreads, P), bf16)
        for s in range(cfg.spreads):
            for i in range(P):
                unit = s * P * cfg.per + (i if cfg.per == 1 else 0)
                if unit < width * NE:
                    for r in PART_ROWS:
                        m[r + unit // width, s, i] = 1
                else:
                    m[SHARED_ROW, s, i] = 1
        return m

    def flat(w):
        return w.transpose(1, 0, 2).reshape(D, -1)

    out["l0f_w_in"] = c(flat(a["L0_ffn_w1"]))
    out["l0f_w_out"] = rows(a["L0_ffn_w2"])
    out["l0f_w_router"] = c(a["L0_ffn_w_router"])
    out["l0f_pick"] = pick(L0_FFN, 512)
    out["l0f_b_in"] = c(a["L0_ffn_b1"].reshape(-1, P).T)
    out["l0f_b_out"] = c(a["L0_ffn_b2"])
    out["l0f_b_router"] = everywhere(a["L0_ffn_b_router"])

    units = L1_FFN.chunks * P

    def padded(w, axis):
        pad = [(0, 0), (0, 0)]
        pad[axis] = (0, units - w.shape[axis])
        return c(np.pad(w, pad))

    out["l1f_w_in"] = padded(np.concatenate([flat(a["L1_ffn_W1"]), a["L1_ffn_Ws1"]], 1), 1)
    out["l1f_w_up"] = padded(np.concatenate([flat(a["L1_ffn_W2"]), a["L1_ffn_Ws2"]], 1), 1)
    out["l1f_w_out"] = rows(padded(np.concatenate([a["L1_ffn_W3"].reshape(-1, D), a["L1_ffn_Ws3"]], 0), 0))
    out["l1f_w_router"] = c(a["L1_ffn_Wg"])
    out["l1f_pick"] = pick(L1_FFN, 176)

    out["l2f_w_in"] = c(flat(a["L2_ffn_gate_w"]))
    out["l2f_w_up"] = c(flat(a["L2_ffn_up_w"]))
    out["l2f_w_out"] = rows(a["L2_ffn_down_w"])
    out["l2f_w_router"] = c(a["L2_ffn_router_w"].T)
    out["l2f_pick"] = pick(L2_FFN, 256)
    out["l2f_b_router"] = everywhere(a["L2_ffn_router_b"])

    out["l3f_w_in"] = c(flat(a["L3_ffn_W1"]))
    out["l3f_w_out"] = rows(a["L3_ffn_W2"])
    out["l3f_w_router"] = c(a["L3_ffn_Wr"])
    out["l3f_pick"] = pick(L3_FFN, 256)
    out["l3f_b_in"] = c(a["L3_ffn_b1"].reshape(-1, P).T)
    out["l3f_b_out"] = c(a["L3_ffn_b2"])
    out["l3f_b_router"] = everywhere(a["L3_ffn_br"])
    return out


def kernel(**inputs):
    import numpy as _np
    import concourse.bacc as _bacc
    from concourse import mybir as _mybir
    from concourse.bass_utils import run_bass_kernel_spmd as _run

    nc = _bacc.Bacc("TRN2", target_bir_lowering=False, num_devices=1)
    arrays = laid_out(inputs)
    dram = {n: nc.dram_tensor("in_" + n, a.shape, _mybir.dt.from_np(a.dtype), kind="ExternalInput").ap()
            for n, a in arrays.items()}
    out = nc.dram_tensor("out", (B * S, D), _mybir.dt.float32, kind="ExternalOutput").ap()
    program(nc, dram, out)
    r = _run(nc, [{"in_" + n: a for n, a in arrays.items()}], core_ids=[0])
    return r.results[0]["out"].reshape(B, S, D)
```

```python
from contextlib import ExitStack

import concourse.bass as bass
import numpy as np
from concourse import mybir

F32 = mybir.dt.float32
F32R = mybir.dt.float32r
I32 = mybir.dt.int32
ALU = mybir.AluOpType
ACT = mybir.ActivationFunctionType
AX = mybir.AxisListType.X

P = 128
B, S, D, CTX = 64, 64, 128, 256
TILES = B * S // P
GT = 4
GROUPS = TILES // GT
GN = GT * P
NE = 8
LN_EPS = 1e-5
SLOTS = 4
HEADROOM = 16


class Signals:

    def __init__(self, nc, ctx, kind, by_engine):
        named = {name: ctx.enter_context(nc.semaphore(f"{kind}_{name}"))
                 for engine in by_engine for name in by_engine[engine]}
        self.done = named
        self.semaphores = {engine: [named[name] for name in by_engine[engine]] for engine in by_engine}
        self.values = {name: HEADROOM for name in named}

    def at(self):
        return dict(self.values)

    def phase_ends(self, counts, default):
        for name in self.values:
            self.values[name] += counts.get(name, default)


class Link:

    def __init__(self, eng, semaphore, value):
        self.eng, self.semaphore, self.value = eng, semaphore, value

    def __call__(self, instruction):
        self.value = self.value + 1
        instruction.then_inc(self.semaphore, 1)
        self.eng.wait_ge(self.semaphore, self.value)


class Core:

    def __init__(self, nc, ctx):
        self.nc, self.ctx = nc, ctx
        self.x = self.sb("x_tok", [P, TILES, D])
        self.mean_var = self.sb("mean_var", [P, TILES, 2])
        self.rstd = self.sb("rstd", [P, TILES])
        self.ident = self.sb("ident", [P, P])
        self.ctx_loads = 0

    def sb(self, name, shape, dt=F32):
        return self.ctx.enter_context(self.nc.sbuf_tensor(name, shape, dt))


class Times:

    def __init__(self, turn_x, y, xt, logits, split_xt, route, fn, combine, turn_w, weights, turn_y, update, norm):
        self.turn_x, self.xt, self.logits, self.split_xt, self.route, self.fn = turn_x, xt, logits, split_xt, route, fn
        self.combine, self.turn_w, self.weights, self.turn_y = combine, turn_w, weights, turn_y
        self.y, self.update, self.norm = y, update, norm


LONG = Times(0, 2, 5, 5, 8, (9, 9, 10), 12, 13, 13, 17, 17, 21, 23)
MIDDLE = Times(0, 2, 4, 3, 6, (7, 7, 8), 9, 10, 9, 13, 11, 15, 15)
GATED = Times(0, 2, 4, 3, 5, (6, 6, 7), 9, 9, 8, 12, 11, 14, 15)
SHORT = Times(0, 2, 4, 3, 5, (5, 6, 7), 8, 9, 8, 11, 11, 13, 13)

class Experts:

    def __init__(self, tag, chunks, per, act, top, gated=False, b1=False, b2=False, br=False,
                 times_prob=False,
                 times=LONG):
        self.shared = False
        self.high_on_act = gated
        self.ahead = 3 if gated else 4
        self.high_behind = 2
        self.spread_ahead = per + 1
        self.times = times
        self.drained = self.ahead - 2
        self.tag, self.chunks, self.per, self.act, self.top = tag, chunks, per, act, top
        self.gated, self.b1, self.b2, self.br, self.times_prob = gated, b1, b2, br, times_prob
        self.spreads = chunks // per
        self.whole = top == 1 and not times_prob
        self.route_steps = (19 if top == 2 else 8 if times_prob else 6) + (1 if self.whole else 2)


UPDATE_STEPS = 3
HIDDEN = 4


def in_pairs(eng, body):
    body(0, 0)
    body(1, 1)
    with eng.Fori(1, GROUPS // 2 - 1) as pair:
        body(pair * 2, 0)
        body(pair * 2 + 1, 1)
    body(GROUPS - 2, 0)
    body(GROUPS - 1, 1)


def is_group(g, *which):
    return isinstance(g, int) and g in which


def experts_phase(core, cfg, io, loaded, out=None):
    nc = core.nc
    n, per = cfg.chunks, cfg.per
    done, at = core.expert_signals.done, core.expert_signals.at()

    with ExitStack() as local:
        def sb(name, shape, dt=F32):
            return local.enter_context(nc.sbuf_tensor(f"{cfg.tag}_{name}", shape, dt))

        def pb(name, shape):
            return local.enter_context(nc.psum_tensor(f"{cfg.tag}_{name}", shape, F32))

        xn = sb("xn", [P, 2, GT, D])
        xt = sb("xt", [P, GN])
        xt_hi = sb("xt_hi", [P, 2, GN], F32R)
        xt_lo = sb("xt_lo", [P, 2, GN], F32R)
        acts = 2 if cfg.gated else HIDDEN
        act = sb("act", [P, acts, GN])
        prod = sb("prod", [P, 2, GN]) if cfg.gated else None
        hid = sb("hid", [P, HIDDEN, GN])
        hid_hi = sb("hid_hi", [P, HIDDEN, GN], F32R)
        hid_lo = sb("hid_lo", [P, HIDDEN, GN], F32R)
        y_sb = sb("y_sb", [P, GN])
        logit = sb("logit", [P, GT, NE])
        others = sb("others", [P, GT, NE])
        hits = sb("hits", [P, GT, NE])
        first = sb("first", [P, GT, NE])
        second = sb("second", [P, GT, NE])
        best = sb("best", [P, GT])
        col = sb("col", [P, 4, GT])
        gap = sb("gap", [P, GT])
        fn = sb("fn", [P, GT, NE])
        w_tok = sb("w_tok", [P, GT, NE])
        w_t = sb("w_t", [NE, 2 if cfg.b2 else 1, GN])
        w_parts = sb("w_parts", [P, 2, GN], F32R)
        std = sb("std", [P, TILES])
        stats = sb("stats", [P, GT, 6])
        mv = sb("mv", [P, GT, 2])

        g_ps = pb("g_ps", [P, 2, GN])
        u_ps = pb("u_ps", [P, 2, GN]) if cfg.gated else None
        w_ps = pb("w_ps", [P, 2, GN])
        y_ps = pb("y_ps", [P, GN])
        side = pb("side", [P, GN])

        def age(c):
            return [d for d in range(1, n + 1) if (c - d) % n % HIDDEN == c % HIDDEN][0]

        block = local.enter_context(nc.Block())

        @block.tensor
        def _(pe):
            def turn_x(g, buf):
                pe.wait_ge(done["normed"], at["normed"] + g + 1)
                pe.wait_ge(done["x_updated"], at["x_updated"] + g - 2)
                for t in range(GT):
                    mm = nc.tensor.transpose(side[:, t * P:(t + 1) * P], xn[:, buf, t, :], core.ident[:, :])
                mm.then_inc(done["x_turned"], 1)

            def logits(g, buf):
                pe.wait_ge(done["xt_ready"], at["xt_ready"] + g + 1)
                for t in range(GT):
                    mm = nc.tensor.matmul(side[:, t * NE:(t + 1) * NE], xt[:, t * P:(t + 1) * P],
                                          io["w_router"], start=True, stop=True)
                mm.then_inc(done["logits"], 1)

            def turn_w(g):
                pe.wait_ge(done["routed"], at["routed"] + g + 1)
                for t in range(GT):
                    mm = nc.tensor.transpose(side[0:NE, t * P:(t + 1) * P], w_tok[:, t, :], core.ident[:, :])
                mm.then_inc(done["w_turned"], 1)

            def turn_y(g):
                pe.wait_ge(done["y_out"], at["y_out"] + g + 1)
                pe.wait_ge(done["x_updated"], at["x_updated"] + g)
                ahead = min(g + 3, GROUPS) if isinstance(g, int) else g + 3
                pe.wait_ge(done["parts_ready"], at["parts_ready"] + ahead)
                for t in range(GT):
                    mm = nc.tensor.transpose(side[:, t * P:(t + 1) * P], y_sb[:, t * P:(t + 1) * P],
                                             core.ident[:, :])
                mm.then_inc(done["y_turned"], 1)

            def times_x(to, name, buf, c):
                cols = slice(c * P, (c + 1) * P)
                hi, lo = io[name + "_hi"][:, cols], io[name + "_lo"][:, cols]
                nc.tensor.matmul(to, hi, xt_hi[:, buf, :], start=True, stop=False)
                nc.tensor.matmul(to, hi, xt_lo[:, buf, :], start=False, stop=False)
                return nc.tensor.matmul(to, lo, xt_hi[:, buf, :], start=False, stop=True)

            def project(g, buf, c):
                k = g * n + c
                if c == 0:
                    pe.wait_ge(done["xt_split"], at["xt_split"] + g + 1)
                pe.wait_ge(done["activated"], at["activated"] + k - 1)
                times_x(g_ps[:, c % 2, :], "w_in", buf, c).then_inc(done["projected"], 1)
                if cfg.gated:
                    pe.wait_ge(done["gated"], at["gated"] + k - 1)
                    times_x(u_ps[:, c % 2, :], "w_up", buf, c).then_inc(done["up_projected"], 1)

            def spread(g, buf, c):
                if c == 0:
                    pe.wait_ge(done["parts_ready"], at["parts_ready"] + g + 1)
                if c % per == 0:
                    s = c // per
                    pe.wait_ge(done["weighted"], at["weighted"] + g * n + c - per)
                    nc.tensor.matmul(w_ps[:, s % 2, :], io["pick"][:, s, :], w_parts[:, buf, :],
                                     start=True, stop=True).then_inc(done["spread"], 1)

            def add(g, buf, c):
                k = g * n + c
                if c == 0:
                    pe.wait_ge(done["y_out"], at["y_out"] + g)
                    if cfg.b2:
                        nc.tensor.matmul(y_ps[:, :], io["b_out"], w_t[:, buf, :], start=True, stop=False)
                hi, lo = io["w_out_hi"][:, c, :], io["w_out_lo"][:, c, :]
                pe.wait_ge(done["hid_hi"], at["hid_hi"] + k + 1)
                nc.tensor.matmul(y_ps[:, :], hi, hid_hi[:, c % HIDDEN, :], start=(c == 0 and not cfg.b2), stop=False)
                nc.tensor.matmul(y_ps[:, :], lo, hid_hi[:, c % HIDDEN, :], start=False, stop=False)
                pe.wait_ge(done["hid_lo"], at["hid_lo"] + k + 1)
                nc.tensor.matmul(y_ps[:, :], hi, hid_lo[:, c % HIDDEN, :], start=False, stop=(c == n - 1))\
                    .then_inc(done["summed"], 1)

            def body(g, buf):
                last = is_group(g, GROUPS - 1)
                for c in range(n):
                    if c + cfg.spread_ahead < n:
                        spread(g, buf, c + cfg.spread_ahead)
                    elif not last:
                        spread(g + 1, 1 - buf, c + cfg.spread_ahead - n)
                    if c + cfg.ahead < n:
                        project(g, buf, c + cfg.ahead)
                    elif not last:
                        project(g + 1, 1 - buf, c + cfg.ahead - n)
                    add(g, buf, c)
                    if c == cfg.times.turn_x and not last:
                        turn_x(g + 1, 1 - buf)
                    if c == cfg.times.logits and not last:
                        logits(g + 1, 1 - buf)
                    if c == cfg.times.turn_w and not last:
                        turn_w(g + 1)
                    if c == cfg.times.turn_y and not is_group(g, 0):
                        turn_y(g - 1)

            for s, v in loaded:
                pe.wait_ge(s, v)
            turn_x(0, 0)
            logits(0, 0)
            for c in range(2):
                project(0, 0, c)
            turn_w(0)
            for c in range(cfg.spread_ahead):
                spread(0, 0, c)
            for c in range(2, cfg.ahead):
                project(0, 0, c)
            in_pairs(pe, body)
            turn_y(GROUPS - 1)

        @block.scalar
        def _(act_eng):
            def xt_out(g, buf):
                act_eng.wait_ge(done["x_turned"], at["x_turned"] + g + 1)
                act_eng.wait_ge(done["xt_split"], at["xt_split"] + g)
                nc.scalar.activation(xt_hi[:, buf, :], side[:, :], ACT.Copy)
                nc.scalar.activation(xt[:, :], side[:, :], ACT.Copy).then_inc(done["xt_ready"], 1)

            def route_fn(g):
                if cfg.top == 2:
                    act_eng.wait_ge(done["gap_ready"], at["gap_ready"] + g + 1)
                    nc.scalar.activation(fn[:, :, 0], gap[:, :], ACT.Tanh, scale=0.5)\
                        .then_inc(done["fn_ready"], 1)
                elif cfg.times_prob:
                    act_eng.wait_ge(done["gap_ready"], at["gap_ready"] + g + 1)
                    nc.scalar.activation(fn[:, :, :], others[:, :, :], ACT.Exp).then_inc(done["fn_ready"], 1)

            def y_out(g):
                act_eng.wait_ge(done["summed"], at["summed"] + (g + 1) * n)
                act_eng.wait_ge(done["y_turned"], at["y_turned"] + g)
                nc.scalar.activation(y_sb[:, :], y_ps[:, :], ACT.Copy).then_inc(done["y_out"], 1)

            def activate(g, c):
                k = g * n + c
                act_eng.wait_ge(done["projected"], at["projected"] + k + 1)
                if cfg.gated:
                    act_eng.wait_ge(done["gated"], at["gated"] + k - 1)
                else:
                    act_eng.wait_ge(done["weighted"], at["weighted"] + k - acts + 1)
                bias = io["b_in"][:, c:c + 1] if cfg.b1 else 0.0
                nc.scalar.activation(act[:, c % acts, :], g_ps[:, c % 2, :], cfg.act, bias=bias)\
                    .then_inc(done["activated"], 1)

            def high(g, c):
                k = g * n + c
                act_eng.wait_ge(done["weighted"], at["weighted"] + k + 1)
                act_eng.wait_ge(done["summed"], at["summed"] + k - age(c) + 1)
                nc.scalar.activation(hid_hi[:, c % HIDDEN, :], hid[:, c % HIDDEN, :], ACT.Copy)\
                    .then_inc(done["hid_hi"], 1)

            def body(g, buf):
                last = is_group(g, GROUPS - 1)
                for c in range(n):
                    activate(g, c)
                    if cfg.high_on_act and c >= cfg.high_behind:
                        high(g, c - cfg.high_behind)
                    elif cfg.high_on_act and not is_group(g, 0):
                        high(g - 1, n + c - cfg.high_behind)
                    if c == cfg.times.y and not is_group(g, 0):
                        y_out(g - 1)
                    if c == cfg.times.xt and not last:
                        xt_out(g + 1, 1 - buf)
                    if c == cfg.times.fn and not last:
                        route_fn(g + 1)

            act_eng.wait_ge(done["std_in"], at["std_in"] + 1)
            nc.scalar.activation(std[:, :], std[:, :], ACT.Sqrt).then_inc(done["std"], 1)
            for s, v in loaded:
                act_eng.wait_ge(s, v)
            xt_out(0, 0)
            route_fn(0)
            in_pairs(act_eng, body)
            if cfg.high_on_act:
                for c in range(n - cfg.high_behind, n):
                    high(GROUPS - 1, c)
            y_out(GROUPS - 1)

        @block.vector
        def _(dve):
            V = nc.vector

            def per_token(ap):
                return ap.unsqueeze(2).broadcast_to([P, GT, NE])

            def norm(g, buf):
                dve.wait_ge(done["x_turned"], at["x_turned"] + g - 1)
                for t in range(GT):
                    i = g * GT + t
                    ins = V.tensor_scalar(xn[:, buf, t, :], core.x[:, bass.ds(i, 1), :],
                                          core.mean_var[:, bass.ds(i, 1), 0], core.rstd[:, bass.ds(i, 1)],
                                          ALU.subtract, ALU.mult)
                ins.then_inc(done["normed"], 1)

            def one_hot(link, values, out):
                link(V.tensor_reduce(col[:, 0, :], values, AX, ALU.max))
                link(V.tensor_tensor(hits[:, :, :], values, per_token(col[:, 0, :]), ALU.is_equal))
                link(V.tensor_tensor(hits[:, :, :], hits[:, :, :], io["falling"], ALU.mult))
                link(V.tensor_reduce(col[:, 1, :], hits[:, :, :], AX, ALU.max))
                link(V.tensor_tensor(out, hits[:, :, :], per_token(col[:, 1, :]), ALU.is_equal))

            def route_a(g):
                dve.wait_ge(done["logits"], at["logits"] + g + 1)
                dve.wait_ge(done["w_turned"], at["w_turned"] + g)
                link = Link(dve, done["route_step"], at["route_step"] + g * cfg.route_steps)
                got = side[:, 0:GT * NE].rearrange("p (t e) -> p t e", e=NE)
                if cfg.br:
                    link(V.tensor_tensor(logit[:, :, :], got, io["b_router"], ALU.add))
                else:
                    link(V.tensor_copy(logit[:, :, :], got))
                one_hot(link, logit[:, :, :], first[:, :, :])
                return link

            def route_b(g, link):
                if cfg.top == 2:
                    link(V.tensor_copy(best[:, :], col[:, 0, :]))
                    link(V.tensor_scalar(others[:, :, :], first[:, :, :], -1.0, 1.0, ALU.mult, ALU.add))
                    link(V.tensor_tensor(others[:, :, :], others[:, :, :], logit[:, :, :], ALU.mult))
                    link(V.scalar_tensor_tensor(others[:, :, :], first[:, :, :], -3e38, others[:, :, :],
                                                ALU.mult, ALU.add))

            def route_c(g, link):
                if cfg.top == 2:
                    one_hot(link, others[:, :, :], second[:, :, :])
                    V.tensor_tensor(gap[:, :], best[:, :], col[:, 0, :], ALU.subtract)\
                        .then_inc(done["gap_ready"], 1)
                elif cfg.times_prob:
                    V.tensor_tensor(others[:, :, :], logit[:, :, :], per_token(col[:, 0, :]), ALU.subtract)\
                        .then_inc(done["gap_ready"], 1)
                else:
                    V.tensor_copy(w_tok[:, :, :], first[:, :, :]).then_inc(done["routed"], 1)

            def combine(g, link):
                if cfg.top == 2:
                    dve.wait_ge(done["fn_ready"], at["fn_ready"] + g + 1)
                    link(V.tensor_scalar(col[:, 2, :], fn[:, :, 0], 0.5, 0.5, ALU.mult, ALU.add))
                    link(V.tensor_scalar(col[:, 3, :], fn[:, :, 0], -0.5, 0.5, ALU.mult, ALU.add))
                    link(V.tensor_tensor(first[:, :, :], first[:, :, :], per_token(col[:, 2, :]), ALU.mult))
                    link(V.tensor_tensor(second[:, :, :], second[:, :, :], per_token(col[:, 3, :]), ALU.mult))
                    V.tensor_tensor(w_tok[:, :, :], first[:, :, :], second[:, :, :], ALU.add)\
                        .then_inc(done["routed"], 1)
                elif cfg.times_prob:
                    dve.wait_ge(done["fn_ready"], at["fn_ready"] + g + 1)
                    link(V.tensor_reduce(col[:, 2, :], fn[:, :, :], AX, ALU.add))
                    link(V.reciprocal(col[:, 3, :], col[:, 2, :]))
                    V.tensor_tensor(w_tok[:, :, :], first[:, :, :], per_token(col[:, 3, :]), ALU.mult)\
                        .then_inc(done["routed"], 1)

            def weights_out(g, buf, link):
                dve.wait_ge(done["w_turned"], at["w_turned"] + g + 1)
                high, low = (w_parts[r:r + NE, buf, :] for r in PART_ROWS)
                row = w_t[:, buf if cfg.b2 else 0, :]
                link(V.tensor_copy(row, side[0:NE, :]))
                if cfg.whole:
                    V.tensor_copy(high, row).then_inc(done["parts_ready"], 1)
                else:
                    link(V.tensor_copy(high, row))
                    V.tensor_tensor(low, row, high.bitcast(F32), ALU.subtract)\
                        .then_inc(done["parts_ready"], 1)

            def update_x(g):
                dve.wait_ge(done["y_turned"], at["y_turned"] + g + 1)
                link = Link(dve, done["update_step"], at["update_step"] + g * UPDATE_STEPS)
                x4 = core.x[:, bass.ds(g * GT, GT), :]
                link(V.tensor_tensor(x4, x4, side[:, :].rearrange("p (t d) -> p t d", d=D), ALU.add))
                dve.sem_inc(core.passed, 1)
                for t in range(GT):
                    ins = V.bn_stats(stats[:, t, :], core.x[:, bass.ds(g * GT + t, 1), :])
                link(ins)
                dve.sem_inc(core.passed, 1)
                for t in range(GT):
                    ins = V.bn_aggr(mv[:, t, :], stats[:, t, :])
                link(ins)
                V.tensor_copy(core.mean_var[:, bass.ds(g * GT, GT), :], mv[:, :, :])\
                    .then_inc(done["x_updated"], 1)

            def split_xt(g, buf):
                dve.wait_ge(done["xt_ready"], at["xt_ready"] + g + 1)
                V.tensor_tensor(xt_lo[:, buf, :], xt[:, :], xt_hi[:, buf, :].bitcast(F32), ALU.subtract)\
                    .then_inc(done["xt_split"], 1)

            def gate(g, c):
                k = g * n + c
                dve.wait_ge(done["activated"], at["activated"] + k + 1)
                dve.wait_ge(done["up_projected"], at["up_projected"] + k + 1)
                dve.wait_ge(done["weighted"], at["weighted"] + k - 1)
                V.tensor_tensor(prod[:, c % 2, :], act[:, c % acts, :], u_ps[:, c % 2, :], ALU.mult)\
                    .then_inc(done["gated"], 1)

            def weight(g, c):
                k = g * n + c
                if cfg.gated:
                    dve.wait_ge(done["gated"], at["gated"] + k + 1)
                    got = prod[:, c % 2, :]
                else:
                    dve.wait_ge(done["activated"], at["activated"] + k + 1)
                    got = act[:, c % acts, :]
                dve.wait_ge(done["spread"], at["spread"] + g * cfg.spreads + c // per + 1)
                dve.wait_ge(done["hid_lo"], at["hid_lo"] + k - age(c) + 1)
                V.tensor_tensor(hid[:, c % HIDDEN, :], got, w_ps[:, (c // per) % 2, :], ALU.mult)\
                    .then_inc(done["weighted"], 1)
                if not cfg.high_on_act:
                    dve.wait_ge(done["weighted"], at["weighted"] + k + 1)
                    dve.wait_ge(done["summed"], at["summed"] + k - age(c) + 1)
                    V.tensor_copy(hid_hi[:, c % HIDDEN, :], hid[:, c % HIDDEN, :]).then_inc(done["hid_hi"], 1)

            def body(g, buf):
                last = is_group(g, GROUPS - 1)
                for c in range(n):
                    if cfg.gated and c + cfg.drained < n:
                        gate(g, c + cfg.drained)
                    elif cfg.gated and not last:
                        gate(g + 1, c + cfg.drained - n)
                    weight(g, c)
                    if c == cfg.times.split_xt and not last:
                        split_xt(g + 1, 1 - buf)
                    if c == cfg.times.route[0] and not last:
                        link = route_a(g + 1)
                    if c == cfg.times.route[1] and not last:
                        route_b(g + 1, link)
                    if c == cfg.times.route[2] and not last:
                        route_c(g + 1, link)
                    if c == cfg.times.combine and not last:
                        combine(g + 1, link)
                    if c == cfg.times.weights and not last:
                        weights_out(g + 1, 1 - buf, link)
                    if c == cfg.times.update and not is_group(g, 0):
                        update_x(g - 1)
                    if c == cfg.times.norm and not is_group(g, GROUPS - 2, GROUPS - 1):
                        norm(g + 2, buf)

            V.tensor_scalar(std[:, :], core.mean_var[:, :, 1], LN_EPS, None, ALU.add).then_inc(done["std_in"], 1)
            V.memset(act[:, 0, :], 0.0).then_inc(done["cleared"], 1)
            V.memset(act[:, 1, :], 1.0).then_inc(done["cleared"], 1)
            dve.wait_ge(done["cleared"], at["cleared"] + 2)
            for buf in range(2):
                ins = V.tensor_copy(w_parts[:, buf, :], act[:, 0, :])
            ins.then_inc(done["cleared"], 1)
            dve.wait_ge(done["cleared"], at["cleared"] + 3)
            if cfg.shared:
                for buf in range(2):
                    V.tensor_copy(w_parts[SHARED_ROW:SHARED_ROW + 1, buf, :], act[SHARED_ROW:SHARED_ROW + 1, 1, :])
            dve.wait_ge(done["std"], at["std"] + 1)
            V.reciprocal(core.rstd[:, :], std[:, :]).then_inc(done["rstd"], 1)
            dve.wait_ge(done["rstd"], at["rstd"] + 1)
            for s, v in loaded:
                dve.wait_ge(s, v)
            norm(0, 0)
            norm(1, 1)
            split_xt(0, 0)
            link = route_a(0)
            route_b(0, link)
            route_c(0, link)
            combine(0, link)
            weights_out(0, 0, link)
            if cfg.gated:
                for c in range(cfg.drained):
                    gate(0, c)
            in_pairs(dve, body)
            update_x(GROUPS - 1)

        @block.gpsimd
        def _(pool):
            def body(g, buf):
                for c in range(n):
                    k = g * n + c
                    pool.wait_ge(done["hid_hi"], at["hid_hi"] + k + 1)
                    nc.gpsimd.tensor_tensor(hid_lo[:, c % HIDDEN, :], hid[:, c % HIDDEN, :],
                                            hid_hi[:, c % HIDDEN, :].bitcast(F32), ALU.subtract)\
                        .then_inc(done["hid_lo"], 1)

            in_pairs(pool, body)

        @block.sync
        def _(sp):
            if out is None:
                return
            for g in range(GROUPS):
                sp.wait_ge(done["x_updated"], at["x_updated"] + g + 1)
                sp.dma_start(out[g * GN:(g + 1) * GN, :].rearrange("(t p) d -> p t d", p=P),
                             core.x[:, g * GT:(g + 1) * GT, :]).then_inc(core.out_done, 16)
            sp.wait_ge(core.out_done, 16 * GROUPS)

    counts = {"projected": GROUPS * n, "activated": GROUPS * n, "weighted": GROUPS * n, "summed": GROUPS * n,
              "hid_hi": GROUPS * n, "hid_lo": GROUPS * n,
              "spread": GROUPS * cfg.spreads, "route_step": GROUPS * cfg.route_steps,
              "update_step": GROUPS * UPDATE_STEPS, "std_in": 1, "std": 1, "rstd": 1, "cleared": 3,
              "up_projected": GROUPS * n * cfg.gated, "gated": GROUPS * n * cfg.gated,
              "gap_ready": GROUPS * (not cfg.whole), "fn_ready": GROUPS * (not cfg.whole)}
    core.expert_signals.phase_ends(counts, GROUPS)


EXPERT_SIGNALS = {
    "PE": ("x_turned", "logits", "w_turned", "y_turned", "projected", "up_projected", "spread", "summed"),
    "ACT": ("xt_ready", "fn_ready", "y_out", "activated", "std"),
    "DVE": ("normed", "routed", "parts_ready", "x_updated", "gated", "weighted", "std_in", "rstd",
            "cleared", "route_step", "update_step", "gap_ready", "xt_split", "hid_hi"),
    "Pool": ("hid_lo",),
}


H0 = 8
HD0 = D // H0
PAIRS0 = H0 // 2
MASKED = -1e30


def over_slots(eng, step):
    for slot in range(SLOTS):
        step(slot, slot, 0)
    with eng.Fori(1, TILES // SLOTS - 1) as quad:
        for slot in range(SLOTS):
            step(quad * SLOTS + slot, slot, quad)
    for slot in range(SLOTS):
        step(TILES - SLOTS + slot, slot, TILES // SLOTS - 1)


def split_load(core, sp, phase, i, b):
    weights, words = core.splits[phase]
    signals = core.split_signals
    sp.wait_ge(signals.done["low"], signals.at()["low"] + i - 1)
    sp.sem_inc(core.passed, 1)
    sp.dma_start(core.slices[:, b, 0:words], weights[:, bass.ds(i * words, words)]).then_inc(core.slice_in[b], 16)


def split_high(core, act_eng, phase, i, b, pair):
    _, words = core.splits[phase]
    act_eng.wait_ge(core.slice_in[b], (pair + core.slices_before + 1) * 16)
    core.nc.scalar.activation(core.weights_high[:, bass.ds(i * words, words)], core.slices[:, b, 0:words], ACT.Copy)\
        .then_inc(core.split_signals.done["high"], 1)


def split_low(core, pool, phase, i, b):
    _, words = core.splits[phase]
    signals = core.split_signals
    pool.wait_ge(signals.done["high"], signals.at()["high"] + i + 1)
    pool.sem_inc(core.passed, 1)
    part = bass.ds(i * words, words)
    core.nc.gpsimd.tensor_tensor(core.weights_low[:, part], core.slices[:, b, 0:words],
                                 core.weights_high[:, part].bitcast(F32), ALU.subtract)\
        .then_inc(signals.done["low"], 1)


def up_to_last(j):
    return min(j, TILES - 1) if isinstance(j, int) else j


def is_tile(j, *which):
    return isinstance(j, int) and j in which


def new_rstd(core, std, act_eng=None, dve=None):
    nc, done, at = core.nc, core.attention_signals.done, core.attention_signals.at()
    if act_eng is not None:
        act_eng.wait_ge(done["std_in"], at["std_in"] + 1)
        nc.scalar.activation(std[:, :], std[:, :], ACT.Sqrt).then_inc(done["std"], 1)
    if dve is not None:
        nc.vector.tensor_scalar(std[:, :], core.mean_var[:, :, 1], LN_EPS, None, ALU.add)\
            .then_inc(done["std_in"], 1)
        dve.wait_ge(done["std"], at["std"] + 1)
        nc.vector.reciprocal(core.rstd[:, :], std[:, :]).then_inc(done["rstd"], 1)
        dve.wait_ge(done["rstd"], at["rstd"] + 1)


def add_to_x(core, dve, link, j, result, stats, mv):
    V = core.nc.vector
    xj = core.x[:, bass.ds(j, 1), :]
    link(V.tensor_tensor(xj, xj, result, ALU.add))
    dve.sem_inc(core.passed, 1)
    link(V.bn_stats(stats[:, :], xj))
    dve.sem_inc(core.passed, 1)
    link(V.bn_aggr(mv[:, :], stats[:, :]))
    V.tensor_copy(core.mean_var[:, bass.ds(j, 1), :], mv[:, :].unsqueeze(1))\
        .then_inc(core.attention_signals.done["updated"], 1)


ADD_STEPS = 3
ATTENTION_SIGNALS = {
    "PE": ("x_turned", "projected", "v_projected", "scored", "p_turned", "pv_done", "o_turned", "final",
           "q_projected", "setup"),
    "ACT": ("xt_ready", "v_ready", "exped", "pt_ready", "ot_ready", "std", "qt_ready",
            "null_ready"),
    "DVE": ("normed", "proj_read", "s_read", "shifted", "o_ready", "updated", "std_in", "rstd", "cleared",
            "soft_step", "o_step", "add_step", "k_ready", "y_stats", "y_step"),
    "Pool": ("pool_setup", "pool_var", "y_rstd", "q_ready"),
}


def l0_attention(core, io, loaded, out=None):
    nc = core.nc
    done, at = core.attention_signals.done, core.attention_signals.at()
    scale = float(HD0) ** -0.5

    with ExitStack() as local:
        def sb(name, shape, dt=F32):
            return local.enter_context(nc.sbuf_tensor("l0a_" + name, shape, dt))

        def pb(name, shape):
            return local.enter_context(nc.psum_tensor("l0a_" + name, shape, F32))

        ctx_sb = sb("ctx", [P, SLOTS, 4, 2, S])
        mask_q = sb("mask_q", [P, B * S])
        mask_k = sb("mask_k", [P, TILES, S])
        xn = sb("xn", [P, SLOTS, D])
        xt = sb("xt", [P, SLOTS, P])
        qt = sb("qt", [P, P])
        k_diag = sb("k_diag", [P, 2, H0, S])
        v_diag = sb("v_diag", [P, 2, 2, PAIRS0, 2, HD0 + 1])
        s_sb = sb("s_sb", [P, H0, S])
        probs = sb("probs", [P, H0, S])
        top = sb("top", [P, H0])
        pt = sb("pt", [P, PAIRS0, P])
        o_sb = sb("o_sb", [P, H0, HD0])
        inv = sb("inv", [P, H0])
        ot = sb("ot", [P, P])
        ones = sb("ones", [1, P])
        std = sb("std", [P, TILES])
        stats = sb("stats", [P, 6])
        mv = sb("mv", [P, 2])

        picks_raw = [sb(f"pick_{i}", list(dram.shape)) for i, (_, dram) in enumerate(core.picks)]

        x_ps = pb("x_ps", [P, 512])
        qk_ps = pb("qk_ps", [P, 512])
        v_ps = pb("v_ps", [P, 512])
        s_ps = pb("s_ps", [P, H0, S])
        pt_ps = pb("pt_ps", [P, PAIRS0, P])
        o_ps = pb("o_ps", [P, 512])
        ot_ps = pb("ot_ps", [P, 512])
        y_ps = pb("y_ps", [P, 512])
        o_view = o_ps[:, 0:H0 * (HD0 + 1)].rearrange("p (h d) -> p h d", d=HD0 + 1)
        loads_before = core.slot_loads
        masks_in = core.masks_in

        block = local.enter_context(nc.Block())

        @block.sync
        def _(sp):
            sp.dma_start(mask_q[:, :], core.dram["mask"].rearrange("b s -> (b s)").unsqueeze(0)
                         .broadcast_to([P, B * S])).then_inc(masks_in, 16)
            for b in range(2):
                keys = core.dram["mask"].rearrange("(j b) s -> b j s", b=2)[b:b + 1, :, :]
                sp.dma_start(mask_k[b * S:(b + 1) * S, :, :], keys.broadcast_to([S, TILES, S]))\
                    .then_inc(masks_in, 16)

            def step(j, slot, quad):
                sp.wait_ge(done["v_projected"], at["v_projected"] + j - 3)
                sp.sem_inc(core.passed, 1)
                src = core.dram["ctx_t"][:, bass.ds(j, 1), :, :].rearrange("p j h (b s) -> p (j h b) s", b=2)
                for copy in range(2):
                    sp.dma_start(ctx_sb[:, slot, :, copy, :], src).then_inc(core.slot_in[slot], 16)
                if is_tile(j, SLOTS - 1):
                    for dst, src, semaphore in core.later_loads:
                        sp.dma_start(dst, src).then_inc(semaphore, 16)
                if slot % 2 == 0 and not is_tile(j, *range(SLOTS)):
                    split_load(core, sp, 1, (quad - 1) * 2 + slot // 2, slot // 2)

            over_slots(sp, step)
            for b in range(2):
                split_load(core, sp, 1, SPLIT_SLICES - 2 + b, b)
            for raw, (_, dram) in zip(picks_raw, core.picks):
                sp.dma_start(raw[:], dram[:]).then_inc(core.picks_in, 16)

        @block.tensor
        def _(pe):
            mmul = nc.tensor.matmul

            def context_here(slot, quad):
                pe.wait_ge(core.slot_in[slot], (quad * 2 + loads_before + 2) * 16)

            def turn_x(i, slot):
                pe.wait_ge(done["normed"], at["normed"] + i + 1)
                pe.wait_ge(done["xt_ready"], at["xt_ready"] + i)
                nc.tensor.transpose(x_ps[:, 0:P], xn[:, slot, :], core.ident[:, :]).then_inc(done["x_turned"], 1)

            def project_qk(i, slot, quad):
                pe.wait_ge(done["xt_ready"], at["xt_ready"] + i + 1)
                pe.wait_ge(done["proj_read"], at["proj_read"] + i)
                context_here(slot, quad)
                mmul(qk_ps[:, 0:P], io["w_q"], xt[:, slot, :], start=True, stop=True)
                for half in range(2):
                    mm = mmul(qk_ps[:, P:2 * P], io["w_k"][:, half, :], ctx_sb[:, slot, 2 * half:2 * half + 2, 0, :],
                              start=(half == 0), stop=(half == 1))
                mm.then_inc(done["projected"], 1)

            def project_v(i, slot):
                pe.wait_ge(done["v_ready"], at["v_ready"] + i)
                for b in range(2):
                    for half in range(2):
                        tok = ctx_sb[:, slot, 2 * half + b, :, :]
                        mm = mmul(v_ps[:, b * P:(b + 1) * P], tok, io["w_v"][:, half, :],
                                  start=(half == 0), stop=(half == 1))
                mm.then_inc(done["v_projected"], 1)

            def scores(j):
                pe.wait_ge(done["proj_read"], at["proj_read"] + j + 1)
                pe.wait_ge(done["s_read"], at["s_read"] + j)
                for b in range(2):
                    mm = mmul(s_ps[b * S:(b + 1) * S, :, :], qt[:, b * S:(b + 1) * S], k_diag[:, b, :, :],
                              start=True, stop=True)
                mm.then_inc(done["scored"], 1)

            def turn_p(j):
                pe.wait_ge(done["exped"], at["exped"] + j + 1)
                pe.wait_ge(done["pt_ready"], at["pt_ready"] + j)
                for c in range(PAIRS0):
                    mm = nc.tensor.transpose(pt_ps[:, c, :], probs[:, 2 * c:2 * c + 2, :], core.ident[:, :])
                mm.then_inc(done["p_turned"], 1)

            def weigh_v(j, slot):
                pe.wait_ge(done["pt_ready"], at["pt_ready"] + j + 1)
                pe.wait_ge(done["v_ready"], at["v_ready"] + j + 1)
                pe.wait_ge(done["o_ready"], at["o_ready"] + j)
                for c in range(PAIRS0):
                    for b in range(2):
                        mm = mmul(o_ps[b * S:(b + 1) * S, c * 2 * (HD0 + 1):(c + 1) * 2 * (HD0 + 1)],
                                  pt[:, c, b * S:(b + 1) * S], v_diag[:, slot % 2, b, c, :, :], start=True, stop=True)
                mm.then_inc(done["pv_done"], 1)

            def turn_o(j):
                pe.wait_ge(done["o_ready"], at["o_ready"] + j + 1)
                pe.wait_ge(done["ot_ready"], at["ot_ready"] + j)
                nc.tensor.transpose(ot_ps[:, 0:P], o_sb[:, :, :], core.ident[:, :]).then_inc(done["o_turned"], 1)

            def final(i, slot):
                pe.wait_ge(done["ot_ready"], at["ot_ready"] + i + 1)
                pe.wait_ge(done["add_step"], at["add_step"] + ADD_STEPS * (i - 1) + 1)
                mmul(y_ps[:, 0:D], xt[:, slot, :], io["w_o"][:, 0, :], start=True, stop=False)
                mmul(y_ps[:, 0:D], ot[:, :], io["w_o"][:, 1, :], start=False, stop=False)
                mmul(y_ps[:, 0:D], ones[:, :], io["b_o"], start=False, stop=True).then_inc(done["final"], 1)

            def step(j, slot, quad):
                to_start = is_tile(j, -2, -1)
                if not is_tile(j, -2, TILES - 1):
                    scores(j + 1)
                    project_v(j + 1, (slot + 1) % SLOTS)
                if not (to_start or is_tile(j, 0)):
                    turn_o(j - 1)
                if not to_start:
                    turn_p(j)
                if not is_tile(j, TILES - 2, TILES - 1):
                    project_qk(j + 2, (slot + 2) % SLOTS, quad + (slot + 2) // SLOTS)
                if not (to_start or is_tile(j, 0)):
                    final(j - 1, (slot - 1) % SLOTS)
                if not is_tile(j, TILES - 3, TILES - 2, TILES - 1):
                    turn_x(j + 3, (slot + 3) % SLOTS)
                if not to_start:
                    weigh_v(j, slot)

            for s, v in loaded:
                pe.wait_ge(s, v)
            turn_x(0, 0)
            step(-2, 2, -1)
            step(-1, 3, -1)
            over_slots(pe, step)
            turn_o(TILES - 1)
            final(TILES - 1, SLOTS - 1)

        @block.scalar
        def _(act_eng):
            A = nc.scalar

            def xt_out(j, slot):
                act_eng.wait_ge(done["x_turned"], at["x_turned"] + j + 1)
                act_eng.wait_ge(done["final"], at["final"] + j - 3)
                A.activation(xt[:, slot, :], x_ps[:, 0:P], ACT.Copy).then_inc(done["xt_ready"], 1)

            def v_out(j, buf):
                act_eng.wait_ge(done["v_projected"], at["v_projected"] + j + 1)
                act_eng.wait_ge(done["pv_done"], at["pv_done"] + j - 1)
                for b in range(2):
                    for h in range(2):
                        rows = slice(h * S, (h + 1) * S)
                        src = v_ps[rows, b * P:(b + 1) * P].rearrange("p (c h d) -> p c h d", h=2, d=HD0)
                        ins = A.activation(v_diag[rows, buf, b, :, h, 0:HD0], src[:, :, h, :], ACT.Copy)
                ins.then_inc(done["v_ready"], 1)

            def pt_out(j):
                act_eng.wait_ge(done["p_turned"], at["p_turned"] + j + 1)
                act_eng.wait_ge(done["pv_done"], at["pv_done"] + j)
                A.activation(pt[:, :, :], pt_ps[:, :, :], ACT.Copy).then_inc(done["pt_ready"], 1)

            def ot_out(j):
                act_eng.wait_ge(done["o_turned"], at["o_turned"] + j + 1)
                act_eng.wait_ge(done["final"], at["final"] + j)
                A.activation(ot[:, :], ot_ps[:, 0:P], ACT.Identity, bias=io["b_v"]).then_inc(done["ot_ready"], 1)

            def exps(j):
                act_eng.wait_ge(done["shifted"], at["shifted"] + j + 1)
                act_eng.wait_ge(done["p_turned"], at["p_turned"] + j)
                A.activation(probs[:, :, :], s_sb[:, :, :], ACT.Exp, scale=scale).then_inc(done["exped"], 1)

            def step(j, slot, quad):
                to_start = is_tile(j, -2, -1)
                if not is_tile(j, -2, TILES - 1):
                    v_out(j + 1, (slot + 1) % 2)
                if not (to_start or is_tile(j, 0)):
                    ot_out(j - 1)
                if not to_start:
                    pt_out(j)
                if not is_tile(j, -2, TILES - 1):
                    exps(j + 1)
                if not is_tile(j, TILES - 3, TILES - 2, TILES - 1):
                    xt_out(j + 3, (slot + 3) % SLOTS)
                if slot % 2 == 1 and not is_tile(j, -1):
                    split_high(core, act_eng, 1, quad * 2 + slot // 2, slot // 2, quad)

            new_rstd(core, std, act_eng=act_eng)
            for s, v in loaded:
                act_eng.wait_ge(s, v)
            act_eng.wait_ge(done["cleared"], at["cleared"] + 3)
            xt_out(0, 0)
            step(-2, 2, -1)
            step(-1, 3, -1)
            over_slots(act_eng, step)
            ot_out(TILES - 1)
            act_eng.wait_ge(core.picks_in, 16 * len(core.picks))
            for raw, (pick, _) in zip(picks_raw, core.picks):
                A.activation(pick[:], raw[:], ACT.Copy)

        @block.gpsimd
        def _(pool):
            def step(j, slot, quad):
                if slot % 2 == 1:
                    split_low(core, pool, 1, quad * 2 + slot // 2, slot // 2)

            over_slots(pool, step)

        @block.vector
        def _(dve):
            V = nc.vector

            def norm(j, slot):
                dve.wait_ge(done["x_turned"], at["x_turned"] + j - 3)
                V.tensor_scalar(xn[:, slot, :], core.x[:, bass.ds(j, 1), :], core.mean_var[:, bass.ds(j, 1), 0],
                                core.rstd[:, bass.ds(j, 1)], ALU.subtract, ALU.mult).then_inc(done["normed"], 1)

            def qk_out(j):
                dve.wait_ge(done["projected"], at["projected"] + j + 1)
                dve.wait_ge(done["scored"], at["scored"] + j)
                V.scalar_tensor_tensor(qt[:, :], qk_ps[:, 0:P], io["b_q"], mask_q[:, bass.ds(j * P, P)],
                                       ALU.add, ALU.mult)
                head = io["heads"].unsqueeze(2).broadcast_to([P, H0, S])
                for b in range(2):
                    keys = qk_ps[:, P + b * S:P + (b + 1) * S].unsqueeze(1).broadcast_to([P, H0, S])
                    ins = V.scalar_tensor_tensor(k_diag[:, b, :, :], keys, io["b_k"], head, ALU.add, ALU.mult)
                ins.then_inc(done["proj_read"], 1)

            def soften(j):
                dve.wait_ge(done["scored"], at["scored"] + j + 1)
                dve.wait_ge(done["exped"], at["exped"] + j)
                link = Link(dve, done["soft_step"], at["soft_step"] + j)
                neg = mask_k[:, bass.ds(j, 1), :].broadcast_to([P, H0, S])
                V.tensor_tensor(s_sb[:, :, :], s_ps[:, :, :], neg, ALU.add).then_inc(done["s_read"], 1)
                dve.wait_ge(done["s_read"], at["s_read"] + j + 1)
                link(V.tensor_reduce(top[:, :], s_sb[:, :, :], AX, ALU.max))
                V.tensor_tensor(s_sb[:, :, :], s_sb[:, :, :], top[:, :].unsqueeze(2).broadcast_to([P, H0, S]),
                                ALU.subtract).then_inc(done["shifted"], 1)

            def scale_o(j):
                dve.wait_ge(done["pv_done"], at["pv_done"] + j + 1)
                dve.wait_ge(done["o_turned"], at["o_turned"] + j)
                link = Link(dve, done["o_step"], at["o_step"] + j)
                link(V.reciprocal(inv[:, :], o_view[:, :, HD0]))
                V.tensor_tensor(o_sb[:, :, :], o_view[:, :, 0:HD0],
                                inv[:, :].unsqueeze(2).broadcast_to([P, H0, HD0]), ALU.mult)\
                    .then_inc(done["o_ready"], 1)

            def update(j):
                dve.wait_ge(done["final"], at["final"] + j + 1)
                link = Link(dve, done["add_step"], at["add_step"] + j * ADD_STEPS)
                add_to_x(core, dve, link, j, y_ps[:, 0:D], stats, mv)

            def step(j, slot, quad):
                to_start = is_tile(j, -2, -1)
                if not is_tile(j, -2, TILES - 1):
                    soften(j + 1)
                if not is_tile(j, TILES - 2, TILES - 1):
                    qk_out(j + 2)
                if not (to_start or is_tile(j, 0)):
                    update(j - 1)
                if not to_start:
                    scale_o(j)
                if not (to_start or is_tile(j, *range(TILES - SLOTS, TILES))):
                    norm(j + 4, slot)

            V.memset(v_diag[:, :, :, :, :, :], 0.0).then_inc(done["cleared"], 1)
            V.memset(ones[:, :], 1.0)
            dve.wait_ge(done["cleared"], at["cleared"] + 1)
            for h in range(2):
                ins = V.memset(v_diag[h * S:(h + 1) * S, :, :, :, h, HD0], 1.0)
                ins.then_inc(done["cleared"], 1)
            new_rstd(core, std, dve=dve)
            for s, v in loaded:
                dve.wait_ge(s, v)
            dve.wait_ge(masks_in, 48)
            V.tensor_scalar(mask_k[:, :, :], mask_k[:, :, :], 0.0, MASKED, ALU.is_equal, ALU.mult)\
                .then_inc(done["cleared"], 1)
            for i in range(SLOTS):
                norm(i, i)
            dve.wait_ge(done["cleared"], at["cleared"] + 4)
            step(-2, 2, -1)
            step(-1, 3, -1)
            over_slots(dve, step)
            update(TILES - 1)

    core.attention_signals.phase_ends({
        **{name: TILES for name in ("x_turned", "projected", "v_projected", "scored", "p_turned", "pv_done",
                                    "o_turned", "final", "xt_ready", "v_ready", "exped", "pt_ready", "ot_ready",
                                    "normed", "proj_read", "s_read", "shifted", "o_ready", "updated",
                                    "soft_step", "o_step")},
        "std_in": 1, "std": 1, "rstd": 1, "cleared": 4, "add_step": TILES * ADD_STEPS}, 0)
    core.slot_loads += 2 * TILES // SLOTS
    if out is not None:
        store_x(core, out)


def store_x(core, out):
    nc = core.nc
    with nc.Block() as block:
        @block.sync
        def _(sp):
            sp.dma_start(out.rearrange("(t p) d -> p t d", p=P), core.x[:, :, :]).then_inc(core.out_done, 16)
            sp.wait_ge(core.out_done, 16)


H1 = 16
HD1 = 64
PAIRS1 = H1 // 2
HALF = PAIRS1 // 2
OUT_PIECES = ((0, 3), (3, 3), (6, 2))
L1_EPS = 1e-6
Y_STEPS = 2 + ADD_STEPS


def l1_attention(core, io, loaded, out=None):
    nc = core.nc
    done, at = core.attention_signals.done, core.attention_signals.at()
    scale = float(HD1) ** -0.5

    with ExitStack() as local:
        def sb(name, shape, dt=F32):
            return local.enter_context(nc.sbuf_tensor("l1a_" + name, shape, dt))

        ctx_sb = sb("ctx", [P, SLOTS, 2, P])
        xn = sb("xn", [P, SLOTS, D])
        xt = sb("xt", [P, 2, P])
        qt = sb("qt", [P, PAIRS1, P])
        k_diag = sb("k_diag", [P, PAIRS1, 2, 2, S])
        v_sb = sb("v_sb", [P, 2, 2, PAIRS1, HD1 + 1])
        v_diag = sb("v_diag", [P, 2, 2, 2, PAIRS1, HD1 + 1])
        s_sb = sb("s_sb", [P, H1, S])
        probs = sb("probs", [P, H1, S])
        top = sb("top", [P, H1])
        null = sb("null", [P, 2, H1])
        pt = sb("pt", [P, PAIRS1, P])
        den = sb("den", [P, H1])
        inv = sb("inv", [P, H1])
        o_sb = sb("o_sb", [P, H1, HD1])
        ot = sb("ot", [P, PAIRS1, P])
        ones = sb("ones", [1, P])
        row = sb("row", [1, D])
        std = sb("std", [P, TILES])
        stats = sb("stats", [P, 6])
        mv = sb("mv", [P, 2])
        y_stats = sb("y_stats", [P, 6])
        y_mv = sb("y_mv", [P, 2])
        y_var = sb("y_var", [P, 1])
        y_rstd = sb("y_rstd", [P, 1])
        minus_half = sb("minus_half", [P, 1])
        eps = sb("eps", [P, 1])
        y_sb = sb("y_sb", [P, 1, D])
        act_ps = local.enter_context(nc.psum_tensor("l1a_act_ps", [P, 2, 512], F32))
        dve_ps = local.enter_context(nc.psum_tensor("l1a_dve_ps", [P, 4, 512], F32))
        s_ps = local.enter_context(nc.psum_tensor("l1a_s_ps", [P, 2, 512], F32))
        loads_before = core.slot_loads
        v_in = core.v_in

        def out_piece(i):
            first, n = OUT_PIECES[i]
            view = dve_ps[:, i + 1, 0:n * 2 * (HD1 + 1)].rearrange("p (h d) -> p h d", d=HD1 + 1)
            return view, 2 * first, 2 * n

        block = local.enter_context(nc.Block())

        @block.sync
        def _(sp):
            def load(i, slot):
                sp.wait_ge(done["v_projected"], at["v_projected"] + 2 * (i - 3))
                sp.sem_inc(core.passed, 1)
                sp.dma_start(ctx_sb[:, slot, :, :], core.dram["ctx_t"][:, bass.ds(i, 1), :, :]
                             .rearrange("p j h t -> p (j h) t")).then_inc(core.slot_in[slot], 16)

            def spread(i, buf):
                sp.wait_ge(done["v_ready"], at["v_ready"] + 2 * (i + 1))
                sp.sem_inc(core.passed, 1)
                sp.wait_ge(done["pv_done"], at["pv_done"] + i - 1)
                for b in range(2):
                    for h in range(2):
                        sp.dma_start(v_diag[h * S:(h + 1) * S, buf, b, h, :, :],
                                     v_sb[b * S:(b + 1) * S, buf, h, :, :]).then_inc(v_in[buf], 16)

            def step(j, slot, quad):
                if not is_tile(j, TILES - 1):
                    spread(j + 1, (slot + 1) % 2)
                if not is_tile(j, *range(TILES - SLOTS, TILES)):
                    load(j + SLOTS, slot)
                if slot % 2 == 0:
                    split_load(core, sp, 3, quad * 2 + slot // 2, slot // 2)

            for i in range(SLOTS):
                load(i, i)
            sp.wait_ge(done["cleared"], at["cleared"] + 3)
            spread(0, 0)
            over_slots(sp, step)

        @block.tensor
        def _(pe):
            mmul = nc.tensor.matmul

            def turn_x(i, slot):
                pe.wait_ge(done["normed"], at["normed"] + i + 1)
                pe.wait_ge(done["qt_ready"], at["qt_ready"] + 2 * (i - 1))
                pe.wait_ge(done["xt_ready"], at["xt_ready"] + i)
                nc.tensor.transpose(act_ps[:, 0, 0:P], xn[:, slot, :], core.ident[:, :])\
                    .then_inc(done["x_turned"], 1)

            def project_q(i, slot, p):
                pe.wait_ge(done["xt_ready"], at["xt_ready"] + i + 1)
                pe.wait_ge(done["ot_ready"], at["ot_ready"] + 2 * (i - 3) + p + 1)
                if is_tile(i, 0, 1):
                    pe.wait_ge(done["qt_ready"], at["qt_ready"] + 2 * (i - 1) + p + 1)
                    pe.wait_ge(done["xt_ready"], at["xt_ready"] + i + 2)
                if is_tile(i, 2):
                    pe.wait_ge(done["pt_ready"], at["pt_ready"] + p + 1)
                for c in range(HALF):
                    cols = slice((p * HALF + c) * P, (p * HALF + c + 1) * P)
                    mm = mmul(act_ps[:, 1 - p, c * P:(c + 1) * P], io["w_q"][:, cols], xt[:, slot % 2, :],
                              start=True, stop=True)
                mm.then_inc(done["q_projected"], 1)

            def project_k(i, slot, quad, p):
                if p == 0:
                    pe.wait_ge(core.slot_in[slot], (quad + loads_before + 1) * 16)
                pe.wait_ge(done["o_ready"], at["o_ready"] + 3 * (i - 3) + 2 + p)
                for c in range(HALF):
                    col = (p * HALF + c) * P
                    for half in range(2):
                        mm = mmul(dve_ps[:, 2 + p, c * P:(c + 1) * P], io["w_k"][:, half, col:col + P],
                                  ctx_sb[:, slot, half, :], start=(half == 0), stop=(half == 1))
                mm.then_inc(done["projected"], 1)

            def project_v(i, slot, p):
                if p == 0:
                    pe.wait_ge(done["add_step"], at["add_step"] + Y_STEPS * (i - 3) + 1)
                else:
                    pe.wait_ge(done["o_ready"], at["o_ready"] + 3 * (i - 2) + 1)
                if is_tile(i, 1, 2):
                    pe.wait_ge(done["v_ready"], at["v_ready"] + 2 * (i - 1) + p + 1)
                for half in range(2):
                    mm = mmul(dve_ps[:, p, :], ctx_sb[:, slot, half, :], io["w_v"][:, half, p * 512:(p + 1) * 512],
                              start=(half == 0), stop=(half == 1))
                mm.then_inc(done["v_projected"], 1)

            def scores(i, p):
                pe.wait_ge(done["qt_ready"], at["qt_ready"] + 2 * i + p + 1)
                pe.wait_ge(done["k_ready"], at["k_ready"] + 2 * i + p + 1)
                pe.wait_ge(done["shifted"], at["shifted"] + 2 * (i - 1) + p + 1)
                for c in range(HALF):
                    for b in range(2):
                        mm = mmul(s_ps[b * S:(b + 1) * S, p, c * P:(c + 1) * P],
                                  qt[:, p * HALF + c, b * S:(b + 1) * S], k_diag[:, p * HALF + c, b, :, :],
                                  start=True, stop=True)
                mm.then_inc(done["scored"], 1)

            def turn_p(j, p):
                pe.wait_ge(done["exped"], at["exped"] + 2 * j + p + 1)
                if p == 0 or is_tile(j, TILES - 3, TILES - 2, TILES - 1):
                    pe.wait_ge(done["qt_ready"], at["qt_ready"] + 2 * up_to_last(j + 1) + p + 1)
                if p == 1:
                    pe.wait_ge(done["xt_ready"], at["xt_ready"] + up_to_last(j + 3) + 1)
                if is_tile(j, TILES - 1):
                    pe.wait_ge(done["ot_ready"], at["ot_ready"] + 2 * (j - 2) + p + 1)
                for c in range(HALF):
                    h = 2 * (p * HALF + c)
                    mm = nc.tensor.transpose(act_ps[:, 1 - p, c * P:(c + 1) * P], probs[:, h:h + 2, :],
                                             core.ident[:, :])
                mm.then_inc(done["p_turned"], 1)

            def turn_o(i, p):
                pe.wait_ge(done["o_ready"], at["o_ready"] + 3 * i + 2 + p)
                pe.wait_ge(done["pt_ready"], at["pt_ready"] + 2 * up_to_last(i + 1) + p + 1)
                if is_tile(i, TILES - 1):
                    pe.wait_ge(done["ot_ready"], at["ot_ready"] + 2 * (i - 1) + p + 1)
                for c in range(HALF):
                    h = 2 * (p * HALF + c)
                    mm = nc.tensor.transpose(act_ps[:, 1 - p, c * P:(c + 1) * P], o_sb[:, h:h + 2, :],
                                             core.ident[:, :])
                mm.then_inc(done["o_turned"], 1)

            def final(i):
                pe.wait_ge(done["v_ready"], at["v_ready"] + 2 * up_to_last(i + 2) + 1)
                if is_tile(i, TILES - 2, TILES - 1):
                    pe.wait_ge(done["updated"], at["updated"] + i)
                y = dve_ps[:, 0, 0:D]
                for c in range(PAIRS1):
                    if c % HALF == 0:
                        pe.wait_ge(done["ot_ready"], at["ot_ready"] + 2 * i + c // HALF + 1)
                    mmul(y, ot[:, c, :], io["w_o"][:, c, :], start=(c == 0), stop=False)
                mmul(y, ones[:, :], row[:, :], start=False, stop=True).then_inc(done["final"], 1)

            def weigh_v(j, slot, quad):
                buf = slot % 2
                pe.wait_ge(done["pt_ready"], at["pt_ready"] + 2 * (j + 1))
                pe.wait_ge(v_in[buf], (quad * 2 + slot // 2 + 1) * 64)
                pe.wait_ge(done["v_ready"], at["v_ready"] + 2 * (up_to_last(j + 1) + 1))
                pe.wait_ge(done["o_ready"], at["o_ready"] + 3 * j)
                for i, (first, n) in enumerate(OUT_PIECES):
                    if i > 0:
                        pe.wait_ge(done["k_ready"], at["k_ready"] + 2 * up_to_last(j + 2) + i)
                    for c in range(n):
                        for b in range(2):
                            w = 2 * (HD1 + 1)
                            mm = mmul(dve_ps[b * S:(b + 1) * S, i + 1, c * w:(c + 1) * w],
                                      pt[:, first + c, b * S:(b + 1) * S],
                                      v_diag[:, buf, b, :, first + c, :], start=True, stop=True)
                mm.then_inc(done["pv_done"], 1)

            def step(j, slot, quad):
                to_start = is_tile(j, -2, -1)
                v_next = is_tile(j, -2, TILES - 1)
                qk_next = is_tile(j, TILES - 2, TILES - 1)
                if not v_next:
                    scores(j + 1, 0)
                    scores(j + 1, 1)
                if not is_tile(j, TILES - 3, TILES - 2, TILES - 1):
                    turn_x(j + 3, (slot + 3) % SLOTS)
                for p in range(2):
                    if not to_start:
                        turn_p(j, p)
                    if not v_next:
                        project_v(j + 1, (slot + 1) % SLOTS, p)
                for p in range(2):
                    if not (to_start or is_tile(j, 0)):
                        turn_o(j - 1, p)
                    if not qk_next:
                        project_k(j + 2, (slot + 2) % SLOTS, quad + (slot + 2) // SLOTS, p)
                if not qk_next:
                    project_q(j + 2, (slot + 2) % SLOTS, 0)
                if not (to_start or is_tile(j, 0)):
                    final(j - 1)
                if not qk_next:
                    project_q(j + 2, (slot + 2) % SLOTS, 1)
                if not to_start:
                    weigh_v(j, slot, quad)

            for s, v in loaded:
                pe.wait_ge(s, v)
            for c in range(PAIRS1):
                mm = mmul(dve_ps[0:1, 0, 0:D], io["null_v"], io["w_o"][:, c, :], start=(c == 0),
                          stop=(c == PAIRS1 - 1))
            mm.then_inc(done["setup"], 1)
            pe.wait_ge(done["cleared"], at["cleared"] + 4)
            turn_x(0, 0)
            step(-2, 2, -1)
            step(-1, 3, -1)
            over_slots(pe, step)
            turn_o(TILES - 1, 0)
            turn_o(TILES - 1, 1)
            final(TILES - 1)

        @block.scalar
        def _(act_eng):
            A = nc.scalar

            def halves_of(p):
                return slice(p * HALF, (p + 1) * HALF), slice(p * H1 // 2, (p + 1) * H1 // 2)

            def xt_out(i, slot):
                act_eng.wait_ge(done["x_turned"], at["x_turned"] + i + 1)
                act_eng.wait_ge(done["q_projected"], at["q_projected"] + 2 * (i - 1))
                A.activation(xt[:, slot % 2, :], act_ps[:, 0, 0:P], ACT.Copy).then_inc(done["xt_ready"], 1)

            def pt_out(j, p):
                act_eng.wait_ge(done["p_turned"], at["p_turned"] + 2 * j + p + 1)
                act_eng.wait_ge(done["pv_done"], at["pv_done"] + j)
                A.activation(pt[:, halves_of(p)[0], :], act_ps[:, 1 - p, :], ACT.Copy).then_inc(done["pt_ready"], 1)

            def ot_out(i, p):
                act_eng.wait_ge(done["o_turned"], at["o_turned"] + 2 * i + p + 1)
                act_eng.wait_ge(done["final"], at["final"] + i)
                A.activation(ot[:, halves_of(p)[0], :], act_ps[:, 1 - p, :], ACT.Copy).then_inc(done["ot_ready"], 1)

            def qt_out(i, p):
                act_eng.wait_ge(done["q_projected"], at["q_projected"] + 2 * i + p + 1)
                act_eng.wait_ge(done["scored"], at["scored"] + 2 * i)
                A.activation(qt[:, halves_of(p)[0], :], act_ps[:, 1 - p, :], ACT.Copy).then_inc(done["qt_ready"], 1)

            def exps(i, slot, p):
                heads = halves_of(p)[1]
                act_eng.wait_ge(done["shifted"], at["shifted"] + 2 * i + p + 1)
                act_eng.wait_ge(done["p_turned"], at["p_turned"] + 2 * (i - 1) + p + 1)
                A.activation(probs[:, heads, :], s_sb[:, heads, :], ACT.Exp, scale=scale).then_inc(done["exped"], 1)
                if p == 1:
                    act_eng.wait_ge(done["o_ready"], at["o_ready"] + 3 * (i - 1))
                    A.activation(null[:, slot % 2, :], top[:, :], ACT.Exp, scale=-scale).then_inc(done["null_ready"], 1)

            def step(j, slot, quad):
                to_start = is_tile(j, -2, -1)
                if not is_tile(j, TILES - 3, TILES - 2, TILES - 1):
                    xt_out(j + 3, (slot + 3) % SLOTS)
                if not to_start:
                    pt_out(j, 0)
                    pt_out(j, 1)
                for p in range(2):
                    if not (to_start or is_tile(j, 0)):
                        ot_out(j - 1, p)
                    if not is_tile(j, -2, TILES - 1):
                        exps(j + 1, (slot + 1) % SLOTS, p)
                if not is_tile(j, TILES - 2, TILES - 1):
                    qt_out(j + 2, 0)
                    qt_out(j + 2, 1)
                if slot % 2 == 1 and not is_tile(j, -1):
                    split_high(core, act_eng, 3, quad * 2 + slot // 2, slot // 2, quad)

            new_rstd(core, std, act_eng=act_eng)
            xt_out(0, 0)
            step(-2, 2, -1)
            step(-1, 3, -1)
            over_slots(act_eng, step)
            ot_out(TILES - 1, 0)
            ot_out(TILES - 1, 1)

        @block.gpsimd
        def _(pool):
            G = nc.gpsimd
            G.memset(minus_half[:, :], -0.5).then_inc(done["pool_setup"], 1)
            G.memset(eps[:, :], L1_EPS).then_inc(done["pool_setup"], 1)
            pool.wait_ge(done["pool_setup"], at["pool_setup"] + 2)

            def step(j, slot, quad):
                pool.wait_ge(done["y_stats"], at["y_stats"] + j + 1)
                pool.wait_ge(done["updated"], at["updated"] + j)
                G.tensor_tensor(y_var[:, :], y_mv[:, 1:2], eps[:, :], ALU.add).then_inc(done["pool_var"], 1)
                pool.wait_ge(done["pool_var"], at["pool_var"] + j + 1)
                G.tensor_tensor(y_rstd[:, :], y_var[:, :], minus_half[:, :], ALU.pow).then_inc(done["y_rstd"], 1)
                if slot % 2 == 1:
                    split_low(core, pool, 3, quad * 2 + slot // 2, slot // 2)

            over_slots(pool, step)

        @block.vector
        def _(dve):
            V = nc.vector

            def norm(i, slot):
                dve.wait_ge(done["x_turned"], at["x_turned"] + i - 3)
                V.tensor_scalar(xn[:, slot, :], core.x[:, bass.ds(i, 1), :], core.mean_var[:, bass.ds(i, 1), 0],
                                core.rstd[:, bass.ds(i, 1)], ALU.subtract, ALU.mult).then_inc(done["normed"], 1)

            def k_out(i):
                dve.wait_ge(done["scored"], at["scored"] + 2 * i)
                for p in range(2):
                    dve.wait_ge(done["projected"], at["projected"] + 2 * i + p + 1)
                    for h in range(2):
                        rows = slice(h * S, (h + 1) * S)
                        src = dve_ps[rows, 2 + p, :].rearrange("p (c b s) -> p c b s", c=HALF, b=2)
                        ins = V.tensor_scalar(k_diag[rows, p * HALF:(p + 1) * HALF, :, h, :], src,
                                              io["null_k"][rows, :], None, ALU.subtract)
                    ins.then_inc(done["k_ready"], 1)

            def v_out(i, slot, quad):
                dve.wait_ge(v_in[slot % 2], (quad * 2 + slot // 2) * 64)
                for p in range(2):
                    dve.wait_ge(done["v_projected"], at["v_projected"] + 2 * i + p + 1)
                    V.tensor_tensor(v_sb[:, slot % 2, p, :, 0:HD1],
                                    dve_ps[:, p, :].rearrange("p (c d) -> p c d", d=HD1),
                                    io["null_v_row"].unsqueeze(1).broadcast_to([P, PAIRS1, HD1]), ALU.subtract)\
                        .then_inc(done["v_ready"], 1)

            def soften(j):
                link = Link(dve, done["soft_step"], at["soft_step"] + 2 * j)
                dve.wait_ge(done["null_ready"], at["null_ready"] + j)
                for p in range(2):
                    dve.wait_ge(done["scored"], at["scored"] + 2 * j + p + 1)
                    hs = slice(p * H1 // 2, (p + 1) * H1 // 2)
                    ins = V.tensor_reduce(top[:, hs], s_ps[:, p, :].rearrange("p (h s) -> p h s", s=S), AX, ALU.max)
                link(ins)
                link(V.tensor_scalar(top[:, :], top[:, :], 0.0, None, ALU.max))
                for p in range(2):
                    hs = slice(p * H1 // 2, (p + 1) * H1 // 2)
                    ins = V.tensor_tensor(s_sb[:, hs, :], s_ps[:, p, :].rearrange("p (h s) -> p h s", s=S),
                                          top[:, hs].unsqueeze(2).broadcast_to([P, H1 // 2, S]), ALU.subtract)
                    ins.then_inc(done["shifted"], 1)

            def scale_o(j, slot):
                dve.wait_ge(done["pv_done"], at["pv_done"] + j + 1)
                dve.wait_ge(done["null_ready"], at["null_ready"] + j + 1)
                dve.wait_ge(done["o_turned"], at["o_turned"] + 2 * j)
                link = Link(dve, done["o_step"], at["o_step"] + 2 * j)
                for i in range(3):
                    view, h0, n = out_piece(i)
                    ins = V.tensor_tensor(den[:, h0:h0 + n], view[:, :, HD1], null[:, slot % 2, h0:h0 + n],
                                          ALU.add)
                link(ins)
                link(V.reciprocal(inv[:, :], den[:, :]))
                for i in range(3):
                    view, h0, n = out_piece(i)
                    V.tensor_tensor(o_sb[:, h0:h0 + n, :], view[:, :, 0:HD1],
                                    inv[:, h0:h0 + n].unsqueeze(2).broadcast_to([P, n, HD1]), ALU.mult)\
                        .then_inc(done["o_ready"], 1)

            def y_statistics(j):
                dve.wait_ge(done["final"], at["final"] + j + 1)
                dve.wait_ge(done["y_rstd"], at["y_rstd"] + j)
                V.bn_stats(y_stats[:, :], dve_ps[:, 0, 0:D]).then_inc(done["y_step"], 1)
                dve.wait_ge(done["y_step"], at["y_step"] + j + 1)
                dve.sem_inc(core.passed, 1)
                V.bn_aggr(y_mv[:, :], y_stats[:, :]).then_inc(done["y_stats"], 1)

            def update(j):
                dve.wait_ge(done["y_stats"], at["y_stats"] + j + 1)
                dve.wait_ge(done["y_rstd"], at["y_rstd"] + j + 1)
                link = Link(dve, done["add_step"], at["add_step"] + j * Y_STEPS)
                xj = core.x[:, bass.ds(j, 1), :]
                y = dve_ps[:, 0, 0:D].unsqueeze(1)
                link(V.scalar_tensor_tensor(y_sb[:, :, :], y, y_mv[:, 0:1], io["ln_scale"].unsqueeze(1),
                                            ALU.subtract, ALU.mult))
                link(V.scalar_tensor_tensor(y_sb[:, :, :], y_sb[:, :, :], y_rstd[:, :],
                                            io["ln_bias"].unsqueeze(1), ALU.mult, ALU.add))
                add_to_x(core, dve, link, j, y_sb[:, 0, :], stats, mv)

            def step(j, slot, quad):
                to_start = is_tile(j, -2, -1)
                if not is_tile(j, -2, TILES - 1):
                    soften(j + 1)
                    v_out(j + 1, (slot + 1) % SLOTS, quad + (slot + 1) // SLOTS)
                if not is_tile(j, TILES - 2, TILES - 1):
                    k_out(j + 2)
                if not (to_start or is_tile(j, 0)):
                    y_statistics(j - 1)
                if not (to_start or is_tile(j, *range(TILES - SLOTS, TILES))):
                    norm(j + 4, slot)
                if not (to_start or is_tile(j, 0)):
                    update(j - 1)
                if not to_start:
                    scale_o(j, slot)

            V.memset(v_diag[:, :, :, :, :, :], 0.0).then_inc(done["cleared"], 1)
            V.memset(k_diag[:, :, :, :, :], 0.0).then_inc(done["cleared"], 1)
            V.memset(ones[:, :], 1.0)
            V.memset(v_sb[:, :, :, :, :], 1.0).then_inc(done["cleared"], 1)
            new_rstd(core, std, dve=dve)
            for s, v in loaded:
                dve.wait_ge(s, v)
            dve.wait_ge(done["setup"], at["setup"] + 1)
            V.tensor_copy(row[:, :], dve_ps[0:1, 0, 0:D]).then_inc(done["cleared"], 1)
            dve.wait_ge(done["cleared"], at["cleared"] + 4)
            for i in range(SLOTS):
                norm(i, i)
            step(-2, 2, -1)
            step(-1, 3, -1)
            over_slots(dve, step)
            y_statistics(TILES - 1)
            update(TILES - 1)

    one, two = TILES, 2 * TILES
    core.attention_signals.phase_ends({
        "x_turned": one, "q_projected": two, "projected": two, "v_projected": two, "scored": two,
        "p_turned": two, "pv_done": one, "o_turned": two, "final": one, "setup": 1,
        "xt_ready": one, "qt_ready": two, "pt_ready": two, "ot_ready": two, "exped": two, "null_ready": one,
        "std": 1, "std_in": 1, "rstd": 1, "cleared": 4, "normed": one, "shifted": two, "k_ready": two,
        "v_ready": two, "o_ready": 3 * TILES, "soft_step": two, "o_step": two, "y_stats": one, "y_step": one,
        "updated": one, "add_step": Y_STEPS * TILES, "pool_setup": 2, "pool_var": one, "y_rstd": one}, 0)
    core.slot_loads += TILES // SLOTS
    if out is not None:
        store_x(core, out)


RMS_EPS2 = 1e-5
LOG_P = -0.001


def l2_depool(core, io, loaded, out=None):
    nc = core.nc
    done, at = core.depool_signals.done, core.depool_signals.at()

    with ExitStack() as local:
        def sb(name, shape, dt=F32):
            return local.enter_context(nc.sbuf_tensor("l2d_" + name, shape, dt))

        def pb(name, shape):
            return local.enter_context(nc.psum_tensor("l2d_" + name, shape, F32))

        lens = sb("lens", [B, S], I32)
        count = sb("count", [B, S])
        ones_row = sb("ones_row", [B, S])
        last = sb("last", [B, S])
        wrap = sb("wrap", [B, S])
        plug = sb("plug", [B, S])
        cube = sb("cube", [B, S, S])
        all_ones = sb("all_ones", [B, S])
        spread_m = sb("spread_m", [P, TILES, P])
        w_in = sb("w_in", [P, D])
        ms = sb("ms", [P, TILES])
        std = sb("std", [P, TILES])
        xn = sb("xn", [P, 2, GT, D])
        xt = sb("xt", [P, 2, GN])
        ctx_sb = sb("ctx", [P, 2, GT, CTX])
        squares = sb("squares", [P, CTX])
        ssq = sb("ssq", [P, GT])
        msq = sb("msq", [P, GT])
        scale_c = sb("scale_c", [P, GT])
        minus_half = sb("minus_half", [P, GT])
        patch = sb("patch", [P, 2, GT, D])
        y_sb = sb("y_sb", [P, GN])
        stats = sb("stats", [P, GT, 6])
        mv = sb("mv", [P, GT, 2])
        m_ps = pb("m_ps", [P, 2, 512])
        x_ps = pb("x_ps", [P, GN])
        y_ps = pb("y_ps", [P, 2, GN])
        t_ps = pb("t_ps", [P, GN])
        base = core.ctx_loads

        block = local.enter_context(nc.Block())

        @block.sync
        def _(sp):
            sp.dma_start(lens[:, :], core.dram["lens"]).then_inc(core.lens_in, 16)
            tokens = core.dram["ctx_tok"].rearrange("(t p) f -> p t f", p=P)

            def body(g, buf):
                sp.wait_ge(done["patches"], at["patches"] + g - 1)
                sp.sem_inc(core.passed, 1)
                sp.dma_start(ctx_sb[:, buf, :, :], tokens[:, bass.ds(g * GT, GT), :]).then_inc(core.ctx_in[buf], 16)
                if not is_group(g, 0):
                    for b in range(2):
                        split_load(core, sp, 5, (g - 1) * 2 + b, b)

            in_pairs(sp, body)
            for b in range(2):
                split_load(core, sp, 5, SPLIT_SLICES - 2 + b, b)

        @block.tensor
        def _(pe):
            mmul = nc.tensor.matmul

            def turn_x(g, buf):
                pe.wait_ge(done["normed"], at["normed"] + g + 1)
                pe.wait_ge(done["xt_ready"], at["xt_ready"] + g)
                for t in range(GT):
                    mm = nc.tensor.transpose(x_ps[:, t * P:(t + 1) * P], xn[:, buf, t, :], core.ident[:, :])
                mm.then_inc(done["x_turned"], 1)

            def mix(g, buf):
                pe.wait_ge(done["xt_ready"], at["xt_ready"] + g + 1)
                pe.wait_ge(done["patches"], at["patches"] + g + 1)
                pe.wait_ge(done["y_out"], at["y_out"] + g - 1)
                for t in range(GT):
                    to = y_ps[:, buf, t * P:(t + 1) * P]
                    mmul(to, w_in[:, :], xt[:, buf, t * P:(t + 1) * P], start=True, stop=False)
                    mm = mmul(to, patch[:, buf, t, :], spread_m[:, bass.ds(g * GT + t, 1), :]
                              .rearrange("p a s -> p (a s)"), start=False, stop=True)
                mm.then_inc(done["mixed"], 1)

            def turn_y(g):
                pe.wait_ge(done["y_out"], at["y_out"] + g + 1)
                pe.wait_ge(done["updated"], at["updated"] + g)
                for t in range(GT):
                    mm = nc.tensor.transpose(t_ps[:, t * P:(t + 1) * P], y_sb[:, t * P:(t + 1) * P], core.ident[:, :])
                mm.then_inc(done["y_turned"], 1)

            def body(g, buf):
                if not is_group(g, GROUPS - 1):
                    turn_x(g + 1, 1 - buf)
                mix(g, buf)
                if not is_group(g, 0):
                    turn_y(g - 1)

            for s, v in loaded:
                pe.wait_ge(s, v)
            pe.wait_ge(done["plugged"], at["plugged"] + 1)
            flat = cube[:, :, :].rearrange("p b s -> p (b s)")
            for n in range(8):
                pe.wait_ge(done["compared"], at["compared"] + n - 1)
                mmul(m_ps[0:S, n % 2, :], all_ones[:, :], flat[:, n * 512:(n + 1) * 512], start=True, stop=True)\
                    .then_inc(done["spread"], 1)
            for n in range(8):
                pe.wait_ge(done["compared"], at["compared"] + 8)
                pe.wait_ge(done["m_out"], at["m_out"] + n - 1)
                mmul(m_ps[:, n % 2, :], io["decay"], flat[:, n * 512:(n + 1) * 512], start=True, stop=True)\
                    .then_inc(done["m_made"], 1)
            turn_x(0, 0)
            pe.wait_ge(done["m_out"], at["m_out"] + 8)
            in_pairs(pe, body)
            turn_y(GROUPS - 1)

        @block.scalar
        def _(act_eng):
            A = nc.scalar

            def y_out(g, buf):
                act_eng.wait_ge(done["mixed"], at["mixed"] + g + 1)
                act_eng.wait_ge(done["y_turned"], at["y_turned"] + g)
                A.activation(y_sb[:, :], y_ps[:, buf, :], ACT.Identity, bias=io["b_in"]).then_inc(done["y_out"], 1)

            def xt_out(g, buf):
                act_eng.wait_ge(done["x_turned"], at["x_turned"] + g + 1)
                act_eng.wait_ge(done["mixed"], at["mixed"] + g - 1)
                A.activation(xt[:, buf, :], x_ps[:, :], ACT.Copy).then_inc(done["xt_ready"], 1)

            def group(g, buf, pair):
                if not is_group(g, GROUPS - 1):
                    xt_out(g + 1, 1 - buf)
                if not is_group(g, GROUPS - 2, GROUPS - 1):
                    squares_of(g + 2, buf, pair + 1)
                y_out(g, buf)
                for b in range(2):
                    split_high(core, act_eng, 5, g * 2 + b, b, g)

            def squares_of(g, buf, pair):
                act_eng.wait_ge(core.ctx_in[buf], (pair + base + 1) * 16)
                act_eng.wait_ge(done["msq"], at["msq"] + g)
                for t in range(GT):
                    A.activation(squares[:, :], ctx_sb[:, buf, t, :], ACT.Square, accum_out=ssq[:, t:t + 1])\
                        .then_inc(done["square_step"], 1)
                    act_eng.wait_ge(done["square_step"], at["square_step"] + g * GT + t + 1)

            act_eng.wait_ge(done["std_in"], at["std_in"] + 1)
            A.activation(std[:, :], std[:, :], ACT.Sqrt).then_inc(done["std"], 1)
            act_eng.wait_ge(done["std_in"], at["std_in"] + 2)
            A.activation(ms[:, :], ms[:, :], ACT.Sqrt).then_inc(done["std"], 1)
            for s, v in loaded:
                act_eng.wait_ge(s, v)
            squares_of(0, 0, 0)
            squares_of(1, 1, 0)
            xt_out(0, 0)
            group(0, 0, 0)
            group(1, 1, 0)
            with act_eng.Fori(1, GROUPS // 2 - 1) as pair:
                group(pair * 2, 0, pair)
                group(pair * 2 + 1, 1, pair)
            group(GROUPS - 2, 0, GROUPS // 2 - 1)
            group(GROUPS - 1, 1, GROUPS // 2 - 1)

        @block.gpsimd
        def _(pool):
            G = nc.gpsimd
            G.memset(minus_half[:, :], -0.5).then_inc(done["pool_setup"], 1)
            pool.wait_ge(done["pool_setup"], at["pool_setup"] + 1)

            def scales(g):
                pool.wait_ge(done["msq"], at["msq"] + g + 1)
                pool.wait_ge(done["patches"], at["patches"] + g)
                G.tensor_tensor(scale_c[:, :], msq[:, :], minus_half[:, :], ALU.pow).then_inc(done["scale_c"], 1)

            def body(g, buf):
                if not is_group(g, GROUPS - 2, GROUPS - 1):
                    scales(g + 2)
                for b in range(2):
                    split_low(core, pool, 5, g * 2 + b, b)

            scales(0)
            scales(1)
            in_pairs(pool, body)

        @block.vector
        def _(dve):
            V = nc.vector

            def norm(g, buf):
                dve.wait_ge(done["x_turned"], at["x_turned"] + g - 1)
                for t in range(GT):
                    i = g * GT + t
                    ins = V.tensor_scalar(xn[:, buf, t, :], core.x[:, bass.ds(i, 1), :],
                                          core.mean_var[:, bass.ds(i, 1), 0], core.rstd[:, bass.ds(i, 1)],
                                          ALU.subtract, ALU.mult)
                ins.then_inc(done["normed"], 1)

            def mean_squares(g):
                dve.wait_ge(done["square_step"], at["square_step"] + (g + 1) * GT)
                dve.wait_ge(done["scale_c"], at["scale_c"] + g)
                V.tensor_scalar(msq[:, :], ssq[:, :], 1.0 / CTX, RMS_EPS2, ALU.mult, ALU.add)\
                    .then_inc(done["msq"], 1)

            def patches(g, buf):
                dve.wait_ge(done["scale_c"], at["scale_c"] + g + 1)
                dve.wait_ge(done["mixed"], at["mixed"] + g - 1)
                for t in range(GT):
                    ins = V.scalar_tensor_tensor(patch[:, buf, t, :], ctx_sb[:, buf, t, 0:D], scale_c[:, t:t + 1],
                                                 io["g_init"], ALU.mult, ALU.mult)
                ins.then_inc(done["patches"], 1)

            def update(g):
                dve.wait_ge(done["y_turned"], at["y_turned"] + g + 1)
                link = Link(dve, done["update_step"], at["update_step"] + g * UPDATE_STEPS)
                x4 = core.x[:, bass.ds(g * GT, GT), :]
                link(V.tensor_tensor(x4, x4, t_ps[:, :].rearrange("p (t d) -> p t d", d=D), ALU.add))
                dve.sem_inc(core.passed, 1)
                for t in range(GT):
                    ins = V.bn_stats(stats[:, t, :], core.x[:, bass.ds(g * GT + t, 1), :])
                link(ins)
                dve.sem_inc(core.passed, 1)
                for t in range(GT):
                    ins = V.bn_aggr(mv[:, t, :], stats[:, t, :])
                link(ins)
                V.tensor_copy(core.mean_var[:, bass.ds(g * GT, GT), :], mv[:, :, :]).then_inc(done["updated"], 1)

            def body(g, buf):
                if not is_group(g, GROUPS - 1):
                    patches(g + 1, 1 - buf)
                if not is_group(g, 0):
                    update(g - 1)
                if not is_group(g, GROUPS - 2, GROUPS - 1):
                    norm(g + 2, buf)
                    mean_squares(g + 2)

            link = Link(dve, done["setup_step"], at["setup_step"])
            link(V.tensor_scalar(std[:, :], core.mean_var[:, :, 1], LN_EPS, None, ALU.add))
            V.memset(ones_row[:, :], 1.0).then_inc(done["std_in"], 1)
            link(V.memset(all_ones[:, :], 1.0))
            link(V.memset(spread_m[:, :, :], 0.0))
            dve.wait_ge(done["std"], at["std"] + 1)
            link(V.reciprocal(core.rstd[:, :], std[:, :]))
            link(V.tensor_tensor(ms[:, :], core.rstd[:, :], core.rstd[:, :], ALU.mult))
            link(V.tensor_tensor(ms[:, :], ms[:, :], core.mean_var[:, :, 1], ALU.mult))
            V.tensor_scalar(ms[:, :], ms[:, :], RMS_EPS2, None, ALU.add).then_inc(done["std_in"], 1)
            dve.wait_ge(done["std"], at["std"] + 2)
            link(V.reciprocal(ms[:, :], ms[:, :]))
            link(V.tensor_tensor(core.rstd[:, :], core.rstd[:, :], ms[:, :], ALU.mult))
            for s, v in loaded:
                dve.wait_ge(s, v)
            norm(0, 0)
            norm(1, 1)
            link(V.tensor_scalar(w_in[:, :], io["w_in"], io["g_res"], None, ALU.mult))
            dve.wait_ge(core.lens_in, 16)
            link(V.tensor_copy(count[:, :], lens[:, :]))
            link(V.tensor_tensor_scan(last[:, :], ones_row[:, :], count[:, :], 0.0, ALU.mult, ALU.add))
            link(V.tensor_scalar(last[:, :], last[:, :], -1.0, None, ALU.add))
            link(V.tensor_scalar(wrap[:, :], last[:, :], 0.0, float(S), ALU.is_lt, ALU.mult))
            link(V.tensor_tensor(last[:, :], last[:, :], wrap[:, :], ALU.add))
            link(V.tensor_tensor(cube[:, :, :], last[:, :].unsqueeze(1).broadcast_to([B, S, S]),
                                 io["token"].unsqueeze(2).broadcast_to([B, S, S]), ALU.is_equal))
            link(V.tensor_reduce(wrap[:, :], cube[:, :, :], AX, ALU.max))
            link(V.tensor_tensor_scan(count[:, :], ones_row[:, :], wrap[:, :], 0.0, ALU.mult, ALU.add))
            link(V.tensor_scalar(plug[:, :], count[:, :], -1.0, 0.0, ALU.add, ALU.max))
            link(V.tensor_scalar(plug[:, :], plug[:, :], float(S - 1), None, ALU.min))
            V.tensor_tensor(cube[:, :, :], plug[:, :].unsqueeze(1).broadcast_to([B, B, S]),
                            core.ident[0:B, 0:B].unsqueeze(2).broadcast_to([B, B, S]), ALU.mult)\
                .then_inc(done["plugged"], 1)
            flat = cube[:, :, :].rearrange("p b s -> p (b s)")
            for n in range(8):
                dve.wait_ge(done["spread"], at["spread"] + n + 1)
                V.tensor_scalar(flat[:, n * 512:(n + 1) * 512], m_ps[0:S, n % 2, :], io["number"], None, ALU.is_equal)\
                    .then_inc(done["compared"], 1)
            for n in range(8):
                dve.wait_ge(done["m_made"], at["m_made"] + n + 1)
                got = m_ps[:, n % 2, :].rearrange("p (t b s) -> p t b s", b=2, s=S)
                for b in range(2):
                    rows = slice(b * S, (b + 1) * S)
                    ins = V.tensor_copy(spread_m[rows, n * GT:(n + 1) * GT, b * S:(b + 1) * S], got[rows, :, b, :])
                ins.then_inc(done["m_out"], 1)
            mean_squares(0)
            patches(0, 0)
            mean_squares(1)
            in_pairs(dve, body)
            update(GROUPS - 1)

    core.ctx_loads += GROUPS // 2
    if out is not None:
        store_x(core, out)


DEPOOL_SIGNALS = {
    "PE": ("x_turned", "mixed", "y_turned", "spread", "m_made"),
    "ACT": ("xt_ready", "y_out", "square_step", "std"),
    "Pool": ("pool_setup", "scale_c"),
    "DVE": ("normed", "patches", "msq", "updated", "update_step", "std_in", "setup_step", "plugged", "compared",
            "m_out"),
}


H3 = 16
HD3 = D // H3
KEYS3 = 2 * S
BANK_HEADS = 512 // KEYS3
BANKS3 = H3 // BANK_HEADS


def l3_attention(core, io, loaded, out=None):
    nc = core.nc
    done, at = core.attention_signals.done, core.attention_signals.at()
    scale = float(HD3) ** -0.5

    with ExitStack() as local:
        def sb(name, shape, dt=F32):
            return local.enter_context(nc.sbuf_tensor("l3a_" + name, shape, dt))

        def pb(name, shape):
            return local.enter_context(nc.psum_tensor("l3a_" + name, shape, F32))

        k_all = sb("k_all", [P, SLOTS, 2, 2, S])
        ctx_v = sb("ctx_v", [S, SLOTS, 2, D])
        v_all = sb("v_all", [P, SLOTS, 2, H3, HD3 + 1])
        xn = sb("xn", [P, SLOTS, D])
        xt = sb("xt", [P, P])
        qt = sb("qt", [P, P])
        q_head = sb("q_head", [P, 2, H3, S])
        s_sb = sb("s_sb", [P, H3, KEYS3])
        probs = sb("probs", [P, H3, KEYS3])
        top = sb("top", [P, H3])
        pt = sb("pt", [P, H3, P])
        inv = sb("inv", [P, H3])
        o_sb = sb("o_sb", [P, H3, HD3])
        ot = sb("ot", [P, P])
        ones = sb("ones", [1, P])
        std = sb("std", [P, TILES])
        stats = sb("stats", [P, 6])
        mv = sb("mv", [P, 2])
        act_ps = pb("act_ps", [P, 2, 512])
        s_ps = pb("s_ps", [P, BANKS3, BANK_HEADS, KEYS3])
        qkv_ps = pb("qkv_ps", [P, 4, P])
        o_ps = pb("o_ps", [P, 512])
        o_view = o_ps[:, 0:H3 * (HD3 + 1)].rearrange("p (h d) -> p h d", d=HD3 + 1)
        y_ps = qkv_ps[:, 0, :]
        loads_before = core.slot_loads

        def heads_of(p):
            return slice(p * BANK_HEADS, (p + 1) * BANK_HEADS)

        def context_loads(quad):
            return (2 * quad + loads_before + 2) * 16

        block = local.enter_context(nc.Block())

        @block.sync
        def _(sp):
            tokens = core.dram["ctx_tok"].rearrange("(j b s) f -> s j b f", b=2, s=S)

            def step(j, slot, quad):
                sp.wait_ge(done["pv_done"], at["pv_done"] + j - 3)
                sp.sem_inc(core.passed, 1)
                keys = core.dram["ctx_t"][:, bass.ds(j, 1), 0, :].rearrange("p j (b s) -> p (j b) s", b=2)
                sp.dma_start(k_all[:, slot, :, 0, :], keys).then_inc(core.slot_in[slot], 16)
                sp.dma_start(ctx_v[:, slot, :, :], tokens[:, bass.ds(j, 1), :, D:2 * D]
                             .rearrange("s j b f -> s (j b) f")).then_inc(core.slot_in[slot], 16)
                if slot % 2 == 0 and not is_tile(j, *range(SLOTS)):
                    split_load(core, sp, 7, (quad - 1) * 2 + slot // 2, slot // 2)

            over_slots(sp, step)
            for b in range(2):
                split_load(core, sp, 7, SPLIT_SLICES - 2 + b, b)

        @block.tensor
        def _(pe):
            mmul = nc.tensor.matmul

            def project(i):
                pe.wait_ge(done["xt_ready"], at["xt_ready"] + i + 1)
                pe.wait_ge(done["k_ready"], at["k_ready"] + i)
                pe.wait_ge(done["updated"], at["updated"] + i - 3)
                for part in range(2):
                    mmul(qkv_ps[:, part, :], io["w_qkv"][:, part * D:(part + 1) * D], xt[:, :], start=True, stop=True)
                for b in range(2):
                    mm = mmul(qkv_ps[S:P, 2 + b, :], xt[:, b * S:(b + 1) * S], io["w_qkv"][:, 2 * D:3 * D],
                              start=True, stop=True)
                mm.then_inc(done["projected"], 1)

            def turn_x(i, slot):
                pe.wait_ge(done["normed"], at["normed"] + i + 1)
                pe.wait_ge(done["xt_ready"], at["xt_ready"] + i)
                if not is_tile(i, 0, 1, 2):
                    pe.wait_ge(done["pt_ready"], at["pt_ready"] + BANKS3 * (i - 3))
                nc.tensor.transpose(act_ps[:, 1, 0:P], xn[:, slot, :], core.ident[:, :])\
                    .then_inc(done["x_turned"], 1)

            def scores(i, slot, quad, p):
                if p == 0:
                    pe.wait_ge(done["q_ready"], at["q_ready"] + i + 1)
                    pe.wait_ge(core.slot_in[slot], context_loads(quad))
                pe.wait_ge(done["shifted"], at["shifted"] + BANKS3 * (i - 1) + p + 1)
                for h in range(BANK_HEADS):
                    for b in range(2):
                        mm = mmul(s_ps[b * S:(b + 1) * S, p, h, :], q_head[:, b, p * BANK_HEADS + h, :],
                                  k_all[:, slot, b, :, :], start=True, stop=True)
                mm.then_inc(done["scored"], 1)

            def turn_p(j, p):
                pe.wait_ge(done["exped"], at["exped"] + BANKS3 * j + p + 1)
                if p == 0:
                    pe.wait_ge(done["ot_ready"], at["ot_ready"] + j)
                elif p == 1:
                    pe.wait_ge(done["xt_ready"], at["xt_ready"] + up_to_last(j + 3) + 1)
                else:
                    pe.wait_ge(done["pt_ready"], at["pt_ready"] + BANKS3 * j + p - 1)
                for h in range(BANK_HEADS):
                    mm = nc.tensor.transpose(act_ps[:, p % 2, h * P:(h + 1) * P],
                                             probs[:, p * BANK_HEADS + h, :], core.ident[:, :])
                mm.then_inc(done["p_turned"], 1)

            def turn_o(i):
                pe.wait_ge(done["o_ready"], at["o_ready"] + i + 1)
                pe.wait_ge(done["pt_ready"], at["pt_ready"] + BANKS3 * i + BANKS3 - 1)
                nc.tensor.transpose(act_ps[:, 0, 0:P], o_sb[:, :, :], core.ident[:, :]).then_inc(done["o_turned"], 1)

            def weigh_v(j, slot):
                pe.wait_ge(done["v_ready"], at["v_ready"] + j + 1)
                pe.wait_ge(done["o_ready"], at["o_ready"] + j)
                for p in range(BANKS3):
                    pe.wait_ge(done["pt_ready"], at["pt_ready"] + BANKS3 * j + p + 1)
                    for h in range(p * BANK_HEADS, (p + 1) * BANK_HEADS):
                        for b in range(2):
                            mm = mmul(o_ps[b * S:(b + 1) * S, h * (HD3 + 1):(h + 1) * (HD3 + 1)],
                                      pt[:, h, b * S:(b + 1) * S], v_all[:, slot, b, h, :], start=True, stop=True)
                mm.then_inc(done["pv_done"], 1)

            def final(i):
                pe.wait_ge(done["ot_ready"], at["ot_ready"] + i + 1)
                pe.wait_ge(done["k_ready"], at["k_ready"] + up_to_last(i + 3) + 1)
                mmul(y_ps, ot[:, :], io["w_proj"], start=True, stop=False)
                mmul(y_ps, ones[:, :], io["b_proj"], start=False, stop=True).then_inc(done["final"], 1)

            def step(j, slot, quad):
                if not is_tile(j, TILES - 2, TILES - 1):
                    project(j + 2)
                if not is_tile(j, TILES - 3, TILES - 2, TILES - 1):
                    turn_x(j + 3, (slot + 3) % SLOTS)
                if not is_tile(j, 0):
                    turn_o(j - 1)
                for p in range(BANKS3):
                    if not is_tile(j, TILES - 1):
                        scores(j + 1, (slot + 1) % SLOTS, quad + (slot + 1) // SLOTS, p)
                    turn_p(j, p)
                if not is_tile(j, 0):
                    final(j - 1)
                weigh_v(j, slot)

            for s, v in loaded:
                pe.wait_ge(s, v)
            pe.wait_ge(done["cleared"], at["cleared"] + 1)
            turn_x(0, 0)
            project(0)
            turn_x(1, 1)
            project(1)
            turn_x(2, 2)
            for p in range(BANKS3):
                scores(0, 0, 0, p)
            over_slots(pe, step)
            turn_o(TILES - 1)
            final(TILES - 1)

        @block.scalar
        def _(act_eng):
            A = nc.scalar

            def xt_out(i):
                act_eng.wait_ge(done["x_turned"], at["x_turned"] + i + 1)
                act_eng.wait_ge(done["projected"], at["projected"] + i)
                A.activation(xt[:, :], act_ps[:, 1, 0:P], ACT.Copy).then_inc(done["xt_ready"], 1)

            def pt_out(j):
                act_eng.wait_ge(done["pv_done"], at["pv_done"] + j)
                for p in range(BANKS3):
                    act_eng.wait_ge(done["p_turned"], at["p_turned"] + BANKS3 * j + p + 1)
                    A.activation(pt[:, heads_of(p), :], act_ps[:, p % 2, :], ACT.Copy).then_inc(done["pt_ready"], 1)

            def ot_out(i):
                act_eng.wait_ge(done["o_turned"], at["o_turned"] + i + 1)
                act_eng.wait_ge(done["final"], at["final"] + i)
                A.activation(ot[:, :], act_ps[:, 0, 0:P], ACT.Copy).then_inc(done["ot_ready"], 1)

            def exps(i):
                for p in range(BANKS3):
                    act_eng.wait_ge(done["shifted"], at["shifted"] + BANKS3 * i + p + 1)
                    act_eng.wait_ge(done["p_turned"], at["p_turned"] + BANKS3 * (i - 1) + p + 1)
                    A.activation(probs[:, heads_of(p), :], s_sb[:, heads_of(p), :], ACT.Exp, scale=scale)\
                        .then_inc(done["exped"], 1)

            def step(j, slot, quad):
                if not is_tile(j, TILES - 3, TILES - 2, TILES - 1):
                    xt_out(j + 3)
                if not is_tile(j, 0):
                    ot_out(j - 1)
                pt_out(j)
                if not is_tile(j, TILES - 1):
                    exps(j + 1)
                if slot % 2 == 1 and not is_tile(j, -1):
                    split_high(core, act_eng, 7, quad * 2 + slot // 2, slot // 2, quad)

            new_rstd(core, std, act_eng=act_eng)
            for i in range(3):
                xt_out(i)
            exps(0)
            over_slots(act_eng, step)
            ot_out(TILES - 1)

        @block.gpsimd
        def _(pool):
            G = nc.gpsimd

            def q_and_v(i, slot, quad):
                pool.wait_ge(done["pv_done"], at["pv_done"] + i - 3)
                pool.wait_ge(core.slot_in[slot], context_loads(quad))
                pool.sem_inc(core.passed, 1)
                G.tensor_copy(v_all[0:S, slot, :, :, 0:HD3],
                              ctx_v[:, slot, :, :].rearrange("p b (h d) -> p b h d", d=HD3))\
                    .then_inc(done["v_ready"], 1)
                pool.wait_ge(done["k_ready"], at["k_ready"] + i + 1)
                pool.wait_ge(done["scored"], at["scored"] + BANKS3 * i)
                for b in range(2):
                    ins = G.tensor_tensor(q_head[:, b, :, :],
                                          qt[:, b * S:(b + 1) * S].unsqueeze(1).broadcast_to([P, H3, S]),
                                          io["heads"].unsqueeze(2).broadcast_to([P, H3, S]), ALU.mult)
                ins.then_inc(done["q_ready"], 1)

            def step(j, slot, quad):
                if not is_tile(j, TILES - 2, TILES - 1):
                    q_and_v(j + 2, (slot + 2) % SLOTS, quad + (slot + 2) // SLOTS)
                if slot % 2 == 1:
                    split_low(core, pool, 7, quad * 2 + slot // 2, slot // 2)

            for s, v in loaded:
                pool.wait_ge(s, v)
            pool.wait_ge(done["cleared"], at["cleared"] + 2)
            q_and_v(0, 0, 0)
            q_and_v(1, 1, 0)
            over_slots(pool, step)

        @block.vector
        def _(dve):
            V = nc.vector

            def norm(i, slot):
                dve.wait_ge(done["x_turned"], at["x_turned"] + i - 3)
                V.tensor_scalar(xn[:, slot, :], core.x[:, bass.ds(i, 1), :], core.mean_var[:, bass.ds(i, 1), 0],
                                core.rstd[:, bass.ds(i, 1)], ALU.subtract, ALU.mult).then_inc(done["normed"], 1)

            def qkv_out(i, slot):
                dve.wait_ge(done["projected"], at["projected"] + i + 1)
                dve.wait_ge(done["q_ready"], at["q_ready"] + i)
                dve.wait_ge(done["pv_done"], at["pv_done"] + i - 3)
                V.tensor_copy(qt[:, :], qkv_ps[:, 0, :])
                V.tensor_copy(k_all[:, slot, :, 1, :], qkv_ps[:, 1, :].rearrange("p (b s) -> p b s", b=2))
                V.tensor_copy(v_all[S:P, slot, :, :, 0:HD3],
                              qkv_ps[S:P, 2:4, :].rearrange("p b (h d) -> p b h d", d=HD3))\
                    .then_inc(done["k_ready"], 1)

            def soften(i):
                link = Link(dve, done["soft_step"], at["soft_step"] + BANKS3 * i)
                for p in range(BANKS3):
                    dve.wait_ge(done["scored"], at["scored"] + BANKS3 * i + p + 1)
                    dve.wait_ge(done["exped"], at["exped"] + BANKS3 * (i - 1) + p + 1)
                    link(V.tensor_reduce(top[:, heads_of(p)], s_ps[:, p, :, :], AX, ALU.max))
                    V.tensor_tensor(s_sb[:, heads_of(p), :], s_ps[:, p, :, :],
                                    top[:, heads_of(p)].unsqueeze(2).broadcast_to([P, BANK_HEADS, KEYS3]),
                                    ALU.subtract).then_inc(done["shifted"], 1)

            def scale_o(j):
                dve.wait_ge(done["pv_done"], at["pv_done"] + j + 1)
                dve.wait_ge(done["o_turned"], at["o_turned"] + j)
                link = Link(dve, done["o_step"], at["o_step"] + j)
                link(V.reciprocal(inv[:, :], o_view[:, :, HD3]))
                V.tensor_tensor(o_sb[:, :, :], o_view[:, :, 0:HD3],
                                inv[:, :].unsqueeze(2).broadcast_to([P, H3, HD3]), ALU.mult)\
                    .then_inc(done["o_ready"], 1)

            def update(i):
                dve.wait_ge(done["final"], at["final"] + i + 1)
                add_to_x(core, dve, Link(dve, done["add_step"], at["add_step"] + i * ADD_STEPS), i, y_ps, stats, mv)

            def step(j, slot, quad):
                if not is_tile(j, TILES - 2, TILES - 1):
                    qkv_out(j + 2, (slot + 2) % SLOTS)
                if not is_tile(j, TILES - 1):
                    soften(j + 1)
                if not is_tile(j, TILES - 4, TILES - 3, TILES - 2, TILES - 1):
                    norm(j + 4, slot)
                if not is_tile(j, 0):
                    update(j - 1)
                scale_o(j)

            V.memset(ones[:, :], 1.0).then_inc(done["cleared"], 1)
            V.memset(v_all[:, :, :, :, :], 1.0).then_inc(done["cleared"], 1)
            dve.wait_ge(done["cleared"], at["cleared"] + 2)
            new_rstd(core, std, dve=dve)
            for s, v in loaded:
                dve.wait_ge(s, v)
            for i in range(SLOTS):
                norm(i, i)
            qkv_out(0, 0)
            qkv_out(1, 1)
            soften(0)
            over_slots(dve, step)
            update(TILES - 1)

    core.slot_loads += 2 * TILES // SLOTS
    if out is not None:
        store_x(core, out)


L0_FFN = Experts("l0f", 32, 4, ACT.Gelu, top=1, b1=True, b2=True, br=True)
L1_FFN = Experts("l1f", 14, 1, ACT.Silu, top=2, gated=True, times=SHORT)
L1_FFN.shared = True
L2_FFN = Experts("l2f", 16, 2, ACT.Silu, top=2, gated=True, br=True, times=GATED)
L3_FFN = Experts("l3f", 16, 2, ACT.Relu, top=1, b1=True, b2=True, br=True, times_prob=True,
                 times=MIDDLE)


SPLIT_SLICES = 16
MOST_WORDS = 2 * L0_FFN.chunks * P

PART_ROWS = (0, 32)
SHARED_ROW = 96


SPLIT_SIGNALS = {"ACT": ("high",), "Pool": ("low",)}


def opening(core, src, loads):
    nc = core.nc
    kinds = (core.expert_signals, core.attention_signals, core.depool_signals, core.split_signals)
    with ExitStack() as local:
        stats = local.enter_context(nc.sbuf_tensor("open_stats", [P, GT, 6], F32))
        mv = local.enter_context(nc.sbuf_tensor("open_mv", [P, GT, 2], F32))
        block = local.enter_context(nc.Block())

        @block.sync
        def _(sp):
            for g in range(GROUPS):
                sp.dma_start(core.x[:, g * GT:(g + 1) * GT, :],
                             src[g * GN:(g + 1) * GN, :].rearrange("(t p) d -> p t d", p=P))\
                    .then_inc(core.x_in[g], 16)
            for dst, dram, sem in loads:
                sp.dma_start(dst, dram).then_inc(sem, 16)

        @block.tensor
        def _(pe):
            for kind in kinds:
                for semaphore in kind.semaphores.get("PE", ()):
                    pe.sem_inc(semaphore, HEADROOM)

        @block.scalar
        def _(act_eng):
            for kind in kinds:
                for semaphore in kind.semaphores.get("ACT", ()):
                    act_eng.sem_inc(semaphore, HEADROOM)

        @block.gpsimd
        def _(pool):
            for kind in kinds:
                for semaphore in kind.semaphores.get("Pool", ()):
                    pool.sem_inc(semaphore, HEADROOM)

        @block.vector
        def _(dve):
            V = nc.vector
            for kind in kinds:
                for semaphore in kind.semaphores.get("DVE", ()):
                    dve.sem_inc(semaphore, HEADROOM)
            link = Link(dve, core.statistics_step, 0)
            for g in range(GROUPS):
                dve.wait_ge(core.x_in[g], 16)
                for t in range(GT):
                    ins = V.bn_stats(stats[:, t, :], core.x[:, g * GT + t, :])
                link(ins)
                for t in range(GT):
                    ins = V.bn_aggr(mv[:, t, :], stats[:, t, :])
                link(ins)
                link(V.tensor_copy(core.mean_var[:, g * GT:(g + 1) * GT, :], mv[:, :, :]))


def program(nc, dram, out, phases="01234567"):
    with ExitStack() as ctx:
        core = Core(nc, ctx)
        core.expert_signals = Signals(nc, ctx, "experts", EXPERT_SIGNALS)
        core.attention_signals = Signals(nc, ctx, "attention", ATTENTION_SIGNALS)
        core.depool_signals = Signals(nc, ctx, "depool", DEPOOL_SIGNALS)
        core.split_signals = Signals(nc, ctx, "split", SPLIT_SIGNALS)
        core.statistics_step = ctx.enter_context(nc.semaphore("statistics_step"))
        core.dram = dram
        core.ctx_in = [ctx.enter_context(nc.semaphore(f"ctx_in_{b}")) for b in range(2)]
        core.slot_in = [ctx.enter_context(nc.semaphore(f"slot_in_{slot}")) for slot in range(SLOTS)]
        core.slot_loads = 0
        core.v_in = [ctx.enter_context(nc.semaphore(f"v_in_{b}")) for b in range(2)]
        core.lens_in = ctx.enter_context(nc.semaphore("lens_in"))
        core.masks_in = ctx.enter_context(nc.semaphore("masks_in"))
        core.x_in = [ctx.enter_context(nc.semaphore(f"x_in_{g}")) for g in range(GROUPS)]
        core.picks_in = ctx.enter_context(nc.semaphore("picks_in"))
        core.passed = ctx.enter_context(nc.semaphore("passed"))
        core.out_done = ctx.enter_context(nc.semaphore("out_done"))
        loads, io = [], {}
        core.later_loads = []

        core.weights_high = core.sb("weights_high", [P, MOST_WORDS], F32R)
        core.weights_low = core.sb("weights_low", [P, MOST_WORDS], F32R)
        core.slices = core.sb("weight_slices", [P, 2, MOST_WORDS // SPLIT_SLICES])
        core.slice_in = [ctx.enter_context(nc.semaphore(f"slice_in_{b}")) for b in range(2)]
        core.slices_before = 0
        core.splits = {}

        def load(phase, *names):
            if str(phase) not in phases:
                return
            sem = ctx.enter_context(nc.semaphore(f"loaded_{phase}"))
            for name in names:
                a = dram[name]
                held = core.sb("s_" + name, list(a.shape), a.dtype)[:]
                (loads if phase == 0 or "0" not in phases else core.later_loads).append((held, a[:], sem))
                io[name] = held
            return (sem, 16 * len(names))

        def parts_of_weights(phase, cfg):
            names = ("w_in", "w_up", "w_out") if cfg.gated else ("w_in", "w_out")
            words = cfg.chunks * P
            core.splits[phase] = (dram[cfg.tag + "_weights"], len(names) * words // SPLIT_SLICES)
            held = {}
            for part, both in (("_hi", core.weights_high), ("_lo", core.weights_low)):
                for i, name in enumerate(names):
                    view = both[:, i * words:(i + 1) * words]
                    held[name + part] = view.rearrange("p (c d) -> p c d", d=D) if name == "w_out" else view
            return held

        sem0 = ctx.enter_context(nc.semaphore("loaded_consts"))
        for t, name in ((core.ident, "ident"),):
            loads.append((t[:], dram[name][:], sem0))
        falling = core.sb("s_falling", [P, GT, NE])
        loads.append((falling[:], dram["falling"][:], sem0))
        picks = {name: core.sb("s_" + name, list(dram[name].shape), F32R) for name in ("pick", "l1f_pick")}
        pick, io["l1f_pick"] = picks["pick"], picks["l1f_pick"][:]
        consts = (sem0, 32)

        def tensors(phase, tag, names):
            got = load(phase, *[tag + "_" + n for n in names])
            if got is None:
                return
            held = {n: io[tag + "_" + n] for n in names}
            if phase in plan:
                held.update(parts_of_weights(phase, plan[phase][0]))
            if tag + "_pick" in io:
                held["pick"] = io[tag + "_pick"]
            return got, {"pick": pick[:], **held, "falling": falling[:]}

        plan = {
            1: (L0_FFN, ("w_router", "b_in", "b_out", "b_router")),
            3: (L1_FFN, ("w_router",)),
            5: (L2_FFN, ("w_router", "b_router")),
            7: (L3_FFN, ("w_router", "b_in", "b_out", "b_router")),
        }
        attention = {
            2: (l1_attention, "l1a", ("w_q", "w_k", "w_v", "w_o", "null_k", "null_v", "null_v_row", "ln_scale",
                                      "ln_bias")),
            4: (l2_depool, "l2d", ("w_in", "b_in", "g_res", "g_init", "token", "number", "decay")),
            6: (l3_attention, "l3a", ("w_qkv", "w_proj", "b_proj", "heads")),
            0: (l0_attention, "l0a", ("w_q", "w_k", "w_v", "w_o", "b_q", "b_k", "b_v", "b_o", "heads")),
        }
        tagged = {**{p: (cfg.tag, names) for p, (cfg, names) in plan.items()},
                  **{p: (tag, names) for p, (_, tag, names) in attention.items()}}
        ready = {p: tensors(p, *tagged[p]) for p in sorted(tagged)}
        core.picks = [(picks[name], dram[name]) for name in picks]
        opening(core, dram["x"], loads)
        last = phases[-1]
        for p in sorted(int(c) for c in phases):
            got, held = ready[p]
            to = out if str(p) == last else None
            if p in plan:
                experts_phase(core, plan[p][0], held, [consts, got], to)
            else:
                attention[p][0](core, held, [consts, got], to)
                core.split_signals.phase_ends({}, SPLIT_SLICES)
                core.slices_before += SPLIT_SLICES // 2


def laid_out(inputs):
    import numpy as np

    a = {k: np.asarray(v) for k, v in inputs.items()}
    c = np.ascontiguousarray
    out = {"x": c(a["x"].reshape(B * S, D)), "ident": np.eye(P, dtype=np.float32)}

    def everywhere(v):
        return c(np.broadcast_to(v, (P, GT, NE)))

    out["falling"] = everywhere(np.arange(NE, 0, -1, dtype=np.float32))

    ctx = a["ctx_2048"].reshape(TILES, P, 2, P)
    out["ctx_t"] = c(ctx.transpose(3, 0, 2, 1))
    out["mask"] = c(a["mask_BxS2_fk1"])

    def halves(w):
        return c(w.reshape(-1, P, w.shape[1]).transpose(1, 0, 2))

    def column(v):
        return c(v.reshape(-1, 1))

    w_src = a["L0_xattn_W_src"].T
    out["l0a_w_q"] = c(a["L0_xattn_W_tgt"].T)
    out["l0a_w_k"] = halves(w_src[:, :D])
    out["l0a_w_v"] = halves(w_src[:, D:])
    out["l0a_w_o"] = halves(a["L0_xattn_W_out"].T)
    out["l0a_b_q"] = column(a["L0_xattn_b_tgt"])
    out["l0a_b_k"] = column(a["L0_xattn_b_src"][:D])
    out["l0a_b_v"] = column(a["L0_xattn_b_src"][D:])
    out["l0a_b_o"] = c(a["L0_xattn_b_out"].reshape(1, D))
    out["l0a_heads"] = np.repeat(np.eye(H0, dtype=np.float32), HD0, axis=0)

    w_kv = a["L1_xattn_Wkv"]
    w_v = w_kv[:, H1 * HD1:].reshape(CTX, PAIRS1, 2, HD1).transpose(0, 2, 1, 3).reshape(CTX, -1)
    out["l1a_w_q"] = c(a["L1_xattn_Wq"])
    out["l1a_w_k"] = halves(w_kv[:, :H1 * HD1])
    out["l1a_w_v"] = halves(w_v)
    out["l1a_w_o"] = halves(a["L1_xattn_Wout"])
    null = a["L1_xattn_null_kv"]
    out["l1a_null_k"] = column(np.concatenate([null[0], null[0]]))
    out["l1a_null_v"] = column(np.concatenate([null[1], null[1]]))
    out["l1a_null_v_row"] = c(np.broadcast_to(null[1], (P, HD1)))
    out["l1a_ln_scale"] = c(np.broadcast_to(a["L1_xattn_ln_scale"], (P, D)))
    out["l1a_ln_bias"] = c(np.broadcast_to(a["L1_xattn_ln_bias"], (P, D)))

    out["ctx_tok"] = c(a["ctx_2048"].reshape(B * S, CTX))
    out["lens"] = c(a["mask_BxS2_if0"].astype(np.int32, copy=False))
    out["l2d_w_in"] = c(a["L2_xattn_W_in"].T)
    out["l2d_b_in"] = column(a["L2_xattn_b_in"])
    out["l2d_g_res"] = column(a["L2_xattn_g_res"])
    out["l2d_g_init"] = c(np.broadcast_to(a["L2_xattn_g_init"][:D], (P, D)))
    out["l2d_token"] = c(np.broadcast_to(np.arange(S, dtype=np.float32), (B, S)))
    out["l2d_number"] = column(np.arange(S, dtype=np.float32))
    step = np.arange(S)[:, None] - np.arange(S)[None, :]
    decay = np.where(step >= 0, np.exp(LOG_P) * (-np.expm1(LOG_P)) ** np.maximum(step, 0), 0.0)
    out["l2d_decay"] = c(np.concatenate([decay, decay], 1).astype(np.float32))

    out["l3a_w_qkv"] = c(a["L3_xattn_w_qkv"].T)
    out["l3a_w_proj"] = c(a["L3_xattn_w_proj"].T)
    out["l3a_b_proj"] = c(a["L3_xattn_b_proj"].reshape(1, D))
    out["l3a_heads"] = np.repeat(np.eye(H3, dtype=np.float32), HD3, axis=0)

    def rows(w):
        return c(w.reshape(-1, P, D).transpose(1, 0, 2))

    def side_by_side(*weights):
        return c(np.concatenate([w.reshape(P, -1) for w in weights], 1))

    def pick(cfg, width):
        m = np.zeros((P, cfg.spreads, P), np.float32)
        for s in range(cfg.spreads):
            for i in range(P):
                unit = s * P * cfg.per + (i if cfg.per == 1 else 0)
                if unit < width * NE:
                    for r in PART_ROWS:
                        m[r + unit // width, s, i] = 1
                else:
                    m[SHARED_ROW, s, i] = 1
        return m

    def flat(w):
        return w.transpose(1, 0, 2).reshape(D, -1)

    out["l0f_weights"] = side_by_side(flat(a["L0_ffn_w1"]), rows(a["L0_ffn_w2"]))
    out["l0f_w_router"] = c(a["L0_ffn_w_router"])
    out["pick"] = pick(L0_FFN, 512)
    out["l0f_b_in"] = c(a["L0_ffn_b1"].reshape(-1, P).T)
    out["l0f_b_out"] = c(a["L0_ffn_b2"])
    out["l0f_b_router"] = everywhere(a["L0_ffn_b_router"])

    units = L1_FFN.chunks * P

    def padded(w, axis):
        pad = [(0, 0), (0, 0)]
        pad[axis] = (0, units - w.shape[axis])
        return c(np.pad(w, pad))

    w_in = padded(np.concatenate([flat(a["L1_ffn_W1"]), a["L1_ffn_Ws1"]], 1), 1)
    w_up = padded(np.concatenate([flat(a["L1_ffn_W2"]), a["L1_ffn_Ws2"]], 1), 1)
    w_out = rows(padded(np.concatenate([a["L1_ffn_W3"].reshape(-1, D), a["L1_ffn_Ws3"]], 0), 0))
    out["l1f_weights"] = side_by_side(w_in, w_up, w_out)
    out["l1f_w_router"] = c(a["L1_ffn_Wg"])
    out["l1f_pick"] = pick(L1_FFN, 176)

    out["l2f_weights"] = side_by_side(flat(a["L2_ffn_gate_w"]), flat(a["L2_ffn_up_w"]), rows(a["L2_ffn_down_w"]))
    out["l2f_w_router"] = c(a["L2_ffn_router_w"].T)
    out["l2f_b_router"] = everywhere(a["L2_ffn_router_b"])

    out["l3f_weights"] = side_by_side(flat(a["L3_ffn_W1"]), rows(a["L3_ffn_W2"]))
    out["l3f_w_router"] = c(a["L3_ffn_Wr"])
    out["l3f_b_in"] = c(a["L3_ffn_b1"].reshape(-1, P).T)
    out["l3f_b_out"] = c(a["L3_ffn_b2"])
    out["l3f_b_router"] = everywhere(a["L3_ffn_br"])
    return out


def kernel(**inputs):
    import numpy as _np
    import concourse.bacc as _bacc
    from concourse import mybir as _mybir
    from concourse.bass_utils import run_bass_kernel_spmd as _run

    nc = _bacc.Bacc("TRN2", target_bir_lowering=False, num_devices=1)
    arrays = laid_out(inputs)
    dram = {n: nc.dram_tensor("in_" + n, a.shape, _mybir.dt.from_np(a.dtype), kind="ExternalInput").ap()
            for n, a in arrays.items()}
    out = nc.dram_tensor("out", (B * S, D), _mybir.dt.float32, kind="ExternalOutput").ap()
    program(nc, dram, out)
    r = _run(nc, [{"in_" + n: a for n, a in arrays.items()}], core_ids=[0])
    return r.results[0]["out"].reshape(B, S, D)
```
